# Optimizing a Trainium2 kernel written in Bass

```python
import numpy as np
import jax
import jax.numpy as jnp

def _softmax(x, axis=-1):
    return jax.nn.softmax(x, axis=axis)

def _gelu(x):
    return jax.nn.gelu(x, approximate=True)

def _silu(x):
    return jax.nn.silu(x)

def _sigmoid(x):
    return jax.nn.sigmoid(x)

def _layernorm(x, axis=-1, eps=1e-05):
    m = jnp.mean(x, axis=axis, keepdims=True)
    v = jnp.var(x, axis=axis, keepdims=True)
    return (x - m) / jnp.sqrt(v + eps)

def _scatter_add(tgt, idx, src, axis=0):
    return tgt.at[idx].add(src)

def _segment_sum(src, seg, n):
    return jax.ops.segment_sum(src, seg, n)
kernel_name = 'mk_prb_d2_jaxref_r8_c6744f'

def setup_inputs(seed: int=0):
    np.random.seed(seed)
    _w = jnp.asarray

    def _L0_attn_setup():
        import jax, jax.numpy as jnp
        from jax import lax
        import numpy as np
        B, S, D, H = (4, 256, 128, 16)
        HD = D // H
        EPS = 1e-08
        LN_EPS = 1e-05
        key = jax.random.key(seed)
        ks = jax.random.split(key, 8)
        sc = 1.0 / np.sqrt(D)
        return {'x': jax.random.normal(ks[0], (B, S, D), jnp.float32), 'time_mix_r': jnp.full((1, 1, D), 0.5, jnp.float32), 'time_mix_k': jnp.full((1, 1, D), 0.5, jnp.float32), 'time_mix_v': jnp.full((1, 1, D), 0.5, jnp.float32), 'W_r': jax.random.normal(ks[1], (D, D), jnp.float32) * sc, 'W_k': jax.random.normal(ks[2], (D, D), jnp.float32) * sc, 'W_v': jax.random.normal(ks[3], (D, D), jnp.float32) * sc, 'W_o': jax.random.normal(ks[4], (D, D), jnp.float32) * sc, 'time_decay': jax.random.normal(ks[5], (H, HD), jnp.float32) * 0.1 - 5.0, 'time_first': jax.random.normal(ks[6], (H, HD), jnp.float32) * 0.1, 'ln_gamma': jnp.ones((D,), jnp.float32), 'ln_beta': jnp.zeros((D,), jnp.float32)}
    _L0_attn_in = _L0_attn_setup()

    def _L0_ffn_setup():
        import jax, jax.numpy as jnp
        import numpy as np
        TOP_K = 2

        def _moe(x, Wr, br, W1, b1, W2, b2):
            B, S, D = x.shape
            E = Wr.shape[1]
            xt = x.reshape(-1, D)
            logits = xt @ Wr + br
            top_vals, top_idx = jax.lax.top_k(logits, TOP_K)
            mask = jnp.zeros_like(logits, dtype=bool).at[jnp.arange(xt.shape[0])[:, None], top_idx].set(True)
            sparse_logits = jnp.where(mask, logits, -jnp.inf)
            gate = jax.nn.softmax(sparse_logits, axis=-1)
            h = jax.nn.relu(jnp.einsum('td,edh->teh', xt, W1) + b1)
            y = jnp.einsum('teh,ehd->ted', h, W2) + b2
            out = jnp.einsum('ted,te->td', y, gate)
            return out.reshape(B, S, D)
        key = jax.random.key(seed)
        ks = jax.random.split(key, 5)
        B, S, D, E, H = (2, 256, 128, 8, 512)
        scale = 1.0 / np.sqrt(D)
        return {'x': jax.random.normal(ks[0], (B, S, D), dtype=jnp.float32), 'Wr': jax.random.normal(ks[1], (D, E), dtype=jnp.float32) * scale, 'br': jnp.zeros((E,), dtype=jnp.float32), 'W1': jax.random.normal(ks[2], (E, D, H), dtype=jnp.float32) * scale, 'b1': jnp.zeros((E, H), dtype=jnp.float32), 'W2': jax.random.normal(ks[3], (E, H, D), dtype=jnp.float32) * (1.0 / np.sqrt(H)), 'b2': jnp.zeros((E, D), dtype=jnp.float32)}
    _L0_ffn_in = _L0_ffn_setup()

    def _L1_attn_setup():
        import jax, jax.numpy as jnp
        import numpy as np
        DIM = 128
        D_INNER = 128
        N_STATE = 32
        N_BLOCKS = 4
        TOP_K = 2
        ROUTER_TEMP = 1.0
        INIT_BETA_BIAS = 2.0
        BATCH = 16
        T = 256

        def _xavier(key, shape):
            fan_out, fan_in = shape
            lim = jnp.sqrt(6.0 / (fan_in + fan_out))
            return jax.random.uniform(key, shape, jnp.float32, -lim, lim)

        def _cell_scan(x_rnn, W_router, W_kv, W_beta, b_beta, W_q):
            Tt, batch, D = x_rnn.shape
            n, nb = (N_STATE, N_BLOCKS)
            xf = x_rnn.reshape(Tt * batch, D)
            logits = (xf @ W_router.T).reshape(Tt, batch, nb) / ROUTER_TEMP
            kv = (xf @ W_kv.T).reshape(Tt, batch, nb, 2, n)
            beta = jax.nn.sigmoid((xf @ W_beta.T).reshape(Tt, batch, nb, n) + b_beta)
            q = (xf @ W_q.T).reshape(Tt, batch, n)
            S0 = jnp.zeros((batch, nb, n, n), x_rnn.dtype)
            rows = jnp.arange(batch)[:, None]

            def step(S, inp):
                logits_t, k_t, v_t, beta_t, q_t = inp
                _, idx = jax.lax.top_k(logits_t, TOP_K)
                mask = jnp.zeros_like(logits_t).at[rows, idx].set(1.0)
                sm = jax.nn.softmax(logits_t, axis=-1)
                uw = mask * sm
                uw = uw / (uw.sum(-1, keepdims=True) + 1e-08)
                kn = k_t / (jnp.linalg.norm(k_t, axis=-1, keepdims=True) + 1e-06)
                retrieved = jnp.einsum('bnij,bnj->bni', S, kn)
                delta = v_t - retrieved
                outer = delta[..., :, None] * kn[..., None, :]
                S_upd = jnp.tanh(beta_t[..., None] * S + outer)
                w = uw[..., None, None]
                S_new = (1.0 - w) * S + w * S_upd
                Sq = jnp.einsum('bnij,bj->bni', S_new, q_t)
                block_out = Sq * (Sq * jax.nn.sigmoid(Sq))
                out_t = jnp.einsum('bn,bnd->bd', sm, block_out)
                return (S_new, out_t)
            S_final, outs = jax.lax.scan(step, S0, (logits, kv[..., 0, :], kv[..., 1, :], beta, q))
            return (outs, S_final)

        def _reference_tuple_inner(x, W_in, W_router, W_kv, W_beta, b_beta, W_q, W_out):
            x_proj = jax.nn.silu(x @ W_in.T)
            x_rnn = jnp.transpose(x_proj, (1, 0, 2))
            cell_out, S_final = _cell_scan(x_rnn, W_router, W_kv, W_beta, b_beta, W_q)
            y = jnp.transpose(cell_out, (1, 0, 2)) @ W_out.T
            return (y, S_final)
        key = jax.random.key(seed)
        ks = jax.random.split(key, 7)
        x = jax.random.normal(ks[0], (BATCH, T, DIM), jnp.float32)
        W_in = _xavier(ks[1], (D_INNER, DIM))
        W_router = _xavier(ks[2], (N_BLOCKS, D_INNER))
        W_kv = _xavier(ks[3], (N_BLOCKS * 2 * N_STATE, D_INNER))
        W_beta = _xavier(ks[4], (N_BLOCKS * N_STATE, D_INNER))
        b_beta = jnp.full((N_BLOCKS, N_STATE), INIT_BETA_BIAS, jnp.float32)
        W_q = _xavier(ks[5], (N_STATE, D_INNER))
        W_out = _xavier(ks[6], (DIM, N_STATE))
        return {'x': x, 'W_in': W_in, 'W_router': W_router, 'W_kv': W_kv, 'W_beta': W_beta, 'b_beta': b_beta, 'W_q': W_q, 'W_out': W_out}
    _L1_attn_in = _L1_attn_setup()

    def _L1_ffn_setup():
        import jax, jax.numpy as jnp
        import numpy as np
        B, T, C, H, E, K, F = (2, 256, 128, 16, 8, 2, 256)
        EPS = 1e-05

        def layernorm(x, w):
            m = x.mean(-1, keepdims=True)
            v = x.var(-1, keepdims=True)
            return (x - m) * jax.lax.rsqrt(v + EPS) * w

        def attention(x, c_attn_w, c_proj_w):
            b, t, c = x.shape
            hd = c // H
            q, k, v = jnp.split(x @ c_attn_w, 3, axis=-1)
            q = q.reshape(b, t, H, hd).transpose(0, 2, 1, 3)
            k = k.reshape(b, t, H, hd).transpose(0, 2, 1, 3)
            v = v.reshape(b, t, H, hd).transpose(0, 2, 1, 3)
            att = jnp.einsum('bhqd,bhkd->bhqk', q, k) / jnp.sqrt(jnp.asarray(hd, x.dtype))
            causal = jnp.tril(jnp.ones((t, t), bool))
            att = jnp.where(causal, att, jnp.asarray(-jnp.inf, att.dtype))
            att = jax.nn.softmax(att, axis=-1)
            y = jnp.einsum('bhqk,bhkd->bhqd', att, v)
            y = y.transpose(0, 2, 1, 3).reshape(b, t, c)
            return y @ c_proj_w

        def moe_mlp(x, router_w, w1, w2):
            b, t, c = x.shape
            xf = x.reshape(-1, c)
            router_logits = xf @ router_w
            probs = jax.nn.softmax(router_logits.astype(jnp.float32), axis=-1)
            rw, sel = jax.lax.top_k(probs, K)
            rw = rw / rw.sum(axis=-1, keepdims=True)
            rw = rw.astype(x.dtype)
            w1e = w1.reshape(c, E, F).transpose(1, 0, 2)
            w2e = w2.reshape(E, F, c)
            h = jax.nn.gelu(jnp.einsum('nc,ecf->enf', xf, w1e), approximate=False)
            y_all = jnp.einsum('enf,efc->nec', h, w2e)
            y_sel = jnp.take_along_axis(y_all, sel[:, :, None], axis=1)
            y = (y_sel * rw[:, :, None]).sum(axis=1)
            return y.reshape(b, t, c)
        key = jax.random.key(seed)
        ks = jax.random.split(key, 6)
        s = 0.02
        return {'x': jax.random.normal(ks[0], (B, T, C), jnp.float32), 'ln1_w': jnp.ones((C,), jnp.float32), 'c_attn_w': jax.random.normal(ks[1], (C, 3 * C), jnp.float32) * s, 'c_proj_w': jax.random.normal(ks[2], (C, C), jnp.float32) * s, 'ln2_w': jnp.ones((C,), jnp.float32), 'router_w': jax.random.normal(ks[3], (C, E), jnp.float32) * s, 'w1': jnp.clip(jax.random.normal(ks[4], (C, E * F), jnp.float32) * s, -0.06, 0.06), 'w2': jnp.clip(jax.random.normal(ks[5], (E * F, C), jnp.float32) * s, -0.06, 0.06)}
    _L1_ffn_in = _L1_ffn_setup()
    _d = {'L0_attn_x': _L0_attn_in['x'], 'L0_attn_time_mix_r': _L0_attn_in['time_mix_r'], 'L0_attn_time_mix_k': _L0_attn_in['time_mix_k'], 'L0_attn_time_mix_v': _L0_attn_in['time_mix_v'], 'L0_attn_W_r': _L0_attn_in['W_r'], 'L0_attn_W_k': _L0_attn_in['W_k'], 'L0_attn_W_v': _L0_attn_in['W_v'], 'L0_attn_W_o': _L0_attn_in['W_o'], 'L0_attn_time_decay': _L0_attn_in['time_decay'], 'L0_attn_time_first': _L0_attn_in['time_first'], 'L0_attn_ln_gamma': _L0_attn_in['ln_gamma'], 'L0_attn_ln_beta': _L0_attn_in['ln_beta'], 'L0_ffn_Wr': _L0_ffn_in['Wr'], 'L0_ffn_br': _L0_ffn_in['br'], 'L0_ffn_W1': _L0_ffn_in['W1'], 'L0_ffn_b1': _L0_ffn_in['b1'], 'L0_ffn_W2': _L0_ffn_in['W2'], 'L0_ffn_b2': _L0_ffn_in['b2'], 'L1_attn_W_in': _L1_attn_in['W_in'], 'L1_attn_W_router': _L1_attn_in['W_router'], 'L1_attn_W_kv': _L1_attn_in['W_kv'], 'L1_attn_W_beta': _L1_attn_in['W_beta'], 'L1_attn_b_beta': _L1_attn_in['b_beta'], 'L1_attn_W_q': _L1_attn_in['W_q'], 'L1_attn_W_out': _L1_attn_in['W_out'], 'L1_ffn_ln1_w': _L1_ffn_in['ln1_w'], 'L1_ffn_c_attn_w': _L1_ffn_in['c_attn_w'], 'L1_ffn_c_proj_w': _L1_ffn_in['c_proj_w'], 'L1_ffn_ln2_w': _L1_ffn_in['ln2_w'], 'L1_ffn_router_w': _L1_ffn_in['router_w'], 'L1_ffn_w1': _L1_ffn_in['w1'], 'L1_ffn_w2': _L1_ffn_in['w2']}
    _x0 = _d['L0_attn_x']
    _d['L0_attn_x'] = jax.random.normal(jax.random.fold_in(jax.random.key(seed), 1), (32, 256, 128), dtype=_x0.dtype)
    del _x0
    return _d

def reference(L0_attn_x, L0_attn_time_mix_r, L0_attn_time_mix_k, L0_attn_time_mix_v, L0_attn_W_r, L0_attn_W_k, L0_attn_W_v, L0_attn_W_o, L0_attn_time_decay, L0_attn_time_first, L0_attn_ln_gamma, L0_attn_ln_beta, L0_ffn_Wr, L0_ffn_br, L0_ffn_W1, L0_ffn_b1, L0_ffn_W2, L0_ffn_b2, L1_attn_W_in, L1_attn_W_router, L1_attn_W_kv, L1_attn_W_beta, L1_attn_b_beta, L1_attn_W_q, L1_attn_W_out, L1_ffn_ln1_w, L1_ffn_c_attn_w, L1_ffn_c_proj_w, L1_ffn_ln2_w, L1_ffn_router_w, L1_ffn_w1, L1_ffn_w2):

    def _L0_attn_ref(x, time_mix_r, time_mix_k, time_mix_v, W_r, W_k, W_v, W_o, time_decay, time_first, ln_gamma, ln_beta):
        import jax, jax.numpy as jnp
        from jax import lax
        import numpy as np
        B, S, D, H = (4, 256, 128, 16)
        HD = D // H
        EPS = 1e-08
        LN_EPS = 1e-05
        b, s, d = x.shape
        h, hd = time_decay.shape
        shifted = jnp.pad(x[:, :-1, :], ((0, 0), (1, 0), (0, 0)))
        xr = x * time_mix_r + shifted * (1.0 - time_mix_r)
        xk = x * time_mix_k + shifted * (1.0 - time_mix_k)
        xv = x * time_mix_v + shifted * (1.0 - time_mix_v)
        r = (xr @ W_r.T).reshape(b, s, h, hd)
        k = (xk @ W_k.T).reshape(b, s, h, hd)
        v = (xv @ W_v.T).reshape(b, s, h, hd)
        w = -jnp.exp(time_decay)
        u = time_first

        def step(carry, kv):
            a, bst = carry
            kt, vt = kv
            wk = kt + u
            p = jnp.maximum(bst, wk)
            e1 = jnp.exp(bst - p)
            e2 = jnp.exp(wk - p)
            out = (e1 * a + e2 * vt) / (e1 + e2 + EPS)
            ww = bst + w
            p2 = jnp.maximum(ww, kt)
            e1b = jnp.exp(ww - p2)
            e2b = jnp.exp(kt - p2)
            a_new = e1b * a + e2b * vt
            b_new = p2 + jnp.log(e1b + e2b + EPS)
            return ((a_new, b_new), out)
        a0 = jnp.zeros((b, h, hd), x.dtype)
        b0 = jnp.full((b, h, hd), -1e+38, x.dtype)
        kT = jnp.moveaxis(k, 1, 0)
        vT = jnp.moveaxis(v, 1, 0)
        _, outs = lax.scan(step, (a0, b0), (kT, vT))
        wkv = jnp.moveaxis(outs, 0, 1)
        rwkv = jax.nn.sigmoid(r) * wkv
        mean = jnp.mean(rwkv, axis=(1, 3), keepdims=True)
        var = jnp.var(rwkv, axis=(1, 3), keepdims=True)
        normed = (rwkv - mean) * lax.rsqrt(var + LN_EPS)
        normed = normed * ln_gamma.reshape(1, 1, h, hd) + ln_beta.reshape(1, 1, h, hd)
        return normed.reshape(b, s, d) @ W_o.T

    def _L0_ffn_ref(x, Wr, br, W1, b1, W2, b2):
        import jax, jax.numpy as jnp
        import numpy as np
        TOP_K = 2

        def _moe(x, Wr, br, W1, b1, W2, b2):
            B, S, D = x.shape
            E = Wr.shape[1]
            xt = x.reshape(-1, D)
            logits = xt @ Wr + br
            top_vals, top_idx = jax.lax.top_k(logits, TOP_K)
            mask = jnp.zeros_like(logits, dtype=bool).at[jnp.arange(xt.shape[0])[:, None], top_idx].set(True)
            sparse_logits = jnp.where(mask, logits, -jnp.inf)
            gate = jax.nn.softmax(sparse_logits, axis=-1)
            h = jax.nn.relu(jnp.einsum('td,edh->teh', xt, W1) + b1)
            y = jnp.einsum('teh,ehd->ted', h, W2) + b2
            out = jnp.einsum('ted,te->td', y, gate)
            return out.reshape(B, S, D)
        return _moe(x, Wr, br, W1, b1, W2, b2)

    def _L1_attn_ref(x, W_in, W_router, W_kv, W_beta, b_beta, W_q, W_out):
        import jax, jax.numpy as jnp
        import numpy as np
        DIM = 128
        D_INNER = 128
        N_STATE = 32
        N_BLOCKS = 4
        TOP_K = 2
        ROUTER_TEMP = 1.0
        INIT_BETA_BIAS = 2.0
        BATCH = 16
        T = 256

        def _xavier(key, shape):
            fan_out, fan_in = shape
            lim = jnp.sqrt(6.0 / (fan_in + fan_out))
            return jax.random.uniform(key, shape, jnp.float32, -lim, lim)

        def _cell_scan(x_rnn, W_router, W_kv, W_beta, b_beta, W_q):
            Tt, batch, D = x_rnn.shape
            n, nb = (N_STATE, N_BLOCKS)
            xf = x_rnn.reshape(Tt * batch, D)
            logits = (xf @ W_router.T).reshape(Tt, batch, nb) / ROUTER_TEMP
            kv = (xf @ W_kv.T).reshape(Tt, batch, nb, 2, n)
            beta = jax.nn.sigmoid((xf @ W_beta.T).reshape(Tt, batch, nb, n) + b_beta)
            q = (xf @ W_q.T).reshape(Tt, batch, n)
            S0 = jnp.zeros((batch, nb, n, n), x_rnn.dtype)
            rows = jnp.arange(batch)[:, None]

            def step(S, inp):
                logits_t, k_t, v_t, beta_t, q_t = inp
                _, idx = jax.lax.top_k(logits_t, TOP_K)
                mask = jnp.zeros_like(logits_t).at[rows, idx].set(1.0)
                sm = jax.nn.softmax(logits_t, axis=-1)
                uw = mask * sm
                uw = uw / (uw.sum(-1, keepdims=True) + 1e-08)
                kn = k_t / (jnp.linalg.norm(k_t, axis=-1, keepdims=True) + 1e-06)
                retrieved = jnp.einsum('bnij,bnj->bni', S, kn)
                delta = v_t - retrieved
                outer = delta[..., :, None] * kn[..., None, :]
                S_upd = jnp.tanh(beta_t[..., None] * S + outer)
                w = uw[..., None, None]
                S_new = (1.0 - w) * S + w * S_upd
                Sq = jnp.einsum('bnij,bj->bni', S_new, q_t)
                block_out = Sq * (Sq * jax.nn.sigmoid(Sq))
                out_t = jnp.einsum('bn,bnd->bd', sm, block_out)
                return (S_new, out_t)
            S_final, outs = jax.lax.scan(step, S0, (logits, kv[..., 0, :], kv[..., 1, :], beta, q))
            return (outs, S_final)

        def _reference_tuple_inner(x, W_in, W_router, W_kv, W_beta, b_beta, W_q, W_out):
            x_proj = jax.nn.silu(x @ W_in.T)
            x_rnn = jnp.transpose(x_proj, (1, 0, 2))
            cell_out, S_final = _cell_scan(x_rnn, W_router, W_kv, W_beta, b_beta, W_q)
            y = jnp.transpose(cell_out, (1, 0, 2)) @ W_out.T
            return (y, S_final)
        return _reference_tuple_inner(x, W_in, W_router, W_kv, W_beta, b_beta, W_q, W_out)[0]

    def _L1_ffn_ref(x, ln1_w, c_attn_w, c_proj_w, ln2_w, router_w, w1, w2):
        import jax, jax.numpy as jnp
        import numpy as np
        B, T, C, H, E, K, F = (2, 256, 128, 16, 8, 2, 256)
        EPS = 1e-05

        def layernorm(x, w):
            m = x.mean(-1, keepdims=True)
            v = x.var(-1, keepdims=True)
            return (x - m) * jax.lax.rsqrt(v + EPS) * w

        def attention(x, c_attn_w, c_proj_w):
            b, t, c = x.shape
            hd = c // H
            q, k, v = jnp.split(x @ c_attn_w, 3, axis=-1)
            q = q.reshape(b, t, H, hd).transpose(0, 2, 1, 3)
            k = k.reshape(b, t, H, hd).transpose(0, 2, 1, 3)
            v = v.reshape(b, t, H, hd).transpose(0, 2, 1, 3)
            att = jnp.einsum('bhqd,bhkd->bhqk', q, k) / jnp.sqrt(jnp.asarray(hd, x.dtype))
            causal = jnp.tril(jnp.ones((t, t), bool))
            att = jnp.where(causal, att, jnp.asarray(-jnp.inf, att.dtype))
            att = jax.nn.softmax(att, axis=-1)
            y = jnp.einsum('bhqk,bhkd->bhqd', att, v)
            y = y.transpose(0, 2, 1, 3).reshape(b, t, c)
            return y @ c_proj_w

        def moe_mlp(x, router_w, w1, w2):
            b, t, c = x.shape
            xf = x.reshape(-1, c)
            router_logits = xf @ router_w
            probs = jax.nn.softmax(router_logits.astype(jnp.float32), axis=-1)
            rw, sel = jax.lax.top_k(probs, K)
            rw = rw / rw.sum(axis=-1, keepdims=True)
            rw = rw.astype(x.dtype)
            w1e = w1.reshape(c, E, F).transpose(1, 0, 2)
            w2e = w2.reshape(E, F, c)
            h = jax.nn.gelu(jnp.einsum('nc,ecf->enf', xf, w1e), approximate=False)
            y_all = jnp.einsum('enf,efc->nec', h, w2e)
            y_sel = jnp.take_along_axis(y_all, sel[:, :, None], axis=1)
            y = (y_sel * rw[:, :, None]).sum(axis=1)
            return y.reshape(b, t, c)
        x = x + attention(layernorm(x, ln1_w), c_attn_w, c_proj_w)
        x = x + moe_mlp(layernorm(x, ln2_w), router_w, w1, w2)
        return x
    x = L0_attn_x
    xn = _layernorm(x, axis=-1)
    x = x + _L0_attn_ref(xn, L0_attn_time_mix_r, L0_attn_time_mix_k, L0_attn_time_mix_v, L0_attn_W_r, L0_attn_W_k, L0_attn_W_v, L0_attn_W_o, L0_attn_time_decay, L0_attn_time_first, L0_attn_ln_gamma, L0_attn_ln_beta) + _L0_ffn_ref(xn, L0_ffn_Wr, L0_ffn_br, L0_ffn_W1, L0_ffn_b1, L0_ffn_W2, L0_ffn_b2)
    xn = _layernorm(x, axis=-1)
    x = x + _L1_attn_ref(xn, L1_attn_W_in, L1_attn_W_router, L1_attn_W_kv, L1_attn_W_beta, L1_attn_b_beta, L1_attn_W_q, L1_attn_W_out) + _L1_ffn_ref(xn, L1_ffn_ln1_w, L1_ffn_c_attn_w, L1_ffn_c_proj_w, L1_ffn_ln2_w, L1_ffn_router_w, L1_ffn_w1, L1_ffn_w2)
    return x

_drawn_inputs = setup_inputs


def setup_inputs(seed=0):
    import zlib

    import numpy as np

    out = dict(_drawn_inputs(seed))
    spreads = {'L0_attn_time_mix_r': (0.5, 0.2),
     'L0_attn_time_mix_k': (0.5, 0.2),
     'L0_attn_time_mix_v': (0.5, 0.2),
     'L0_attn_ln_gamma': (1.0, 0.2),
     'L0_attn_ln_beta': (0.0, 0.1),
     'L0_ffn_br': (0.0, 0.1),
     'L0_ffn_b1': (0.0, 0.1),
     'L0_ffn_b2': (0.0, 0.1),
     'L1_attn_b_beta': (2.0, 0.6),
     'L1_ffn_ln1_w': (1.0, 0.6),
     'L1_ffn_ln2_w': (1.0, 0.6)}
    factors = {'L0_attn_time_decay': 8.0,
     'L0_attn_time_first': 8.0,
     'L1_attn_W_beta': 5.585,
     'L1_ffn_c_attn_w': 4.227,
     'L1_ffn_c_proj_w': 4.2,
     'L1_ffn_router_w': 6.175,
     'L1_ffn_w1': 5.349,
     'L1_ffn_w2': 5.26}
    for name, (base, spread) in spreads.items():
        noise = np.random.default_rng([zlib.crc32(name.encode()), seed]).standard_normal(out[name].shape)
        drawn = base * np.exp(spread * noise) if base else spread * noise
        out[name] = jnp.asarray(drawn.astype(out[name].dtype))
    for name, factor in factors.items():
        out[name] = (out[name] * factor).astype(out[name].dtype)
    return out
```

```python
import concourse.bass as bass
from concourse import mybir
from contextlib import ExitStack

B, T, D = 32, 256, 128
P = 128
UB = 2
UNITS = B // UB
TILES = UB * T // P
TOK = UB * T
E = 8
H0C, H1C = 4, 2
NH, HD = 16, 8
NB, NS = 4, 32
STEPS = T // UNITS
CELL = 4 * NS + NB
LN_EPS, WKV_EPS = 1e-5, 1e-8
LOW = -1e38

F32 = mybir.dt.float32
BF16 = mybir.dt.bfloat16
ALU = mybir.AluOpType
ACT = mybir.ActivationFunctionType
AX = mybir.AxisListType.X

MIX_R, MIX_K, MIX_V, DECAY, FIRST, GAMMA, BETA, LN1_W, LN2_W = range(9)
C_ID = 0
C_GROUP = C_ID + P
C_SEL = C_GROUP + P
C_MASK = C_SEL + NS
C_HOT = C_MASK + 4
C_LT8 = C_HOT + NB
C_LT4 = C_LT8 + E * E
C_BR = C_LT4 + NB * NB
C_BB = C_BR + E
C_B1 = C_BB + NS
C_NHALF = C_B1 + E * H0C
C_HALF = C_NHALF + TILES
C_EPS = C_HALF + STEPS
C_END = C_EPS + 1


PER_CELL = 185
CELL_SEMS = (
    "scaled", "p_proj", "p_copied", "p_b", "p_bt", "p_ss", "p_norm", "p_lc", "p_le", "prep_done",
    "z_ready", "th_done", "w_ready", "sq_ready", "sq_t", "bo_ready", "co_ready", "co_copied",
    "f_var", "f_rstd", "f_xn", "f_tr", "f_xa", "f_q", "f_k", "f_v", "f_qm", "f_kt", "f_vt",
    "f_s", "f_m", "f_e", "f_t", "f_pc", "f_pv", "f_y", "f_yt", "f_yc", "f_pj", "f_x2",
    "h_var", "h_rstd", "h_xn", "h_tr", "h_xm", "h_lg", "h_c", "h_ex", "h_gate",
    "m_hp", "m_h", "m_y", "m_acc", "o_y", "o_x")


class Chain:

    def __init__(self, eng, sem, base=0):
        self.eng, self.sem, self.base, self.n = eng, sem, base, 0

    def done(self, ins):
        ins.then_inc(self.sem, 1)
        self.n += 1

    def settle(self):
        self.eng.wait_ge(self.sem, self.base + self.n)

    def then(self, ins):
        self.done(ins)
        self.settle()


def build(nc, A, out):
    ctx = ExitStack()
    with ctx:
        def sb(name, shape, dt=F32):
            return ctx.enter_context(nc.sbuf_tensor(name, shape, dt))

        def sem(name):
            return ctx.enter_context(nc.semaphore(name))

        X = sb("X", [P, B * T // P, D])
        FT = sb("FT", [P, B * (T + 1)])
        XT = FT[:, :].rearrange("p (b t) -> p b t", b=B)
        XP = FT[:, 0:B * T].rearrange("p (b t) -> p b t", b=B)
        RX = sb("RX", [P, B * T])
        RW = RX[:, :].rearrange("p (b t) -> p b t", b=B)
        XN = RX[:, :].rearrange("p (n d) -> p n d", d=D)
        W1 = sb("W1", [P, E * H0C * P])
        W2 = sb("W2", [P, E * H0C, D])
        WA = sb("WA", [P, 4, D])
        WM = sb("WM", [P, 2, 3, D])
        WR0 = sb("WR0", [P, E])
        B2 = sb("B2", [E, D])
        VEC = sb("VEC", [P, 9])
        CST = sb("CST", [P, C_END])
        NEG = sb("NEG", [P, 3 * P], BF16)
        WIN = sb("WIN", [P, D])
        WC = sb("WC", [P, NB, CELL])
        WOUT = sb("WOUT", [NS, D])
        WQKV = sb("WQKV", [P, 3 * D])
        WPR = sb("WPR", [P, D])
        WR1 = sb("WR1", [P, E])
        HT = sb("HT", [P, 2, H0C * TOK])
        SC = sb("SC", [P, 6 * NS * NS])
        BNS = sb("BNS", [P, TILES, 6])
        MV = sb("MV", [P, TILES, 2])
        VE = sb("VE", [P, TILES])
        RSTD = sb("RSTD", [P, TILES])
        XNT = sb("XNT", [P, TILES, D])
        LG = sb("LG", [P, TILES, E])
        MX = sb("MX", [P, TILES])
        LC = sb("LC", [P, TILES, E])
        EX = sb("EX", [P, TILES, E])
        CMP = sb("CMP", [P, 2, TILES * E * E])
        RK = sb("RK", [P, TILES, E])
        GATE = sb("GATE", [P, TILES, E])
        GS = sb("GS", [P, TILES])
        TB = sb("TB", [P, TOK])
        GT = TB[0:E, :]

        ident = CST[:, C_ID:C_ID + P]

        def vec(c):
            return VEC[:, c:c + 1]

        PB = [ctx.enter_context(nc.psum_tensor(f"PB{i}", [P, 512], F32)) for i in range(8)]

        loaded = sem("loaded")
        late_loaded = sem("late_loaded")
        prepared = sem("prepared")
        dve_chain = sem("dve_chain")

        block = ctx.enter_context(nc.Block())

        Dx = SC[:, 0:1024].rearrange("p (k b t) -> p k b t", k=2, b=UB)
        Ex = SC[:, 1024:2048].rearrange("p (k b t) -> p k b t", k=2, b=UB)
        Fx = HT[:, 0, :].rearrange("p (k b t) -> p k b t", k=4, b=UB)
        Gx = HT[:, 1, :].rearrange("p (k b t) -> p k b t", k=4, b=UB)
        Mx = SC[:, 2048:2560]
        Sx = SC[:, 2560:3072]
        Bx = SC[:, 3072:3072 + UB * (T + 1)].rearrange("p (b t) -> p b t", b=UB)
        Ax = SC[:, 3600:3600 + TOK + 1]
        P1 = SC[:, 4120:4632]
        P2 = SC[:, 4632:5144]
        N1 = SC[:, 5144:5656]
        ER = XNT[:, :, :].rearrange("p n d -> p (n d)")
        WD = W1[:, 0:TOK]
        N2 = W1[:, 512:1024]
        L1 = W1[:, 1024:1536]
        XNa = W1[:, 1536:2048].rearrange("p (n d) -> p n d", d=D)
        MVR = W1[:, 2048:2048 + 2 * B].rearrange("p (b k) -> p b k", k=2)
        BNR = W1[:, 2112:2112 + 6 * UB].rearrange("p (b k) -> p b k", k=6)
        MVU = W1[:, 2130:2130 + 2 * UB].rearrange("p (b k) -> p b k", k=2)
        GMS = W1[:, 2200:2200 + 6 * B].rearrange("p (k b) -> p k b", k=6)
        DW = sb("DW", [P, 2])
        NSC = sb("NSC", [P, 2, B])

        XU = SC[:, 0:TOK]
        RN = SC[:, TOK:2 * TOK]

        def two(ap):
            return ap.rearrange("p (b t) -> p b t", b=UB)

        sig = {n: sem(n) for n in (
            "a_var", "a_rstd", "a_xn", "a_tr", "a_xt", "a_r", "a_kv", "a_er", "a_d", "a_e", "a_s", "a_l",
            "a_f", "a_g", "a_done", "g_mean", "g_dev", "g_var", "g_ve", "g_rstd", "weights_used",
            "b_n", "b_xu", "f_cu", "o_st", "b_lg", "b_c", "b_ex", "b_gate", "b_gt", "b_gtc", "b_at", "b_x", "b_hp", "b_h", "b_y", "b_acc",
            "c_var", "c_rstd", "c_xn", "c_tr", "c_xt", "c_in", "c_xp",
            "decay_exp", "stored") + CELL_SEMS}

        n_early = 5

        def prime(eng, signals):
            for signal in signals:
                eng.sem_inc(signal, 1)

        def apart(eng):
            eng.nop(nofuse=True)

        def norm_stats(dve, ch, src, signal):
            apart(dve)
            for i in range(TILES):
                ch.done(nc.vector.bn_stats(BNS[:, i, :], src(i)))
            ch.settle()
            apart(dve)
            for i in range(TILES):
                ch.done(nc.vector.bn_aggr(MV[:, i, :], BNS[:, i, :]))
            ch.settle()
            nc.vector.tensor_scalar(VE[:, :], MV[:, :, 1], LN_EPS, None, ALU.add).then_inc(signal, 1)

        def norm_apply(dst, src, signal):
            for i in range(TILES):
                last = nc.vector.tensor_scalar(dst(i), src(i), MV[:, i, 0:1], RSTD[:, i:i + 1],
                                               ALU.subtract, ALU.mult)
            last.then_inc(signal, 1)

        def rstd_pow(out_ap, in_ap, n, signal):
            nc.gpsimd.tensor_tensor(out_ap, in_ap, CST[:, C_NHALF:C_NHALF + n], ALU.pow).then_inc(signal, 1)

        def gate_logits(dve, ch, bias, signal):
            if bias:
                ch.then(nc.vector.tensor_tensor(
                    LG[:, :, :], PB[7][:, 0:TILES * E].rearrange("p (n e) -> p n e", e=E),
                    CST[:, C_BR:C_BR + E].unsqueeze(1).to_broadcast([P, TILES, E]), ALU.add))
            else:
                ch.then(nc.vector.tensor_copy(LG[:, :, :], PB[7][:, 0:TILES * E].rearrange("p (n e) -> p n e", e=E)))
            ch.then(nc.vector.tensor_reduce(MX[:, :], LG[:, :, :], AX, ALU.max))
            nc.vector.tensor_tensor(LC[:, :, :], LG[:, :, :], MX[:, :].unsqueeze(2).to_broadcast([P, TILES, E]),
                                    ALU.subtract).then_inc(signal, 1)

        def top_two_rank(ch, lg, rank, n, e, lt):
            other = lg.unsqueeze(2).to_broadcast([P, n, e, e])
            own = lg.unsqueeze(3).to_broadcast([P, n, e, e])
            gt = CMP[:, 0, 0:n * e * e].rearrange("p (n e f) -> p n e f", n=n, e=e)
            eq = CMP[:, 1, 0:n * e * e].rearrange("p (n e f) -> p n e f", n=n, e=e)
            ch.done(nc.vector.tensor_tensor(gt, other, own, ALU.is_gt))
            ch.then(nc.vector.tensor_tensor(eq, other, own, ALU.is_equal))
            low = CST[:, lt:lt + e * e].unsqueeze(1).to_broadcast([P, n, e * e])
            eqf = CMP[:, 1, 0:n * e * e].rearrange("p (n e) -> p n e", n=n)
            ch.then(nc.vector.tensor_tensor(eqf, eqf, low, ALU.mult))
            ch.then(nc.vector.tensor_tensor(CMP[:, 0, 0:n * e * e], CMP[:, 0, 0:n * e * e],
                                            CMP[:, 1, 0:n * e * e], ALU.add))
            ch.then(nc.vector.tensor_reduce(rank, gt, AX, ALU.add))

        def gate_weights(dve, ch, exp_ready, value, signal):
            top_two_rank(ch, LG[:, :, :], RK[:, :, :], TILES, E, C_LT8)
            dve.wait_ge(exp_ready, value)
            ch.then(nc.vector.scalar_tensor_tensor(GATE[:, :, :], RK[:, :, :], 2.0, EX[:, :, :],
                                                   ALU.is_lt, ALU.mult))
            ch.then(nc.vector.tensor_reduce(GS[:, :], GATE[:, :, :], AX, ALU.add))
            ch.then(nc.vector.reciprocal(GS[:, :], GS[:, :]))
            nc.vector.tensor_tensor(GATE[:, :, :], GATE[:, :, :], GS[:, :].unsqueeze(2).to_broadcast([P, TILES, E]),
                                    ALU.mult).then_inc(signal, 1)


        St = SC[:, 0:1024]
        PRD, ZB, BS, TH, WT = (SC[:, k * 1024:(k + 1) * 1024] for k in range(1, 6))
        CU = PRD[:, 0:STEPS * B].rearrange("p (s b) -> p s b", b=B)
        QM = sb("QM", [P, 4, TOK])
        RAW = sb("RAW", [P, STEPS, CELL])
        KN, VV = (HT[:, 0, 1024 + k * 512:1536 + k * 512].rearrange("p (s j) -> p s j", j=NS) for k in range(2))
        QQ, BT = (HT[:, 1, 1024 + k * 512:1536 + k * 512].rearrange("p (s j) -> p s j", j=NS) for k in range(2))
        PEX = W1[:, 2048:3584].rearrange("p (j k) -> p j k", j=3)
        XA = W1[:, 3584:4096]
        W2f = W2[:, :, :].rearrange("p n d -> p (n d)")
        PTS = W2f[:, 2048:3584].rearrange("p (j k) -> p j k", j=3)
        KT = W2f[:, 3584:4096]
        VT = sb("VT", [P, TILES, D])
        WMf = WM[:, :, :, :].rearrange("p a m d -> p (a m d)")
        SQ = WMf[:, 0:STEPS * NS].rearrange("p (s i) -> p s i", i=NS)
        Y = WMf[:, STEPS * NS:STEPS * NS + 2 * D].rearrange("p (q d) -> p q d", d=D)
        YT = WA[:, 0:2, :].rearrange("p a d -> p (a d)")
        RS = sb("RS", [P, UB, 2, NH])
        RI = sb("RI", [P, 2, NH])
        NM = sb("NM", [P, 3, 4])
        SM16 = sb("SM16", [P, 8, STEPS])
        SM64 = WA[:, 2:4, :].rearrange("p a (k s n) -> p (a k) s n", k=2, n=NB)
        RET = NSC

        def v3(ap):
            return ap.rearrange("p (i j) -> p i j", j=NS)

        def bi(ap):
            return ap.unsqueeze(1).to_broadcast([P, NS, NS])

        def bj(ap):
            return ap.unsqueeze(2).to_broadcast([P, NS, NS])

        def tilef(buf, u, i):
            return buf[:, bass.ds(u * TILES + i, 1), :].rearrange("p n d -> p (n d)")

        def cell_sync(sp):
            outs = out.rearrange("(n p) d -> p n d", p=P)
            with sp.Fori(0, UNITS) as u:
                sp.wait_ge(sig["o_x"], 1 + u + 1)
                sp.dma_start(outs[:, bass.ds(u * TILES, TILES), :], X[:, bass.ds(u * TILES, TILES), :]).then_inc(sig["stored"], 16)
            sp.wait_ge(sig["stored"], 16 * UNITS)

        def cell_pool(pool):
            with pool.Fori(0, UNITS) as u:
                pool.wait_ge(sig["f_var"], u + 1)
                rstd_pow(RSTD[:, :], VE[:, :], TILES, sig["f_rstd"])
                pool.wait_ge(sig["p_ss"], u + 1)
                nc.gpsimd.tensor_tensor(SM16[:, 1, :], SM16[:, 0, :], CST[:, C_HALF:C_HALF + STEPS],
                                        ALU.pow).then_inc(sig["p_norm"], 1)
                pool.wait_ge(sig["h_var"], u + 1)
                rstd_pow(RSTD[:, :], VE[:, :], TILES, sig["h_rstd"])

        def cell_act(act):
            def copy_projections(u):
                for g in range(STEPS // 2):
                    act.wait_ge(sig["p_proj"], u * (STEPS // 2) + g + 1)
                    nc.scalar.activation(RAW[:, 2 * g:2 * g + 2, :],
                                         half(g % 2), ACT.Copy).then_inc(sig["p_copied"], 1)

            act.wait_ge(sig["scaled"], 1)
            act.wait_ge(sig["c_xp"], 1 + UNITS)
            with act.Fori(0, UNITS) as u:
                apart(act)
                nc.scalar.activation(CU, XP[:, :, bass.ds(u * STEPS, STEPS)].rearrange("p b t -> p t b"),
                                     ACT.Copy).then_inc(sig["f_cu"], 1)
                act.wait_ge(sig["prep_done"], 1 + u)
                copy_projections(u)
                act.wait_ge(sig["p_b"], u + 1)
                nc.scalar.activation(TB[:, :], TB[:, :], ACT.Tanh, scale=0.5).then_inc(sig["p_bt"], 1)
                act.wait_ge(sig["p_lc"], u + 1)
                nc.scalar.activation(SM64[:, 1, :, :], SM64[:, 0, :, :], ACT.Exp).then_inc(sig["p_le"], 1)
                for st in range(STEPS):
                    act.wait_ge(sig["z_ready"], u * STEPS + st + 1)
                    nc.scalar.activation(TH, ZB, ACT.Tanh).then_inc(sig["th_done"], 1)
                    act.wait_ge(sig["th_done"], u * STEPS + st + 1)
                    nc.scalar.activation(WT, TH, ACT.Copy, scale=SM16[:, 4, st:st + 1]).then_inc(sig["w_ready"], 1)
                    if st == 0:
                        act.wait_ge(sig["f_tr"], u + 1)
                        nc.scalar.activation(XA, PB[6][:, :], ACT.Copy).then_inc(sig["f_xa"], 1)
                        act.wait_ge(sig["f_q"], u + 1)
                        for h in range(4):
                            last = nc.scalar.activation(QM[:, h, :], PB[0][:, :], ACT.Copy,
                                                        scale=CST[:, C_MASK + h:C_MASK + h + 1])
                        last.then_inc(sig["f_qm"], 1)
                        act.wait_ge(sig["f_k"], u + 1)
                        nc.scalar.activation(KT, PB[1][:, :], ACT.Copy).then_inc(sig["f_kt"], 1)
                        act.wait_ge(sig["f_v"], u + 1)
                        nc.scalar.activation(VT[:, :, :], PB[2][:, :].rearrange("p (n d) -> p n d", d=D),
                                             ACT.Copy).then_inc(sig["f_vt"], 1)
                    if st == 5 or st == 9:
                        act.wait_ge(sig["f_yt"], u * UB + (st - 1) // 4)
                        nc.scalar.activation(YT[:, :], PB[6][:, 0:2 * P], ACT.Copy).then_inc(sig["f_yc"], 1)
                    if 1 <= st <= 8:
                        c = st - 1
                        b, g = c // 4, c % 4
                        for j in range(3):
                            act.wait_ge(sig["f_m"], u * 24 + 3 * c + j + 1)
                            heads = range(4) if j == 0 else (2 * j - 2, 2 * j - 1)
                            w = 512 // len(heads)
                            for n, h in enumerate(heads):
                                last = nc.scalar.activation(PEX[:, j, n * w:(n + 1) * w], PB[j][:, n * w:(n + 1) * w],
                                                            ACT.Exp, bias=NM[:, j, n:n + 1],
                                                            accum_out=RS[:, b, min(j, 1), 4 * g + h:4 * g + h + 1])
                            last.then_inc(sig["f_e"], 1)
                        act.wait_ge(sig["f_pv"], 1 + u * 8 + c)
                        for j in range(3):
                            act.wait_ge(sig["f_t"], u * 24 + 3 * c + j + 1)
                            nc.scalar.activation(PTS[:, j, :], PB[3 + j % 2][:, :], ACT.Copy).then_inc(sig["f_pc"], 1)
                    if st == 11:
                        act.wait_ge(sig["h_tr"], u + 1)
                        nc.scalar.activation(XA, PB[6][:, :], ACT.Copy).then_inc(sig["h_xm"], 1)
                        act.wait_ge(sig["h_c"], u + 1)
                        nc.scalar.activation(EX[:, :, :], LC[:, :, :], ACT.Exp).then_inc(sig["h_ex"], 1)
                    if st >= 12:
                        for e in (2 * (st - 12), 2 * (st - 12) + 1):
                            if e >= 2:
                                act.wait_ge(sig["m_y"], u * E + e - 1)
                            for c in range(H1C):
                                act.wait_ge(sig["m_hp"], u * (E * H1C) + e * H1C + c + 1)
                                nc.scalar.activation(HT[:, e % 2, c * TOK:(c + 1) * TOK], PB[2 * (e % 2) + c][:, :],
                                                     ACT.Gelu).then_inc(sig["m_h"], 1)
                act.wait_ge(sig["sq_ready"], u + 1)
                nc.scalar.activation(TB[:, :], SQ[:, :, :].rearrange("p s i -> p (s i)"), ACT.Tanh,
                                     scale=0.5).then_inc(sig["sq_t"], 1)
                act.wait_ge(sig["co_ready"], 1 + u + 1)
                apart(act)
                nc.scalar.activation(XP[0:NS, :, bass.ds(u * STEPS, STEPS)],
                                     PB[7][0:NS, :].rearrange("i (t b) -> i b t", b=B), ACT.Copy).then_inc(sig["co_copied"], 1)
            act.wait_ge(sig["co_copied"], 1 + UNITS)
            with act.Fori(0, UNITS) as u:
                act.wait_ge(sig["o_y"], 1 + u)
                apart(act)
                nc.scalar.activation(two(SC[0:NS, 0:TOK]), XP[0:NS, bass.ds(u * UB, UB), :], ACT.Copy).then_inc(sig["o_st"], 1)

        def half(g):
            return PB[7 if g == 0 else 5][:, 0:2 * CELL].rearrange("p (s c) -> p s c", c=CELL)

        def cell_pe(pe):
            def scores(u, c):
                b, g = c // 4, c % 4
                q0, q1 = 32 * g, 32 * g + 32
                for j in range(3):
                    if c >= 1:
                        pe.wait_ge(sig["f_e"], u * 24 + 3 * (c - 1) + j + 1)
                    if j == 0:
                        nc.tensor.matmul(PB[0][:, :].rearrange("p (h k) -> p h k", h=4), NEG[:, 0:P],
                                         NEG[:, 2 * P:3 * P].unsqueeze(1).to_broadcast([P, 4, P]), start=True, stop=False)
                        for h in range(4):
                            last = nc.tensor.matmul(PB[0][:, h * P:(h + 1) * P], QM[q0:q1, h, b * T:b * T + P],
                                                    KT[q0:q1, b * T:b * T + P], start=False, stop=(h == 3), tile_position=(q0, 0))
                    else:
                        nc.tensor.matmul(PB[j][:, :].rearrange("p (h k) -> p h k", h=2), NEG[:, 0:P],
                                         NEG[:, P:3 * P].unsqueeze(1).to_broadcast([P, 2, 2 * P]), start=True, stop=False)
                        for n in range(2):
                            h = 2 * j - 2 + n
                            last = nc.tensor.matmul(PB[j][:, n * T:(n + 1) * T], QM[q0:q1, h, b * T + P:b * T + 2 * P],
                                                    KT[q0:q1, b * T:b * T + T], start=False, stop=(n == 1), tile_position=(q0, 0))
                    last.then_inc(sig["f_s"], 1)

            def values(u, c):
                b, g = c // 4, c % 4
                for j in range(3):
                    pe.wait_ge(sig["f_e"], u * 24 + 3 * c + j + 1)
                    if j == 2:
                        pe.wait_ge(sig["f_pc"], 1 + u * 24 + 3 * c + 1)
                    elif c >= 1:
                        pe.wait_ge(sig["f_pc"], 1 + u * 24 + 3 * c)
                    for k in range(4):
                        last = nc.tensor.transpose(PB[3 + j % 2][:, k * P:(k + 1) * P], PEX[:, j, k * P:(k + 1) * P], ident)
                    last.then_inc(sig["f_t"], 1)
                if c % 4 == 0:
                    pe.wait_ge(sig["f_y"], 1 + u * UB + b)
                for h in range(4):
                    o = (4 * g + h) * HD
                    if h == 0:
                        pe.wait_ge(sig["f_pc"], 1 + u * 24 + 3 * c + 3)
                    nc.tensor.matmul(PB[5][:, o:o + HD], PTS[:, 0, h * P:(h + 1) * P], VT[:, 2 * b, o:o + HD],
                                     start=True, stop=True)
                    for kt in range(2):
                        col = (h % 2) * T + kt * P
                        last = nc.tensor.matmul(PB[5][:, P + o:P + o + HD], PTS[:, 1 + h // 2, col:col + P],
                                                VT[:, 2 * b + kt, o:o + HD], start=(kt == 0), stop=(kt == 1))
                last.then_inc(sig["f_pv"], 1)

            def project(u, b):
                pe.wait_ge(sig["f_y"], 1 + u * UB + b + 1)
                if b == 1:
                    pe.wait_ge(sig["f_x2"], 1 + u * UB + 1)
                for qt in range(2):
                    last = nc.tensor.transpose(PB[6][:, qt * P:(qt + 1) * P], Y[:, qt, :], ident)
                last.then_inc(sig["f_yt"], 1)
                pe.wait_ge(sig["f_yc"], u * UB + b + 1)
                for qt in range(2):
                    last = nc.tensor.matmul(PB[6][:, (2 + qt) * P:(3 + qt) * P], YT[:, qt * P:(qt + 1) * P], WPR[:, :],
                                            start=True, stop=True)
                last.then_inc(sig["f_pj"], 1)

            def hidden(u, e):
                for c in range(H1C):
                    k = e * H1C + c
                    if e >= 2:
                        pe.wait_ge(sig["m_h"], u * (E * H1C) + k - 2 * H1C + 1)
                    nc.tensor.matmul(PB[2 * (e % 2) + c][:, :], W1[:, k * P:(k + 1) * P], XA, start=True,
                                     stop=True).then_inc(sig["m_hp"], 1)

            pe.wait_ge(sig["c_xp"], 1 + UNITS)
            pe.wait_ge(late_loaded, 16 * 12)
            pe.wait_ge(sig["scaled"], 1)
            with pe.Fori(0, UNITS) as u:
                pe.wait_ge(sig["co_copied"], 1 + u)
                pe.wait_ge(sig["m_acc"], 1 + u * E)
                pe.wait_ge(sig["f_cu"], u + 1)
                for g in range(STEPS // 2):
                    if g >= 2:
                        pe.wait_ge(sig["p_copied"], u * (STEPS // 2) + g - 1)
                    for k in range(2):
                        for n in range(NB):
                            last = nc.tensor.matmul(half(g % 2)[32 * n:32 * n + 32, k, :],
                                                    CU[:, 2 * g + k, :],
                                                    WC[:, n, :], start=True, stop=True, tile_position=(0, 32 * n))
                    last.then_inc(sig["p_proj"], 1)
                pe.wait_ge(sig["f_xn"], u + 1)
                for i in range(TILES):
                    last = nc.tensor.transpose(PB[6][:, i * P:(i + 1) * P], XNT[:, i, :], ident)
                last.then_inc(sig["f_tr"], 1)
                pe.wait_ge(sig["f_xa"], u + 1)
                nc.tensor.matmul(PB[0][:, :], WQKV[:, 0:D], XA, start=True, stop=True).then_inc(sig["f_q"], 1)
                nc.tensor.matmul(PB[1][:, :], WQKV[:, D:2 * D], XA, start=True, stop=True).then_inc(sig["f_k"], 1)
                for i in range(TILES):
                    last = nc.tensor.matmul(PB[2][:, i * P:(i + 1) * P], XA[:, i * P:(i + 1) * P], WQKV[:, 2 * D:3 * D],
                                            start=True, stop=True)
                last.then_inc(sig["f_v"], 1)
                pe.wait_ge(sig["f_vt"], u + 1)
                scores(u, 0)
                for c in range(8):
                    values(u, c)
                    if c < 7:
                        scores(u, c + 1)
                    if c == 3:
                        project(u, 0)
                project(u, 1)
                pe.wait_ge(sig["h_xn"], u + 1)
                for i in range(TILES):
                    last = nc.tensor.transpose(PB[6][:, i * P:(i + 1) * P], XNT[:, i, :], ident)
                last.then_inc(sig["h_tr"], 1)
                pe.wait_ge(sig["h_xm"], u + 1)
                pe.wait_ge(sig["p_copied"], (u + 1) * (STEPS // 2))
                for i in range(TILES):
                    last = nc.tensor.matmul(PB[7][:, i * E:(i + 1) * E], XA[:, i * P:(i + 1) * P], WR1[:, :],
                                            start=True, stop=True)
                last.then_inc(sig["h_lg"], 1)
                hidden(u, 0)
                for e in range(E):
                    if e + 1 < E:
                        hidden(u, e + 1)
                    pe.wait_ge(sig["m_h"], u * (E * H1C) + (e + 1) * H1C)
                    if e >= 2:
                        pe.wait_ge(sig["m_acc"], 1 + u * E + e - 1)
                    yb = PB[4 + e % 2]
                    for i in range(TILES):
                        for c in range(H1C):
                            last = nc.tensor.matmul(yb[:, i * P:(i + 1) * P],
                                                    HT[:, e % 2, c * TOK + i * P:c * TOK + (i + 1) * P],
                                                    W2[:, e * H1C + c, :], start=(c == 0), stop=(c == H1C - 1))
                    last.then_inc(sig["m_y"], 1)
                pe.wait_ge(sig["bo_ready"], u + 1)
                pe.wait_ge(sig["h_c"], u + 1)
                for t in range(STEPS):
                    last = nc.tensor.matmul(PB[7][0:NS, t * B:(t + 1) * B], TB[:, t * NS:(t + 1) * NS],
                                            CST[:, C_SEL:C_SEL + NS], start=True, stop=True)
                last.then_inc(sig["co_ready"], 1)
            pe.wait_ge(sig["co_copied"], 1 + UNITS)
            with pe.Fori(0, UNITS) as u:
                pe.wait_ge(sig["o_st"], u + 1)
                pe.wait_ge(sig["o_x"], 1 + u)
                for i in range(TILES):
                    last = nc.tensor.matmul(PB[0][:, i * P:(i + 1) * P], SC[0:NS, i * P:(i + 1) * P],
                                            WOUT[:, :], start=True, stop=True)
                last.then_inc(sig["o_y"], 1)

        def cell_dve(dve, start):
            V = nc.vector
            ch = Chain(dve, dve_chain, start)
            dve.wait_ge(late_loaded, 16 * 12)
            for w, c in ((WQKV[:, :], LN1_W), (WR1[:, :], LN2_W), (W1[:, 0:E * H1C * P], LN2_W)):
                ch.done(V.tensor_scalar(w, w, vec(c), None, ALU.mult))
            dve.wait_ge(sig["g_rstd"], 1)
            V.memset(St, 0.0).then_inc(sig["scaled"], 1)
            dve.wait_ge(sig["scaled"], 1)
            start += ch.n

            def prep(u, ch):
                kq = lambda c: RAW[:, :, c * NS:(c + 1) * NS]
                b16 = lambda ap: ap.unsqueeze(2).to_broadcast([P, STEPS, NS])
                b4 = lambda ap: ap.unsqueeze(2).to_broadcast([P, STEPS, NB])
                t3 = TB[:, :].rearrange("p (s j) -> p s j", j=NS)
                dve.wait_ge(sig["p_copied"], (u + 1) * (STEPS // 2))
                dve.wait_ge(sig["co_ready"], 1 + u)
                V.tensor_tensor(t3, kq(2), CST[:, C_BB:C_BB + NS].unsqueeze(1).to_broadcast([P, STEPS, NS]),
                                ALU.add).then_inc(sig["p_b"], 1)
                ch.done(V.tensor_reduce(SM16[:, 2, :], RAW[:, :, 4 * NS:CELL], AX, ALU.max))
                ch.then(V.tensor_tensor(KN, kq(0), kq(0), ALU.mult))
                V.tensor_tensor(SM64[:, 0, :, :], RAW[:, :, 4 * NS:CELL], b4(SM16[:, 2, :]), ALU.subtract).then_inc(sig["p_lc"], 1)
                V.tensor_reduce(SM16[:, 0, :], KN, AX, ALU.add).then_inc(sig["p_ss"], 1)
                ch.done(V.tensor_copy(VV, kq(1)))
                ch.done(V.tensor_copy(QQ, kq(3)))
                ch.then(V.tensor_copy(SM64[:, 2, :, :], RAW[:, :, 4 * NS:CELL]))
                top_two_rank(ch, SM64[:, 2, :, :], SM64[:, 3, :, :], STEPS, NB, C_LT4)
                dve.wait_ge(sig["p_le"], u + 1)
                ch.then(V.tensor_reduce(SM16[:, 2, :], SM64[:, 1, :, :], AX, ALU.add))
                ch.then(V.reciprocal(SM16[:, 2, :], SM16[:, 2, :]))
                ch.then(V.tensor_tensor(SM64[:, 1, :, :], SM64[:, 1, :, :], b4(SM16[:, 2, :]), ALU.mult))
                ch.then(V.scalar_tensor_tensor(SM64[:, 3, :, :], SM64[:, 3, :, :], 2.0, SM64[:, 1, :, :],
                                               ALU.is_lt, ALU.mult))
                ch.then(V.tensor_reduce(SM16[:, 3, :], SM64[:, 3, :, :], AX, ALU.add))
                ch.then(V.tensor_scalar(SM16[:, 3, :], SM16[:, 3, :], 1e-8, None, ALU.add))
                ch.then(V.reciprocal(SM16[:, 3, :], SM16[:, 3, :]))
                ch.then(V.tensor_tensor(SM64[:, 3, :, :], SM64[:, 3, :, :], b4(SM16[:, 3, :]), ALU.mult))
                hot = CST[:, C_HOT:C_HOT + NB].unsqueeze(1).to_broadcast([P, STEPS, NB])
                ch.done(V.tensor_tensor(SM64[:, 3, :, :], SM64[:, 3, :, :], hot, ALU.mult))
                ch.then(V.tensor_tensor(SM64[:, 1, :, :], SM64[:, 1, :, :], hot, ALU.mult))
                ch.done(V.tensor_reduce(SM16[:, 4, :], SM64[:, 3, :, :], AX, ALU.add))
                ch.then(V.tensor_reduce(SM16[:, 5, :], SM64[:, 1, :, :], AX, ALU.add))
                ch.done(V.tensor_scalar(SM16[:, 6, :], SM16[:, 4, :], -1.0, 1.0, ALU.mult, ALU.add))
                ch.done(V.tensor_scalar(SM16[:, 7, :], SM16[:, 5, :], 0.5, None, ALU.mult))
                dve.wait_ge(sig["p_norm"], u + 1)
                ch.then(V.tensor_scalar(SM16[:, 1, :], SM16[:, 1, :], 1e-6, None, ALU.add))
                ch.then(V.reciprocal(SM16[:, 1, :], SM16[:, 1, :]))
                ch.done(V.tensor_tensor(KN, kq(0), b16(SM16[:, 1, :]), ALU.mult))
                dve.wait_ge(sig["p_bt"], u + 1)
                V.tensor_scalar(BT, t3, 0.5, 0.5, ALU.mult, ALU.add).then_inc(sig["prep_done"], 1)
                dve.wait_ge(sig["prep_done"], 1 + u + 1)

            def read_state(ch, st):
                ch.then(V.tensor_tensor(v3(PRD), v3(St), bi(QQ[:, st, :]), ALU.mult))
                return V.tensor_reduce(SQ[:, st, :], v3(PRD), AX, ALU.add)

            def scan_step(u, ch, st):
                ch.then(V.tensor_tensor(v3(PRD), v3(St), bi(KN[:, st, :]), ALU.mult))
                ch.then(V.tensor_reduce(RET[:, 0, :], v3(PRD), AX, ALU.add))
                ch.then(V.tensor_tensor(RET[:, 1, :], VV[:, st, :], RET[:, 0, :], ALU.subtract))
                ch.done(V.tensor_tensor(v3(ZB), bj(RET[:, 1, :]), bi(KN[:, st, :]), ALU.mult))
                ch.then(V.tensor_tensor(v3(BS), v3(St), bj(BT[:, st, :]), ALU.mult))
                V.tensor_tensor(ZB, ZB, BS, ALU.add).then_inc(sig["z_ready"], 1)
                if st >= 1:
                    ch.done(read_state(ch, st - 1))
                dve.wait_ge(sig["w_ready"], u * STEPS + st + 1)
                ch.then(V.scalar_tensor_tensor(St, St, SM16[:, 6, st:st + 1], WT, ALU.mult, ALU.add))

            def maxima(u, c):
                for j in range(3):
                    dve.wait_ge(sig["f_s"], u * 24 + 3 * c + j + 1)
                    n = 4 if j == 0 else 2
                    V.tensor_reduce(NM[:, j, 0:n], PB[j][:, :].rearrange("p (h k) -> p h k", h=n), AX, ALU.max,
                                    negate=True).then_inc(sig["f_m"], 1)

            def attention_out(u, ch, b):
                dve.wait_ge(sig["f_pv"], 1 + u * 8 + 4 * (b + 1))
                ch.then(V.reciprocal(RI[:, :, :], RS[:, b, :, :]))
                V.tensor_tensor(Y[:, :, :].rearrange("p q (h d) -> p (q h) d", d=HD),
                                PB[5][:, 0:2 * P].rearrange("p (q d) -> p q d", d=HD),
                                RI[:, :, :].rearrange("p q h -> p (q h)").unsqueeze(2).to_broadcast([P, 2 * NH, HD]),
                                ALU.mult).then_inc(sig["f_y"], 1)

            def residual(u, b):
                dve.wait_ge(sig["f_pj"], u * UB + b + 1)
                x = XN[:, bass.ds(u * TILES + 2 * b, 2), :]
                V.tensor_tensor(x, x, PB[6][:, 2 * P:4 * P].rearrange("p (n d) -> p n d", d=D), ALU.add).then_inc(sig["f_x2"], 1)

            def add_expert(u, e):
                dve.wait_ge(sig["m_y"], u * E + e + 1)
                if e >= 1:
                    dve.wait_ge(sig["m_acc"], 1 + u * E + e)
                for i in range(TILES):
                    x = tilef(XN, u, i)
                    last = V.scalar_tensor_tensor(x, PB[4 + e % 2][:, i * P:(i + 1) * P], GATE[:, i, e:e + 1], x,
                                                  ALU.mult, ALU.add)
                last.then_inc(sig["m_acc"], 1)

            with dve.Fori(0, UNITS) as u:
                ch = Chain(dve, dve_chain, start + u * PER_CELL)
                norm_stats(dve, ch, lambda i: tilef(XN, u, i), sig["f_var"])
                prep(u, ch)
                dve.wait_ge(sig["f_rstd"], u + 1)
                norm_apply(lambda i: XNT[:, i, :], lambda i: tilef(XN, u, i), sig["f_xn"])
                for st in range(STEPS):
                    scan_step(u, ch, st)
                    if st == 5:
                        attention_out(u, ch, 0)
                    if 1 <= st <= 8:
                        maxima(u, st - 1)
                    if st == 6:
                        residual(u, 0)
                    if st == 9:
                        attention_out(u, ch, 1)
                    if st == 10:
                        residual(u, 1)
                        dve.wait_ge(sig["f_x2"], 1 + u * UB + 2)
                        norm_stats(dve, ch, lambda i: tilef(XN, u, i), sig["h_var"])
                    if st == 11:
                        dve.wait_ge(sig["h_rstd"], u + 1)
                        norm_apply(lambda i: XNT[:, i, :], lambda i: tilef(XN, u, i), sig["h_xn"])
                        dve.wait_ge(sig["h_lg"], u + 1)
                        gate_logits(dve, ch, False, sig["h_c"])
                    if st == 12:
                        gate_weights(dve, ch, sig["h_ex"], u + 1, sig["h_gate"])
                        dve.wait_ge(sig["h_gate"], u + 1)
                    if st >= 13:
                        add_expert(u, 2 * (st - 13))
                        add_expert(u, 2 * (st - 13) + 1)
                read_state(ch, STEPS - 1).then_inc(sig["sq_ready"], 1)
                add_expert(u, 6)
                add_expert(u, 7)
                dve.wait_ge(sig["m_acc"], 1 + u * E + E)
                xs = X[:, bass.ds(u * TILES, TILES), :]
                ch.done(V.tensor_tensor(xs, xs, XN[:, bass.ds(u * TILES, TILES), :], ALU.add))
                sqf = SQ[:, :, :].rearrange("p s i -> p (s i)")
                dve.wait_ge(sig["sq_ready"], u + 1)
                dve.wait_ge(sig["sq_t"], u + 1)
                ch.then(V.scalar_tensor_tensor(TB[:, :], TB[:, :], 1.0, sqf, ALU.add, ALU.mult))
                ch.then(V.tensor_tensor(TB[:, :], TB[:, :], sqf, ALU.mult))
                t3 = TB[:, :].rearrange("p (s j) -> p s j", j=NS)
                V.tensor_tensor(t3, t3, SM16[:, 7, :].unsqueeze(2).to_broadcast([P, STEPS, NS]), ALU.mult)\
                    .then_inc(sig["bo_ready"], 1)
                dve.wait_ge(sig["bo_ready"], u + 1)
                assert ch.n == PER_CELL, ch.n
            with dve.Fori(0, UNITS) as u:
                dve.wait_ge(sig["o_y"], 1 + u + 1)
                xs = X[:, bass.ds(u * TILES, TILES), :]
                V.tensor_tensor(xs, xs, PB[0][:, :].rearrange("p (n d) -> p n d", d=D), ALU.add).then_inc(sig["o_x"], 1)


        @block.sync
        def _(sp):
            sp.dma_start(WA[:, :, :], A["WA"]).then_inc(loaded, 16)
            sp.dma_start(VEC[:, :], A["VEC"]).then_inc(loaded, 16)
            sp.dma_start(CST[:, :], A["CST"]).then_inc(loaded, 16)
            sp.dma_start(WR0[:, :], A["WR0"]).then_inc(loaded, 16)
            xs = A["x"].rearrange("(n p) d -> p n d", p=P)
            sp.dma_start(X[:, :, :], xs).then_inc(loaded, 16)
            for dst, name in ((W2[:, :, :], "W2"), (B2[:, :], "B2"), (NEG[:, :], "NEG"), (WIN[:, :], "WIN"),
                              (WC[:, :, :], "WC"), (WOUT[:, :], "WOUT"), (WQKV[:, :], "WQKV"), (WPR[:, :], "WPR"),
                              (WR1[:, :], "WR1")):
                sp.dma_start(dst, A[name]).then_inc(late_loaded, 16)
            sp.wait_ge(sig["g_rstd"], 1)
            sp.wait_ge(sig["weights_used"], 1)
            sp.dma_start(W1[:, :], A["W1"]).then_inc(late_loaded, 16)
            sp.wait_ge(sig["b_acc"], 1 + UNITS * E)
            sp.dma_start(W1[:, 0:E * H1C * P], A["W1b"]).then_inc(late_loaded, 16)
            sp.dma_start(W2[:, 0:E * H1C, :], A["W2b"]).then_inc(late_loaded, 16)
            cell_sync(sp)

        @block.gpsimd
        def _(pool):
            pool.wait_ge(loaded, 16 * n_early)
            with pool.Fori(0, UNITS) as u:
                pool.wait_ge(sig["a_var"], u + 1)
                rstd_pow(RSTD[:, :], VE[:, :], TILES, sig["a_rstd"])
            pool.wait_ge(sig["g_ve"], 1)
            nc.gpsimd.tensor_tensor(GMS[:, 4, :], GMS[:, 3, :], NSC[:, 1, :], ALU.pow).then_inc(sig["g_rstd"], 1)
            with pool.Fori(0, UNITS) as u:
                pool.wait_ge(sig["c_var"], u + 1)
                rstd_pow(RSTD[:, :], VE[:, :], TILES, sig["c_rstd"])
            cell_pool(pool)

        @block.scalar
        def _(act):
            prime(act, (sig["a_xt"], sig["a_er"], sig["b_h"], sig["f_pc"], sig["c_xt"], sig["c_xp"], sig["co_copied"]))
            act.wait_ge(loaded, 16 * n_early)
            nc.scalar.activation(DW[:, 0:1], vec(DECAY), ACT.Exp).then_inc(sig["decay_exp"], 1)
            with act.Fori(0, UNITS) as u:
                act.wait_ge(sig["a_tr"], 1 + u + 1)
                apart(act)
                nc.scalar.activation(XT[:, bass.ds(u * UB, UB), 1:T + 1],
                                     two(PB[0][:, :]), ACT.Copy).then_inc(sig["a_xt"], 1)
                act.wait_ge(sig["a_r"], u + 1)
                act.wait_ge(sig["a_done"], 1 + u)
                nc.scalar.activation(ER, PB[1][:, :], ACT.Exp, scale=-1.0).then_inc(sig["a_er"], 1)
                act.wait_ge(sig["a_d"], u + 1)
                nc.scalar.activation(SC[:, 1024:2048], SC[:, 0:1024], ACT.Exp).then_inc(sig["a_e"], 1)
                act.wait_ge(sig["a_s"], u + 1)
                nc.scalar.activation(L1, Sx, ACT.Ln, bias=CST[:, C_EPS:C_EPS + 1]).then_inc(sig["a_l"], 1)
                act.wait_ge(sig["a_f"], u + 1)
                nc.scalar.activation(HT[:, 1, :], HT[:, 0, :], ACT.Exp).then_inc(sig["a_g"], 1)
            with act.Fori(0, UNITS) as u:
                act.wait_ge(sig["b_y"], 1 + u * E)
                apart(act)
                nc.scalar.activation(two(XU), XT[:, bass.ds(u * UB, UB), 1:T + 1], ACT.Copy).then_inc(sig["b_xu"], 1)
                act.wait_ge(sig["b_c"], u + 1)
                nc.scalar.activation(EX[:, :, :], LC[:, :, :], ACT.Exp).then_inc(sig["b_ex"], 1)
                act.wait_ge(sig["b_gt"], u + 1)
                nc.scalar.activation(GT[:, :], PB[6][0:E, :], ACT.Copy).then_inc(sig["b_gtc"], 1)
                for e in range(E):
                    if e >= 2:
                        act.wait_ge(sig["b_y"], 1 + u * E + e - 1)
                    for c in range(H0C):
                        k = e * H0C + c
                        act.wait_ge(sig["b_hp"], u * (E * H0C) + k + 1)
                        nc.scalar.activation(HT[:, e % 2, c * TOK:(c + 1) * TOK], PB[c][:, :], ACT.Relu,
                                             bias=CST[:, C_B1 + k:C_B1 + k + 1]).then_inc(sig["b_h"], 1)
            with act.Fori(0, UNITS) as u:
                act.wait_ge(sig["c_tr"], 1 + u + 1)
                act.wait_ge(sig["c_in"], 1 + u)
                nc.scalar.activation(HT[:, 0, 0:TOK], PB[0][:, :], ACT.Copy).then_inc(sig["c_xt"], 1)
                act.wait_ge(sig["c_in"], 1 + u + 1)
                apart(act)
                nc.scalar.activation(XP[:, bass.ds(u * UB, UB), :], two(PB[1][:, :]), ACT.Silu).then_inc(sig["c_xp"], 1)
            cell_act(act)

        @block.tensor
        def _(pe):
            prime(pe, (sig["a_tr"], sig["b_at"], sig["b_y"], sig["c_in"], sig["c_tr"], sig["f_pv"], sig["co_ready"], sig["o_y"]))
            pe.wait_ge(loaded, 16 * n_early)
            pe.wait_ge(prepared, 1)
            with pe.Fori(0, UNITS) as u:
                pe.wait_ge(sig["a_xn"], u + 1)
                pe.wait_ge(sig["a_xt"], 1 + u)
                for i in range(TILES):
                    last = nc.tensor.transpose(PB[0][:, i * P:(i + 1) * P], XNa[:, i, :], ident)
                last.then_inc(sig["a_tr"], 1)
                pe.wait_ge(sig["a_xt"], 1 + u + 1)
                pe.wait_ge(sig["a_done"], 1 + u)
                pe.wait_ge(sig["a_er"], 1 + u)
                for m, (bank, signal) in enumerate(((1, sig["a_r"]), (2, None), (3, sig["a_kv"]))):
                    nc.tensor.matmul(two(PB[bank][:, :]), WM[:, 0, m, :], XT[:, bass.ds(u * UB, UB), 1:T + 1],
                                     start=True, stop=False)
                    last = nc.tensor.matmul(two(PB[bank][:, :]), WM[:, 1, m, :], XT[:, bass.ds(u * UB, UB), 0:T],
                                            start=False, stop=True)
                    if signal is not None:
                        last.then_inc(signal, 1)
            pe.wait_ge(sig["a_done"], 1 + UNITS)
            nc.tensor.matmul(PB[0][:, 0:B], CST[:, C_GROUP:C_GROUP + P], MVR[:, :, 0], start=True,
                             stop=True).then_inc(sig["g_mean"], 1)
            pe.wait_ge(sig["g_dev"], 1)
            nc.tensor.matmul(PB[1][:, 0:B], CST[:, C_GROUP:C_GROUP + P], GMS[:, 2, :], start=True,
                             stop=True).then_inc(sig["g_var"], 1)
            pe.wait_ge(late_loaded, 16 * 10)
            with pe.Fori(0, UNITS) as u:
                pe.wait_ge(sig["b_xu"], u + 1)
                for i in range(TILES):
                    last = nc.tensor.matmul(PB[7][:, i * E:(i + 1) * E], XU[:, i * P:(i + 1) * P], WR0[:, :],
                                            start=True, stop=True)
                last.then_inc(sig["b_lg"], 1)

                def hidden(e):
                    for c in range(H0C):
                        k = e * H0C + c
                        if e >= 1:
                            pe.wait_ge(sig["b_h"], 1 + u * (E * H0C) + k - H0C + 1)
                        else:
                            pe.wait_ge(sig["b_h"], 1 + u * (E * H0C))
                        nc.tensor.matmul(PB[c][:, :], W1[:, k * P:(k + 1) * P], XU, start=True,
                                         stop=True).then_inc(sig["b_hp"], 1)

                pe.wait_ge(sig["b_gate"], u + 1)
                pe.wait_ge(sig["b_acc"], 1 + u * E)
                for i in range(TILES):
                    last = nc.tensor.transpose(PB[6][0:E, i * P:(i + 1) * P], GATE[:, i, :], ident)
                last.then_inc(sig["b_gt"], 1)
                hidden(0)
                pe.wait_ge(sig["b_n"], u + 1)
                pe.wait_ge(sig["b_gtc"], u + 1)
                pe.wait_ge(sig["b_x"], 1 + u)
                for i in range(TILES):
                    o = PB[5][:, i * P:(i + 1) * P]
                    nc.tensor.matmul(o, RN[:, i * P:(i + 1) * P],
                                     WA[:, 3, :], start=True, stop=False)
                    last = nc.tensor.matmul(o, GT[:, i * P:(i + 1) * P], B2[:, :], start=False, stop=True)
                last.then_inc(sig["b_at"], 1)
                for e in range(E):
                    if e + 1 < E:
                        hidden(e + 1)
                    pe.wait_ge(sig["b_h"], 1 + u * (E * H0C) + (e + 1) * H0C)
                    if e >= 2:
                        pe.wait_ge(sig["b_acc"], 1 + u * E + e - 1)
                    yb = PB[4 if e % 2 == 0 else 6]
                    for i in range(TILES):
                        for c in range(H0C):
                            last = nc.tensor.matmul(yb[:, i * P:(i + 1) * P],
                                                    HT[:, e % 2, c * TOK + i * P:c * TOK + (i + 1) * P],
                                                    W2[:, e * H0C + c, :], start=(c == 0), stop=(c == H0C - 1))
                    last.then_inc(sig["b_y"], 1)
            with pe.Fori(0, UNITS) as u:
                pe.wait_ge(sig["c_xn"], u + 1)
                pe.wait_ge(sig["c_xt"], 1 + u)
                for i in range(TILES):
                    last = nc.tensor.transpose(PB[0][:, i * P:(i + 1) * P], XNT[:, i, :], ident)
                last.then_inc(sig["c_tr"], 1)
                pe.wait_ge(sig["c_xt"], 1 + u + 1)
                pe.wait_ge(sig["c_xp"], 1 + u)
                nc.tensor.matmul(PB[1][:, :], WIN[:, :], HT[:, 0, 0:TOK], start=True, stop=True).then_inc(sig["c_in"], 1)
            cell_pe(pe)

        @block.vector
        def _(dve):
            prime(dve, (sig["a_done"], sig["b_acc"], sig["b_x"], sig["prep_done"], sig["f_y"], sig["m_acc"], sig["o_x"], sig["f_x2"]))
            V = nc.vector
            dve.wait_ge(loaded, 16 * n_early)
            ch = Chain(dve, dve_chain)
            ch.done(V.memset(XT[:, :, 0:1], 0.0))
            ch.done(V.memset(Dx[:, 0, :, 0:1], LOW))
            ch.done(V.memset(Bx[:, :, 0:1], LOW))
            ch.done(V.memset(Ax[:, 0:1], 0.0))
            for m in range(3):
                ch.done(V.tensor_scalar(WM[:, 0, m, :], WA[:, m, :], vec(MIX_R + m), None, ALU.mult))
            ch.then(V.tensor_scalar(NSC[:, 0, 0:3], VEC[:, 0:3], -1.0, 1.0, ALU.mult, ALU.add))
            for m in range(3):
                ch.done(V.tensor_scalar(WM[:, 1, m, :], WA[:, m, :], NSC[:, 0, m:m + 1], None, ALU.mult))
            dve.wait_ge(sig["decay_exp"], 1)
            ch.then(V.tensor_scalar(DW[:, 1:2], DW[:, 0:1], -1.0, None, ALU.mult))
            ch.then(V.tensor_scalar(WD, CST[:, C_ID:C_ID + 1].to_broadcast([P, TOK]), 0.0, DW[:, 1:2],
                                    ALU.mult, ALU.add))
            V.memset(two(WD)[:, :, 0:1], LOW).then_inc(prepared, 1)
            dve.wait_ge(prepared, 1)
            start = ch.n
            PER_A = 29
            with dve.Fori(0, UNITS) as u:
                ch = Chain(dve, dve_chain, start + u * PER_A)
                tile = lambda i: X[:, bass.ds(u * TILES + i, 1), :].rearrange("p n d -> p (n d)")
                norm_stats(dve, ch, tile, sig["a_var"])
                dve.wait_ge(sig["a_rstd"], u + 1)
                dve.wait_ge(sig["a_tr"], 1 + u)
                norm_apply(lambda i: XNa[:, i, :], tile, sig["a_xn"])
                K, Vv = PB[2][:, :], PB[3][:, :]
                w, first = DW[:, 1:2], vec(FIRST)
                dve.wait_ge(sig["a_kv"], u + 1)
                ch.then(V.tensor_tensor_scan(Mx, WD, K, LOW, ALU.add, ALU.max))
                ch.done(V.scalar_tensor_tensor(Dx[:, 0, :, 1:T], two(Mx)[:, :, 0:T - 1], w, two(Mx)[:, :, 1:T],
                                               ALU.add, ALU.subtract))
                V.tensor_tensor(Dx[:, 1, :, :], two(K), two(Mx), ALU.subtract).then_inc(sig["a_d"], 1)
                dve.wait_ge(sig["a_e"], u + 1)
                V.tensor_tensor_scan(Sx, SC[:, 1024:1536], SC[:, 1536:2048], 0.0, ALU.mult, ALU.add).then_inc(sig["a_s"], 1)
                dve.wait_ge(sig["a_l"], u + 1)
                ch.then(V.tensor_tensor(Bx[:, :, 1:T + 1], two(Mx), two(L1), ALU.add))
                Bp = Bx[:, :, 0:T]
                ch.done(V.scalar_tensor_tensor(two(P2), Bp, w, two(K), ALU.add, ALU.max))
                ch.then(V.scalar_tensor_tensor(two(P1), two(K), first, Bp, ALU.add, ALU.max))
                ch.done(V.scalar_tensor_tensor(Fx[:, 0, :, :], Bp, w, two(P2), ALU.add, ALU.subtract))
                ch.done(V.tensor_tensor(Fx[:, 1, :, :], two(K), two(P2), ALU.subtract))
                ch.done(V.tensor_tensor(Fx[:, 2, :, :], Bp, two(P1), ALU.subtract))
                V.scalar_tensor_tensor(Fx[:, 3, :, :], two(K), first, two(P1), ALU.add, ALU.subtract)\
                    .then_inc(sig["a_f"], 1)
                dve.wait_ge(sig["a_g"], u + 1)
                g = [HT[:, 1, k * TOK:(k + 1) * TOK] for k in range(4)]
                ch.then(V.tensor_tensor(N1, g[1], Vv, ALU.mult))
                ch.then(V.tensor_tensor_scan(Ax[:, 1:TOK + 1], g[0], N1, 0.0, ALU.mult, ALU.add))
                ch.done(V.tensor_tensor(N1, g[2], Ax[:, 0:TOK], ALU.mult))
                ch.then(V.tensor_tensor(N2, g[3], Vv, ALU.mult))
                ch.done(V.tensor_tensor(N1, N1, N2, ALU.add))
                ch.then(V.scalar_tensor_tensor(P1, g[2], WKV_EPS, g[3], ALU.add, ALU.add))
                dve.wait_ge(sig["a_er"], 1 + u + 1)
                ch.then(V.scalar_tensor_tensor(P1, ER, 1.0, P1, ALU.add, ALU.mult))
                ch.then(V.reciprocal(P1, P1))
                rw = RW[:, bass.ds(u * UB, UB), :]
                ch.then(V.tensor_tensor(rw, two(N1), two(P1), ALU.mult))
                apart(dve)
                for b in range(UB):
                    ch.done(V.bn_stats(BNR[:, b, :], RW[:, bass.ds(u * UB + b, 1), :].rearrange("p b t -> p (b t)")))
                ch.settle()
                apart(dve)
                ch.done(V.bn_aggr(MVU[:, 0, :], BNR[:, 0, :]))
                ch.then(V.bn_aggr(MVU[:, 1, :], BNR[:, 1, :]))
                V.tensor_copy(MVR[:, bass.ds(u * UB, UB), :], MVU).then_inc(sig["a_done"], 1)
                assert ch.n == PER_A
            start += UNITS * PER_A
            ch = Chain(dve, dve_chain, start)
            dve.wait_ge(sig["g_mean"], 1)
            dve.wait_ge(sig["a_done"], 1 + UNITS)
            ch.done(V.tensor_copy(GMS[:, 0, :], PB[0][:, 0:B]))
            ch.then(V.tensor_tensor(GMS[:, 1, :], MVR[:, :, 0], PB[0][:, 0:B], ALU.subtract))
            ch.then(V.tensor_tensor(GMS[:, 1, :], GMS[:, 1, :], GMS[:, 1, :], ALU.mult))
            V.tensor_tensor(GMS[:, 2, :], GMS[:, 1, :], MVR[:, :, 1], ALU.add).then_inc(sig["g_dev"], 1)
            dve.wait_ge(sig["g_var"], 1)
            ch.then(V.memset(NSC[:, 1, :], -0.5))
            V.tensor_scalar(GMS[:, 3, :], PB[1][:, 0:B], LN_EPS, None, ALU.add).then_inc(sig["g_ve"], 1)
            dve.wait_ge(sig["g_rstd"], 1)
            ch.then(V.tensor_scalar(NSC[:, 0, :], GMS[:, 4, :], vec(GAMMA), None, ALU.mult))
            ch.then(V.tensor_tensor(GMS[:, 5, :], GMS[:, 0, :], NSC[:, 0, :], ALU.mult))
            V.tensor_scalar(NSC[:, 1, :], GMS[:, 5, :], -1.0, vec(BETA), ALU.mult, ALU.add).then_inc(sig["weights_used"], 1)
            dve.wait_ge(sig["weights_used"], 1)
            start += ch.n
            PER_B = 10
            with dve.Fori(0, UNITS) as u:
                ch = Chain(dve, dve_chain, start + u * PER_B)
                dve.wait_ge(sig["b_at"], 1 + u)
                for b in range(UB):
                    row = RW[:, bass.ds(u * UB + b, 1), :].rearrange("p b t -> p (b t)")
                    last = V.tensor_scalar(RN[:, b * T:(b + 1) * T], row, NSC[:, 0, bass.ds(u * UB + b, 1)],
                                           NSC[:, 1, bass.ds(u * UB + b, 1)], ALU.mult, ALU.add)
                last.then_inc(sig["b_n"], 1)
                dve.wait_ge(sig["b_lg"], u + 1)
                gate_logits(dve, ch, True, sig["b_c"])
                gate_weights(dve, ch, sig["b_ex"], u + 1, sig["b_gate"])
                dve.wait_ge(sig["b_gate"], u + 1)
                dve.wait_ge(sig["b_at"], 1 + u + 1)
                xs = X[:, bass.ds(u * TILES, TILES), :]
                V.tensor_tensor(xs, xs, PB[5][:, :].rearrange("p (n d) -> p n d", d=D), ALU.add).then_inc(sig["b_x"], 1)
                dve.wait_ge(sig["b_x"], 1 + u + 1)
                for e in range(E):
                    dve.wait_ge(sig["b_y"], 1 + u * E + e + 1)
                    if e >= 1:
                        dve.wait_ge(sig["b_acc"], 1 + u * E + e)
                    yb = PB[4 if e % 2 == 0 else 6]
                    for i in range(TILES):
                        x = X[:, bass.ds(u * TILES + i, 1), :].rearrange("p n d -> p (n d)")
                        last = V.scalar_tensor_tensor(x, yb[:, i * P:(i + 1) * P], GATE[:, i, e:e + 1], x,
                                                      ALU.mult, ALU.add)
                    last.then_inc(sig["b_acc"], 1)
                assert ch.n == PER_B
            start += UNITS * PER_B
            dve.wait_ge(sig["b_acc"], 1 + UNITS * E)
            with dve.Fori(0, UNITS) as u:
                ch = Chain(dve, dve_chain, start + u * 9)
                tile = lambda i: X[:, bass.ds(u * TILES + i, 1), :].rearrange("p n d -> p (n d)")
                norm_stats(dve, ch, tile, sig["c_var"])
                dve.wait_ge(sig["c_rstd"], u + 1)
                dve.wait_ge(sig["c_tr"], 1 + u)
                norm_apply(lambda i: XNT[:, i, :], tile, sig["c_xn"])
                dve.wait_ge(sig["c_xn"], u + 1)
                ch.done(V.tensor_copy(XN[:, bass.ds(u * TILES, TILES), :], XNT[:, :, :]))
            start += UNITS * 9
            cell_dve(dve, start)


def kernel(**inputs):
    import numpy as np
    import ml_dtypes
    import concourse.bacc as bacc
    from concourse.bass_utils import run_bass_kernel_spmd

    def arr(n):
        return np.asarray(inputs[n])

    q = np.arange(P)
    cst = np.zeros((P, C_END), np.float32)
    cst[:, C_ID:C_ID + P] = np.eye(P)
    cst[:, C_GROUP:C_GROUP + P] = (q[:, None] // HD == q[None, :] // HD) / HD
    cst[:, C_SEL:C_SEL + NS] = q[:, None] % B == np.arange(B)[None, :]
    cst[:, C_MASK:C_MASK + 4] = (q[:, None] % 32 // HD == np.arange(4)[None, :]) / np.sqrt(HD)
    cst[:, C_HOT:C_HOT + NB] = q[:, None] // B == np.arange(NB)[None, :]
    cst[:, C_LT8:C_LT8 + E * E] = (np.arange(E)[None, :] < np.arange(E)[:, None]).reshape(1, -1)
    cst[:, C_LT4:C_LT4 + NB * NB] = (np.arange(NB)[None, :] < np.arange(NB)[:, None]).reshape(1, -1)
    cst[:, C_BR:C_BR + E] = arr("L0_ffn_br")[None, :]
    cst[:, C_BB:C_BB + NS] = np.repeat(arr("L1_attn_b_beta"), B, axis=0)
    cst[:, C_B1:C_B1 + E * H0C] = arr("L0_ffn_b1").reshape(E * H0C, P).T
    cst[:, C_NHALF:C_NHALF + TILES] = -0.5
    cst[:, C_HALF:C_HALF + STEPS] = 0.5
    cst[:, C_EPS] = WKV_EPS
    neg = np.zeros((P, 3 * P), ml_dtypes.bfloat16)
    neg[:, 0:P] = np.eye(P)
    neg[:, 2 * P:3 * P] = np.where(q[None, :] > q[:, None], -1e30, 0.0)
    wkv = arr("L1_attn_W_kv").reshape(NB, 2, NS, D)
    wb = arr("L1_attn_W_beta").reshape(NB, NS, D)
    wq, wr = arr("L1_attn_W_q"), arr("L1_attn_W_router")
    wc = np.stack([np.concatenate([wkv[n, 0], wkv[n, 1], wb[n], wq, wr]) for n in range(NB)])
    data = {
        "x": arr("L0_attn_x").reshape(B * T, D),
        "WA": np.stack([arr("L0_attn_W_" + c).T for c in "rkvo"], axis=1),
        "VEC": np.stack([arr(n).reshape(D) for n in (
            "L0_attn_time_mix_r", "L0_attn_time_mix_k", "L0_attn_time_mix_v", "L0_attn_time_decay",
            "L0_attn_time_first", "L0_attn_ln_gamma", "L0_attn_ln_beta", "L1_ffn_ln1_w", "L1_ffn_ln2_w")], axis=1),
        "CST": cst, "NEG": neg,
        "WR0": arr("L0_ffn_Wr"),
        "W1": arr("L0_ffn_W1").transpose(1, 0, 2).reshape(D, E * H0C * P),
        "W2": arr("L0_ffn_W2").reshape(E * H0C, P, D).transpose(1, 0, 2),
        "B2": arr("L0_ffn_b2"),
        "WIN": arr("L1_attn_W_in").T,
        "WC": wc.transpose(2, 0, 1),
        "WOUT": arr("L1_attn_W_out").T,
        "WQKV": arr("L1_ffn_c_attn_w"),
        "WPR": arr("L1_ffn_c_proj_w"),
        "WR1": arr("L1_ffn_router_w"),
        "W1b": arr("L1_ffn_w1"),
        "W2b": arr("L1_ffn_w2").reshape(E * H1C, P, D).transpose(1, 0, 2),
    }
    nc = bacc.Bacc("TRN2", target_bir_lowering=False, num_devices=1)
    arrays, aps = {}, {}
    for name, a in data.items():
        a = np.ascontiguousarray(a)
        arrays["in_" + name] = a
        aps[name] = nc.dram_tensor("in_" + name, a.shape, mybir.dt.from_np(a.dtype), kind="ExternalInput").ap()
    out = nc.dram_tensor("out", (B * T, D), F32, kind="ExternalOutput").ap()
    build(nc, aps, out)
    r = run_bass_kernel_spmd(nc, [arrays], core_ids=[0])
    return r.results[0]["out"].reshape(B, T, D)
```

```python
import concourse.bass as bass
from concourse import mybir
from contextlib import ExitStack

B, T, D = 32, 256, 128
P = 128
UB = 2
UNITS = B // UB
TILES = UB * T // P
TOK = UB * T
E = 8
H0C, H1C = 4, 2
NH, HD = 16, 8
NB, NS = 4, 32
STEPS = T // UNITS
CELL = 4 * NS + NB
LN_EPS, WKV_EPS = 1e-5, 1e-8
LOW = -1e38

F32 = mybir.dt.float32
BF16 = mybir.dt.bfloat16
ALU = mybir.AluOpType
ACT = mybir.ActivationFunctionType
AX = mybir.AxisListType.X

MIX_R, MIX_K, MIX_V, DECAY, FIRST, GAMMA, BETA, LN1_W, LN2_W = range(9)
C_ID = 0
C_GROUP = C_ID + P
C_SEL = C_GROUP + P
C_MASK = C_SEL + NS
C_HOT = C_MASK + 4
C_LT8 = C_HOT + NB
C_LT4 = C_LT8 + E * E
C_BR = C_LT4 + NB * NB
C_BB = C_BR + E
C_B1 = C_BB + NS
C_NHALF = C_B1 + E * H0C
C_HALF = C_NHALF + TILES
C_EPS = C_HALF + STEPS
C_END = C_EPS + 1


PER_CELL = 151
CELL_SEMS = (
    "scaled", "p_proj", "p_copied", "p_b", "p_bt", "p_ss", "p_norm", "p_lc", "p_le", "vq_copied", "prep_done",
    "z_ready", "th_done", "w_ready", "sq_product", "sq_summed", "sq_reduced", "sq_ready", "sq_t", "bo_ready", "co_ready", "co_copied",
    "f_var", "f_rstd", "f_xn", "f_tr", "f_xa", "f_q", "f_k", "f_v", "f_qm", "f_kt", "f_vt",
    "f_s", "f_m", "f_e", "f_t", "f_pc", "f_pv", "f_y", "f_yt", "f_yc", "f_pj", "f_x2",
    "h_var", "h_rstd", "h_xn", "h_tr", "h_xm", "h_lg", "h_c", "h_ex", "h_gate",
    "m_hp", "m_h", "m_y", "m_acc", "o_y", "o_x")


class Chain:

    def __init__(self, eng, sem, base=0):
        self.eng, self.sem, self.base, self.n = eng, sem, base, 0

    def done(self, ins):
        ins.then_inc(self.sem, 1)
        self.n += 1

    def mark(self, ins):
        self.done(ins)
        return self.n

    def reach(self, step):
        self.eng.wait_ge(self.sem, self.base + step)

    def settle(self):
        self.eng.wait_ge(self.sem, self.base + self.n)

    def then(self, ins):
        self.done(ins)
        self.settle()


def build(nc, A, out):
    ctx = ExitStack()
    with ctx:
        def sb(name, shape, dt=F32):
            return ctx.enter_context(nc.sbuf_tensor(name, shape, dt))

        def sem(name):
            return ctx.enter_context(nc.semaphore(name))

        X = sb("X", [P, B * T // P, D])
        FT = sb("FT", [P, B * (T + 1)])
        XT = FT[:, :].rearrange("p (b t) -> p b t", b=B)
        XP = FT[:, 0:B * T].rearrange("p (b t) -> p b t", b=B)
        RX = sb("RX", [P, B * T])
        RW = RX[:, :].rearrange("p (b t) -> p b t", b=B)
        XN = RX[:, :].rearrange("p (n d) -> p n d", d=D)
        W1 = sb("W1", [P, E * H0C * P])
        W2 = sb("W2", [P, E * H0C, D])
        WA = sb("WA", [P, 4, D])
        WM = sb("WM", [P, 2, 3, D])
        WR0 = sb("WR0", [P, E])
        B2 = sb("B2", [E, D])
        VEC = sb("VEC", [P, 9])
        CST = sb("CST", [P, C_END])
        NEG = sb("NEG", [P, 3 * P], BF16)
        WIN = sb("WIN", [P, D])
        WC = sb("WC", [P, NB, CELL])
        WOUT = sb("WOUT", [NS, D])
        WQKV = sb("WQKV", [P, 3 * D])
        WPR = sb("WPR", [P, D])
        WR1 = sb("WR1", [P, E])
        HT = sb("HT", [P, 2, H0C * TOK])
        SC = sb("SC", [P, 6 * NS * NS])
        BNS = sb("BNS", [P, TILES, 6])
        MV = sb("MV", [P, TILES, 2])
        VE = sb("VE", [P, TILES])
        RSTD = sb("RSTD", [P, TILES])
        XNT = sb("XNT", [P, TILES, D])
        LG = sb("LG", [P, TILES, E])
        MX = sb("MX", [P, TILES])
        LC = sb("LC", [P, TILES, E])
        EX = sb("EX", [P, TILES, E])
        CMP = sb("CMP", [P, 2, TILES * E * E])
        RK = sb("RK", [P, TILES, E])
        GATE = sb("GATE", [P, TILES, E])
        GS = sb("GS", [P, TILES])
        TB = sb("TB", [P, TOK])
        GT = TB[0:E, :]

        ident = CST[:, C_ID:C_ID + P]

        def vec(c):
            return VEC[:, c:c + 1]

        PB = [ctx.enter_context(nc.psum_tensor(f"PB{i}", [P, 512], F32)) for i in range(8)]

        loaded = sem("loaded")
        late_loaded = sem("late_loaded")
        prepared = sem("prepared")
        dve_chain = sem("dve_chain")

        block = ctx.enter_context(nc.Block())

        Dx = SC[:, 0:1024].rearrange("p (k b t) -> p k b t", k=2, b=UB)
        Ex = SC[:, 1024:2048].rearrange("p (k b t) -> p k b t", k=2, b=UB)
        Fx = HT[:, 0, :].rearrange("p (k b t) -> p k b t", k=4, b=UB)
        Gx = HT[:, 1, :].rearrange("p (k b t) -> p k b t", k=4, b=UB)
        Mx = SC[:, 2048:2560]
        Sx = SC[:, 2560:3072]
        Bx = SC[:, 3072:3072 + UB * (T + 1)].rearrange("p (b t) -> p b t", b=UB)
        Ax = SC[:, 3600:3600 + TOK + 1]
        P1 = SC[:, 4120:4632]
        P2 = SC[:, 4632:5144]
        N1 = SC[:, 5144:5656]
        ER = XNT[:, :, :].rearrange("p n d -> p (n d)")
        WD = W1[:, 0:TOK]
        N2 = W1[:, 512:1024]
        L1 = W1[:, 1024:1536]
        XNa = W1[:, 1536:2048].rearrange("p (n d) -> p n d", d=D)
        MVR = W1[:, 2048:2048 + 2 * B].rearrange("p (b k) -> p b k", k=2)
        BNR = W1[:, 2112:2112 + 6 * UB].rearrange("p (b k) -> p b k", k=6)
        MVU = W1[:, 2130:2130 + 2 * UB].rearrange("p (b k) -> p b k", k=2)
        GMS = W1[:, 2200:2200 + 6 * B].rearrange("p (k b) -> p k b", k=6)
        DW = sb("DW", [P, 2])
        NSC = sb("NSC", [P, 2, B])

        XU = SC[:, 0:TOK]
        RN = SC[:, TOK:2 * TOK]

        def two(ap):
            return ap.rearrange("p (b t) -> p b t", b=UB)

        sig = {n: sem(n) for n in (
            "a_var", "a_rstd", "a_xn", "a_tr", "a_xt", "a_r", "a_kv", "a_er", "a_d", "a_e", "a_s", "a_l",
            "a_f", "a_g", "a_done", "g_mean", "g_dev", "g_var", "g_ve", "g_rstd", "weights_used",
            "b_n", "b_xu", "f_cu", "o_st", "b_lg", "b_c", "b_ex", "b_gate", "b_gt", "b_gtc", "b_at", "b_x", "b_hp", "b_h", "b_y", "b_acc",
            "c_var", "c_rstd", "c_xn", "c_tr", "c_xt", "c_in", "c_xp",
            "decay_exp", "stored") + CELL_SEMS}

        n_early = 5

        def prime(eng, signals):
            for signal in signals:
                eng.sem_inc(signal, 1)

        def apart(eng):
            eng.nop(nofuse=True)

        def norm_stats(dve, ch, src, signal):
            apart(dve)
            for i in range(TILES):
                ch.done(nc.vector.bn_stats(BNS[:, i, :], src(i)))
            ch.settle()
            apart(dve)
            for i in range(TILES):
                ch.done(nc.vector.bn_aggr(MV[:, i, :], BNS[:, i, :]))
            ch.settle()
            nc.vector.tensor_scalar(VE[:, :], MV[:, :, 1], LN_EPS, None, ALU.add).then_inc(signal, 1)

        def norm_apply(dst, src, signal):
            for i in range(TILES):
                last = nc.vector.tensor_scalar(dst(i), src(i), MV[:, i, 0:1], RSTD[:, i:i + 1],
                                               ALU.subtract, ALU.mult)
            last.then_inc(signal, 1)

        def rstd_pow(out_ap, in_ap, n, signal):
            nc.gpsimd.tensor_tensor(out_ap, in_ap, CST[:, C_NHALF:C_NHALF + n], ALU.pow).then_inc(signal, 1)

        def gate_logits(dve, ch, bias, signal):
            if bias:
                ch.then(nc.vector.tensor_tensor(
                    LG[:, :, :], PB[7][:, 0:TILES * E].rearrange("p (n e) -> p n e", e=E),
                    CST[:, C_BR:C_BR + E].unsqueeze(1).to_broadcast([P, TILES, E]), ALU.add))
            else:
                ch.then(nc.vector.tensor_copy(LG[:, :, :], PB[7][:, 0:TILES * E].rearrange("p (n e) -> p n e", e=E)))
            ch.then(nc.vector.tensor_reduce(MX[:, :], LG[:, :, :], AX, ALU.max))
            nc.vector.tensor_tensor(LC[:, :, :], LG[:, :, :], MX[:, :].unsqueeze(2).to_broadcast([P, TILES, E]),
                                    ALU.subtract).then_inc(signal, 1)

        def top_two_rank(ch, lg, rank, n, e, lt):
            other = lg.unsqueeze(2).to_broadcast([P, n, e, e])
            own = lg.unsqueeze(3).to_broadcast([P, n, e, e])
            gt = CMP[:, 0, 0:n * e * e].rearrange("p (n e f) -> p n e f", n=n, e=e)
            eq = CMP[:, 1, 0:n * e * e].rearrange("p (n e f) -> p n e f", n=n, e=e)
            ch.done(nc.vector.tensor_tensor(gt, other, own, ALU.is_gt))
            ch.then(nc.vector.tensor_tensor(eq, other, own, ALU.is_equal))
            low = CST[:, lt:lt + e * e].unsqueeze(1).to_broadcast([P, n, e * e])
            eqf = CMP[:, 1, 0:n * e * e].rearrange("p (n e) -> p n e", n=n)
            ch.then(nc.vector.tensor_tensor(eqf, eqf, low, ALU.mult))
            ch.then(nc.vector.tensor_tensor(CMP[:, 0, 0:n * e * e], CMP[:, 0, 0:n * e * e],
                                            CMP[:, 1, 0:n * e * e], ALU.add))
            ch.then(nc.vector.tensor_reduce(rank, gt, AX, ALU.add))

        def gate_weights(dve, ch, exp_ready, value, signal):
            top_two_rank(ch, LG[:, :, :], RK[:, :, :], TILES, E, C_LT8)
            top_two(dve, ch, exp_ready, value, signal)

        def top_two(dve, ch, exp_ready, value, signal):
            dve.wait_ge(exp_ready, value)
            ch.then(nc.vector.scalar_tensor_tensor(GATE[:, :, :], RK[:, :, :], 2.0, EX[:, :, :],
                                                   ALU.is_lt, ALU.mult))
            ch.then(nc.vector.tensor_reduce(GS[:, :], GATE[:, :, :], AX, ALU.add))
            ch.then(nc.vector.reciprocal(GS[:, :], GS[:, :]))
            nc.vector.tensor_tensor(GATE[:, :, :], GATE[:, :, :], GS[:, :].unsqueeze(2).to_broadcast([P, TILES, E]),
                                    ALU.mult).then_inc(signal, 1)


        St = SC[:, 0:1024]
        PRD, ZB, BS, TH, PQ = (SC[:, k * 1024:(k + 1) * 1024] for k in range(1, 6))
        QM = sb("QM", [P, 4, TOK])
        CU = QM[:, 0, :].rearrange("p (s b) -> p s b", b=B)
        RAW = sb("RAW", [P, STEPS, CELL])
        KN, VV = (HT[:, 0, 1024 + k * 512:1536 + k * 512].rearrange("p (s j) -> p s j", j=NS) for k in range(2))
        QQ, BT = (HT[:, 1, 1024 + k * 512:1536 + k * 512].rearrange("p (s j) -> p s j", j=NS) for k in range(2))
        PEX = W1[:, 2048:3584].rearrange("p (j k) -> p j k", j=3)
        XA = W1[:, 3584:4096]
        W2f = W2[:, :, :].rearrange("p n d -> p (n d)")
        PTS = W2f[:, 2048:3584].rearrange("p (j k) -> p j k", j=3)
        KT = W2f[:, 3584:4096]
        VT = sb("VT", [P, TILES, D])
        WMf = WM[:, :, :, :].rearrange("p a m d -> p (a m d)")
        SQ = WMf[:, 0:STEPS * NS].rearrange("p (s i) -> p s i", i=NS)
        Y = WMf[:, STEPS * NS:STEPS * NS + 2 * D].rearrange("p (q d) -> p q d", d=D)
        YT = WA[:, 0:2, :].rearrange("p a d -> p (a d)")
        RS = sb("RS", [P, UB, 2, NH])
        RI = sb("RI", [P, 2, NH])
        NM = sb("NM", [P, 3, 4])
        SM16 = sb("SM16", [P, 8, STEPS])
        SM64 = WA[:, 2:4, :].rearrange("p a (k s n) -> p (a k) s n", k=2, n=NB)
        RET = NSC

        def v3(ap):
            return ap.rearrange("p (i j) -> p i j", j=NS)

        def bi(ap):
            return ap.unsqueeze(1).to_broadcast([P, NS, NS])

        def bj(ap):
            return ap.unsqueeze(2).to_broadcast([P, NS, NS])

        def tilef(buf, u, i):
            return buf[:, bass.ds(u * TILES + i, 1), :].rearrange("p n d -> p (n d)")

        def cell_sync(sp):
            outs = out.rearrange("(n p) d -> p n d", p=P)
            with sp.Fori(0, UNITS) as u:
                sp.wait_ge(sig["o_x"], 1 + u + 1)
                sp.dma_start(outs[:, bass.ds(u * TILES, TILES), :], X[:, bass.ds(u * TILES, TILES), :]).then_inc(sig["stored"], 16)
            sp.wait_ge(sig["stored"], 16 * UNITS)

        def cell_pool(pool):
            with pool.Fori(0, UNITS) as u:
                pool.wait_ge(sig["f_var"], u + 1)
                rstd_pow(RSTD[:, :], VE[:, :], TILES, sig["f_rstd"])
                pool.wait_ge(sig["p_ss"], u + 1)
                nc.gpsimd.tensor_tensor(SM16[:, 1, :], SM16[:, 0, :], CST[:, C_HALF:C_HALF + STEPS],
                                        ALU.pow).then_inc(sig["p_norm"], 1)
                pool.wait_ge(sig["h_var"], u + 1)
                rstd_pow(RSTD[:, :], VE[:, :], TILES, sig["h_rstd"])

        def cell_act(act):
            def copy_inputs(u, first=0):
                apart(act)
                rows = FT[:, first:first + B * T].rearrange("p (b t) -> p b t", b=B)
                nc.scalar.activation(CU, rows[:, :, bass.ds(u * STEPS, STEPS)].rearrange("p b t -> p t b"),
                                     ACT.Copy).then_inc(sig["f_cu"], 1)

            def copy_projections(u, pairs):
                for g in pairs:
                    act.wait_ge(sig["p_proj"], u * (STEPS // 2) + g + 1)
                    nc.scalar.activation(RAW[:, 2 * g:2 * g + 2, :],
                                         pair_bank(g), ACT.Copy).then_inc(sig["p_copied"], 1)

            def exponentials(u, c):
                b, g = c // 4, c % 4
                for j in range(3):
                    act.wait_ge(sig["f_m"], u * 24 + 3 * c + j + 1)
                    heads = range(4) if j == 0 else (2 * j - 2, 2 * j - 1)
                    w = 512 // len(heads)
                    for n, h in enumerate(heads):
                        last = nc.scalar.activation(PEX[:, j, n * w:(n + 1) * w], PB[j][:, n * w:(n + 1) * w],
                                                    ACT.Exp, bias=NM[:, j, n:n + 1],
                                                    accum_out=RS[:, b, min(j, 1), 4 * g + h:4 * g + h + 1])
                    last.then_inc(sig["f_e"], 1)

            def copy_transposes(u, c):
                act.wait_ge(sig["f_pv"], 1 + u * 8 + c)
                for j in range(3):
                    act.wait_ge(sig["f_t"], u * 24 + 3 * c + j + 1)
                    nc.scalar.activation(PTS[:, j, :], PB[3 + j % 2][:, :], ACT.Copy).then_inc(sig["f_pc"], 1)

            def copy_attention(u, b):
                act.wait_ge(sig["f_yt"], u * UB + b + 1)
                nc.scalar.activation(YT[:, :], PB[6][:, 0:2 * P], ACT.Copy).then_inc(sig["f_yc"], 1)

            def gelu(u, e):
                if e >= 2:
                    act.wait_ge(sig["m_y"], u * E + e - 1)
                for c in range(H1C):
                    act.wait_ge(sig["m_hp"], u * (E * H1C) + e * H1C + c + 1)
                    nc.scalar.activation(HT[:, e % 2, c * TOK:(c + 1) * TOK], PB[2 * (e % 2) + c][:, :],
                                         ACT.Gelu).then_inc(sig["m_h"], 1)

            def before_tanh(u, st):
                if st == 0:
                    act.wait_ge(sig["f_tr"], u + 1)
                    nc.scalar.activation(XA, PB[6][:, :], ACT.Copy).then_inc(sig["f_xa"], 1)
                    act.wait_ge(sig["f_q"], u + 1)
                    for h in range(4):
                        last = nc.scalar.activation(QM[:, h, :], PB[0][:, :], ACT.Copy,
                                                    scale=CST[:, C_MASK + h:C_MASK + h + 1])
                    last.then_inc(sig["f_qm"], 1)
                    act.wait_ge(sig["f_k"], u + 1)
                    nc.scalar.activation(KT, PB[1][:, :], ACT.Copy).then_inc(sig["f_kt"], 1)
                    act.wait_ge(sig["f_v"], u + 1)
                    nc.scalar.activation(VT[:, :, :], PB[2][:, :].rearrange("p (n d) -> p n d", d=D),
                                         ACT.Copy).then_inc(sig["f_vt"], 1)
                if st == 6:
                    copy_attention(u, 0)
                if 1 <= st <= 8:
                    exponentials(u, st - 1)
                if st == 9:
                    copy_projections(u + 1, (0, 1))
                    copy_attention(u, 1)
                    copy_projections(u + 1, (2,))
                if st == 10:
                    copy_projections(u + 1, (5, 6, 7))
                    act.wait_ge(sig["h_tr"], u + 1)
                    nc.scalar.activation(XA, PB[6][:, :], ACT.Copy).then_inc(sig["h_xm"], 1)
                if st == 11:
                    act.wait_ge(sig["h_c"], u + 1)
                    nc.scalar.activation(EX[:, :, :], LC[:, :, :], ACT.Exp).then_inc(sig["h_ex"], 1)
                if 11 <= st <= 14:
                    gelu(u, 2 * (st - 11))

            def after_tanh(u, st):
                if 1 <= st <= 8:
                    copy_transposes(u, st - 1)
                if st == 8:
                    act.wait_ge(sig["f_s"], (u + 1) * 24)
                    act.wait_ge(sig["co_copied"], 1 + u)
                    copy_inputs(u, STEPS)
                if st == 9:
                    copy_projections(u + 1, (3, 4))
                if 11 <= st <= 14:
                    gelu(u, 2 * (st - 11) + 1)

            act.wait_ge(sig["scaled"], 1)
            act.wait_ge(sig["c_xp"], 1 + UNITS)
            copy_inputs(0)
            copy_projections(0, range(STEPS // 2))
            with act.Fori(0, UNITS) as u:
                act.wait_ge(sig["p_b"], u + 1)
                nc.scalar.activation(BS[:, 512:1024], BS[:, 0:512], ACT.Tanh, scale=0.5).then_inc(sig["p_bt"], 1)
                act.wait_ge(sig["p_lc"], u + 1)
                nc.scalar.activation(SM64[:, 1, :, :], SM64[:, 0, :, :], ACT.Exp).then_inc(sig["p_le"], 1)
                act.wait_ge(sig["p_copied"], (u + 1) * (STEPS // 2))
                nc.scalar.activation(VV, RAW[:, :, NS:2 * NS], ACT.Copy)
                nc.scalar.activation(QQ, RAW[:, :, 3 * NS:4 * NS], ACT.Copy).then_inc(sig["vq_copied"], 1)
                for st in range(STEPS):
                    before_tanh(u, st)
                    act.wait_ge(sig["z_ready"], u * STEPS + st + 1)
                    nc.scalar.activation(TH, ZB, ACT.Tanh).then_inc(sig["th_done"], 1)
                    act.wait_ge(sig["th_done"], u * STEPS + st + 1)
                    nc.scalar.activation(TH, TH, ACT.Copy, scale=SM16[:, 4, st:st + 1]).then_inc(sig["w_ready"], 1)
                    after_tanh(u, st)
                act.wait_ge(sig["sq_ready"], u + 1)
                nc.scalar.activation(TB[:, :], SQ[:, :, :].rearrange("p s i -> p (s i)"), ACT.Tanh,
                                     scale=0.5).then_inc(sig["sq_t"], 1)
                act.wait_ge(sig["co_ready"], u + 1)
                apart(act)
                nc.scalar.activation(XP[0:NS, :, bass.ds(u * STEPS, STEPS)],
                                     PB[7][0:NS, :].rearrange("i (t b) -> i b t", b=B), ACT.Copy).then_inc(sig["co_copied"], 1)
            act.wait_ge(sig["co_copied"], 1 + UNITS)
            with act.Fori(0, UNITS) as u:
                act.wait_ge(sig["o_y"], 1 + u)
                apart(act)
                nc.scalar.activation(two(SC[0:NS, 0:TOK]), XP[0:NS, bass.ds(u * UB, UB), :], ACT.Copy).then_inc(sig["o_st"], 1)

        def pair_bank(g):
            return PB[3 + g % 2][:, 0:2 * CELL].rearrange("p (s c) -> p s c", c=CELL)

        def cell_pe(pe):
            def scores(u, c, j):
                b, g = c // 4, c % 4
                q0, q1 = 32 * g, 32 * g + 32
                if c >= 1:
                    pe.wait_ge(sig["f_e"], u * 24 + 3 * (c - 1) + j + 1)
                if j == 0:
                    nc.tensor.matmul(PB[0][:, :].rearrange("p (h k) -> p h k", h=4), NEG[:, 0:P],
                                     NEG[:, 2 * P:3 * P].unsqueeze(1).to_broadcast([P, 4, P]), start=True, stop=False)
                    for h in range(4):
                        last = nc.tensor.matmul(PB[0][:, h * P:(h + 1) * P], QM[q0:q1, h, b * T:b * T + P],
                                                KT[q0:q1, b * T:b * T + P], start=False, stop=(h == 3), tile_position=(q0, 0))
                else:
                    nc.tensor.matmul(PB[j][:, :].rearrange("p (h k) -> p h k", h=2), NEG[:, 0:P],
                                     NEG[:, P:3 * P].unsqueeze(1).to_broadcast([P, 2, 2 * P]), start=True, stop=False)
                    for n in range(2):
                        h = 2 * j - 2 + n
                        last = nc.tensor.matmul(PB[j][:, n * T:(n + 1) * T], QM[q0:q1, h, b * T + P:b * T + 2 * P],
                                                KT[q0:q1, b * T:b * T + T], start=False, stop=(n == 1), tile_position=(q0, 0))
                last.then_inc(sig["f_s"], 1)

            def transposes(u, c, j):
                pe.wait_ge(sig["f_e"], u * 24 + 3 * c + j + 1)
                if j == 2:
                    pe.wait_ge(sig["f_pc"], 1 + u * 24 + 3 * c + 1)
                elif c >= 1:
                    pe.wait_ge(sig["f_pc"], 1 + u * 24 + 3 * c)
                for k in range(4):
                    last = nc.tensor.transpose(PB[3 + j % 2][:, k * P:(k + 1) * P], PEX[:, j, k * P:(k + 1) * P], ident)
                last.then_inc(sig["f_t"], 1)

            def values(u, c):
                b, g = c // 4, c % 4
                if c % 4 == 0:
                    pe.wait_ge(sig["f_y"], 1 + u * UB + b)
                pe.wait_ge(sig["f_pc"], 1 + u * 24 + 3 * c + 3)
                for h in range(4):
                    o = (4 * g + h) * HD
                    nc.tensor.matmul(PB[5][:, o:o + HD], PTS[:, 0, h * P:(h + 1) * P], VT[:, 2 * b, o:o + HD],
                                     start=True, stop=True)
                    for kt in range(2):
                        col = (h % 2) * T + kt * P
                        last = nc.tensor.matmul(PB[5][:, P + o:P + o + HD], PTS[:, 1 + h // 2, col:col + P],
                                                VT[:, 2 * b + kt, o:o + HD], start=(kt == 0), stop=(kt == 1))
                last.then_inc(sig["f_pv"], 1)

            def transpose_attention(u, b):
                pe.wait_ge(sig["f_y"], 1 + u * UB + b + 1)
                if b == 1:
                    pe.wait_ge(sig["f_x2"], 1 + u * UB + 1)
                for qt in range(2):
                    last = nc.tensor.transpose(PB[6][:, qt * P:(qt + 1) * P], Y[:, qt, :], ident)
                last.then_inc(sig["f_yt"], 1)

            def project_attention(u, b):
                pe.wait_ge(sig["f_yc"], u * UB + b + 1)
                for qt in range(2):
                    last = nc.tensor.matmul(PB[6][:, (2 + qt) * P:(3 + qt) * P], YT[:, qt * P:(qt + 1) * P], WPR[:, :],
                                            start=True, stop=True)
                last.then_inc(sig["f_pj"], 1)

            def project_cell(u, pairs):
                for g in pairs:
                    if g >= 2:
                        pe.wait_ge(sig["p_copied"], u * (STEPS // 2) + g - 1)
                    for k in range(2):
                        for n in range(NB):
                            last = nc.tensor.matmul(pair_bank(g)[32 * n:32 * n + 32, k, :],
                                                    CU[:, 2 * g + k, :],
                                                    WC[:, n, :], start=True, stop=True, tile_position=(0, 32 * n))
                    last.then_inc(sig["p_proj"], 1)

            def sum_products(u, k):
                pe.wait_ge(sig["sq_product"], u * STEPS + k + 1)
                if k % 2 == 0 and k > 0:
                    pe.wait_ge(sig["sq_reduced"], u * (STEPS // 2 - 1) + k // 2)
                if k == 0:
                    pe.wait_ge(sig["co_copied"], 1 + u)
                pq = v3(PQ)
                for m in range(NS // 4):
                    last = nc.tensor.matmul(PB[7][:, (k % 2) * P:(k % 2 + 1) * P].rearrange("p (i l) -> p i l", l=4),
                                            ident, pq[:, :, 4 * m:4 * m + 4], start=(m == 0), stop=(m == NS // 4 - 1))
                last.then_inc(sig["sq_summed"], 1)

            def hidden(u, e):
                for c in range(H1C):
                    k = e * H1C + c
                    if e >= 2:
                        pe.wait_ge(sig["m_h"], u * (E * H1C) + k - 2 * H1C + 1)
                    nc.tensor.matmul(PB[2 * (e % 2) + c][:, :], W1[:, k * P:(k + 1) * P], XA, start=True,
                                     stop=True).then_inc(sig["m_hp"], 1)

            def expert_out(u, e):
                pe.wait_ge(sig["m_h"], u * (E * H1C) + (e + 1) * H1C)
                if e >= 2:
                    pe.wait_ge(sig["m_acc"], 1 + u * E + e - 1)
                yb = PB[4 + e % 2]
                for i in range(TILES):
                    for c in range(H1C):
                        last = nc.tensor.matmul(yb[:, i * P:(i + 1) * P],
                                                HT[:, e % 2, c * TOK + i * P:c * TOK + (i + 1) * P],
                                                W2[:, e * H1C + c, :], start=(c == 0), stop=(c == H1C - 1))
                last.then_inc(sig["m_y"], 1)

            pe.wait_ge(sig["c_xp"], 1 + UNITS)
            pe.wait_ge(late_loaded, 16 * 12)
            pe.wait_ge(sig["scaled"], 1)
            pe.wait_ge(sig["f_cu"], 1)
            project_cell(0, range(STEPS // 2))
            with pe.Fori(0, UNITS) as u:
                pe.wait_ge(sig["f_xn"], u + 1)
                for i in range(TILES):
                    last = nc.tensor.transpose(PB[6][:, i * P:(i + 1) * P], XNT[:, i, :], ident)
                last.then_inc(sig["f_tr"], 1)
                pe.wait_ge(sig["f_xa"], u + 1)
                nc.tensor.matmul(PB[0][:, :], WQKV[:, 0:D], XA, start=True, stop=True).then_inc(sig["f_q"], 1)
                nc.tensor.matmul(PB[1][:, :], WQKV[:, D:2 * D], XA, start=True, stop=True).then_inc(sig["f_k"], 1)
                for i in range(TILES):
                    last = nc.tensor.matmul(PB[2][:, i * P:(i + 1) * P], XA[:, i * P:(i + 1) * P], WQKV[:, 2 * D:3 * D],
                                            start=True, stop=True)
                last.then_inc(sig["f_v"], 1)
                pe.wait_ge(sig["f_vt"], u + 1)
                for j in range(3):
                    scores(u, 0, j)
                for c in range(8):
                    if c == 5:
                        project_attention(u, 0)
                    for j in range(3):
                        if j == 2:
                            sum_products(u, c)
                        transposes(u, c, j)
                        if c < 7:
                            scores(u, c + 1, j)
                    if c == 4:
                        transpose_attention(u, 0)
                    values(u, c)
                pe.wait_ge(sig["f_cu"], u + 2)
                pe.wait_ge(sig["f_pc"], 1 + (u + 1) * 24)
                project_cell(u + 1, (0, 1))
                transpose_attention(u, 1)
                project_cell(u + 1, (2,))
                project_attention(u, 1)
                project_cell(u + 1, (3,))
                sum_products(u, 8)
                project_cell(u + 1, (4, 5, 6, 7))
                pe.wait_ge(sig["h_xn"], u + 1)
                for i in range(TILES):
                    last = nc.tensor.transpose(PB[6][:, i * P:(i + 1) * P], XNT[:, i, :], ident)
                last.then_inc(sig["h_tr"], 1)
                pe.wait_ge(sig["h_xm"], u + 1)
                for i in range(TILES):
                    last = nc.tensor.matmul(PB[6][:, i * E:(i + 1) * E], XA[:, i * P:(i + 1) * P], WR1[:, :],
                                            start=True, stop=True)
                last.then_inc(sig["h_lg"], 1)
                hidden(u, 0)
                sum_products(u, 9)
                pe.wait_ge(sig["p_copied"], (u + 2) * (STEPS // 2))
                hidden(u, 1)
                for st in range(11, 15):
                    e = 2 * (st - 11)
                    expert_out(u, e)
                    if e + 2 < E:
                        hidden(u, e + 2)
                    sum_products(u, st - 1)
                    expert_out(u, e + 1)
                    if e + 3 < E:
                        hidden(u, e + 3)
                sum_products(u, 14)
                sum_products(u, 15)
                pe.wait_ge(sig["bo_ready"], u + 1)
                for t in range(STEPS):
                    last = nc.tensor.matmul(PB[7][0:NS, t * B:(t + 1) * B], TB[:, t * NS:(t + 1) * NS],
                                            CST[:, C_SEL:C_SEL + NS], start=True, stop=True)
                last.then_inc(sig["co_ready"], 1)
            pe.wait_ge(sig["co_copied"], 1 + UNITS)
            with pe.Fori(0, UNITS) as u:
                pe.wait_ge(sig["o_st"], u + 1)
                pe.wait_ge(sig["o_x"], 1 + u)
                for i in range(TILES):
                    last = nc.tensor.matmul(PB[0][:, i * P:(i + 1) * P], SC[0:NS, i * P:(i + 1) * P],
                                            WOUT[:, :], start=True, stop=True)
                last.then_inc(sig["o_y"], 1)

        def cell_dve(dve, start):
            V = nc.vector
            ch = Chain(dve, dve_chain, start)
            dve.wait_ge(late_loaded, 16 * 12)
            for w, c in ((WQKV[:, :], LN1_W), (WR1[:, :], LN2_W), (W1[:, 0:E * H1C * P], LN2_W)):
                ch.done(V.tensor_scalar(w, w, vec(c), None, ALU.mult))
            dve.wait_ge(sig["g_rstd"], 1)
            V.memset(St, 0.0).then_inc(sig["scaled"], 1)
            dve.wait_ge(sig["scaled"], 1)
            start += ch.n

            def prep(u, ch):
                kq = lambda c: RAW[:, :, c * NS:(c + 1) * NS]
                b16 = lambda ap: ap.unsqueeze(2).to_broadcast([P, STEPS, NS])
                b4 = lambda ap: ap.unsqueeze(2).to_broadcast([P, STEPS, NB])
                logits = RAW[:, :, 4 * NS:CELL]
                t3 = lambda k: BS[:, k * 512:(k + 1) * 512].rearrange("p (s j) -> p s j", j=NS)
                tile = lambda i: tilef(XN, u, i)
                probs, rank = SM64[:, 1, :, :], SM64[:, 3, :, :]
                dve.wait_ge(sig["p_copied"], (u + 1) * (STEPS // 2))
                m = ch.mark(V.tensor_tensor(KN, kq(0), kq(0), ALU.mult))
                V.tensor_tensor(t3(0), kq(2), CST[:, C_BB:C_BB + NS].unsqueeze(1).to_broadcast([P, STEPS, NS]),
                                ALU.add).then_inc(sig["p_b"], 1)
                n = ch.mark(V.tensor_reduce(SM16[:, 2, :], logits, AX, ALU.max))
                ch.reach(m)
                V.tensor_reduce(SM16[:, 0, :], KN, AX, ALU.add).then_inc(sig["p_ss"], 1)
                ch.reach(n)
                V.tensor_tensor(SM64[:, 0, :, :], logits, b4(SM16[:, 2, :]), ALU.subtract).then_inc(sig["p_lc"], 1)
                apart(dve)
                for i in range(TILES):
                    m = ch.mark(V.bn_stats(BNS[:, i, :], tile(i)))
                other = logits.unsqueeze(2).to_broadcast([P, STEPS, NB, NB])
                own = logits.unsqueeze(3).to_broadcast([P, STEPS, NB, NB])
                larger, equal = (CMP[:, k, :].rearrange("p (n e f) -> p n e f", n=STEPS, e=NB) for k in range(2))
                low = CST[:, C_LT4:C_LT4 + NB * NB].unsqueeze(1).to_broadcast([P, STEPS, NB * NB])
                eqf = CMP[:, 1, :].rearrange("p (n e) -> p n e", n=STEPS)
                n = ch.mark(V.tensor_tensor(equal, other, own, ALU.is_equal))
                ch.reach(m)
                apart(dve)
                for i in range(TILES):
                    m = ch.mark(V.bn_aggr(MV[:, i, :], BNS[:, i, :]))
                ch.done(V.tensor_tensor(larger, other, own, ALU.is_gt))
                ch.reach(m)
                V.tensor_scalar(VE[:, :], MV[:, :, 1], LN_EPS, None, ALU.add).then_inc(sig["f_var"], 1)
                ch.reach(n)
                n = ch.mark(V.tensor_tensor(eqf, eqf, low, ALU.mult))
                dve.wait_ge(sig["p_le"], u + 1)
                m = ch.mark(V.tensor_reduce(SM16[:, 2, :], probs, AX, ALU.add))
                ch.reach(n)
                n = ch.mark(V.tensor_tensor(CMP[:, 0, :], CMP[:, 0, :], CMP[:, 1, :], ALU.add))
                ch.reach(m)
                m = ch.mark(V.reciprocal(SM16[:, 2, :], SM16[:, 2, :]))
                ch.reach(n)
                ch.done(V.tensor_reduce(rank, larger, AX, ALU.add))
                ch.reach(m)
                m = ch.mark(V.tensor_tensor(probs, probs, b4(SM16[:, 2, :]), ALU.mult))
                dve.wait_ge(sig["f_rstd"], u + 1)

                def apply(i):
                    return V.tensor_scalar(XNT[:, i, :], tile(i), MV[:, i, 0:1], RSTD[:, i:i + 1],
                                           ALU.subtract, ALU.mult)
                apply(0)
                ch.reach(m)
                m = ch.mark(V.scalar_tensor_tensor(rank, rank, 2.0, probs, ALU.is_lt, ALU.mult))
                apply(1)
                ch.reach(m)
                m = ch.mark(V.tensor_reduce(SM16[:, 3, :], rank, AX, ALU.add))
                apply(2)
                apply(3).then_inc(sig["f_xn"], 1)
                ch.reach(m)
                m = ch.mark(V.tensor_scalar(SM16[:, 3, :], SM16[:, 3, :], 1e-8, None, ALU.add))
                dve.wait_ge(sig["p_norm"], u + 1)
                n = ch.mark(V.tensor_scalar(SM16[:, 1, :], SM16[:, 1, :], 1e-6, None, ALU.add))
                ch.reach(m)
                m = ch.mark(V.reciprocal(SM16[:, 3, :], SM16[:, 3, :]))
                ch.reach(n)
                n = ch.mark(V.reciprocal(SM16[:, 1, :], SM16[:, 1, :]))
                ch.reach(m)
                m = ch.mark(V.tensor_tensor(rank, rank, b4(SM16[:, 3, :]), ALU.mult))
                ch.reach(n)
                ch.done(V.tensor_tensor(KN, kq(0), b16(SM16[:, 1, :]), ALU.mult))
                hot = CST[:, C_HOT:C_HOT + NB].unsqueeze(1).to_broadcast([P, STEPS, NB])
                ch.reach(m)
                m = ch.mark(V.tensor_tensor(rank, rank, hot, ALU.mult))
                n = ch.mark(V.tensor_tensor(probs, probs, hot, ALU.mult))
                ch.reach(m)
                m = ch.mark(V.tensor_reduce(SM16[:, 4, :], rank, AX, ALU.add))
                ch.reach(n)
                n = ch.mark(V.tensor_reduce(SM16[:, 5, :], probs, AX, ALU.add))
                ch.reach(m)
                ch.done(V.tensor_scalar(SM16[:, 6, :], SM16[:, 4, :], -1.0, 1.0, ALU.mult, ALU.add))
                ch.reach(n)
                ch.done(V.tensor_scalar(SM16[:, 7, :], SM16[:, 5, :], 0.5, None, ALU.mult))
                dve.wait_ge(sig["p_bt"], u + 1)
                V.tensor_scalar(BT, t3(1), 0.5, 0.5, ALU.mult, ALU.add).then_inc(sig["prep_done"], 1)

            def products(u, k):
                dve.wait_ge(sig["sq_summed"], 1 + u * STEPS + k)
                V.tensor_tensor(v3(PQ), v3(St), bi(QQ[:, k, :]), ALU.mult).then_inc(sig["sq_product"], 1)

            def reduce_pair(u, k):
                dve.wait_ge(sig["sq_summed"], 1 + u * STEPS + k + 1)
                return V.tensor_reduce(SQ[:, k - 1:k + 1, :].rearrange("p s i -> p (s i)"),
                                       PB[7][:, 0:2 * P].rearrange("p (n l) -> p n l", l=4), AX, ALU.add)

            def scan_step(u, ch, st, beside):
                beside(0)
                if st >= 1:
                    ch.reach(ch.updated)
                else:
                    dve.wait_ge(sig["prep_done"], u + 1)
                m = ch.mark(V.tensor_tensor(v3(PRD), v3(St), bi(KN[:, st, :]), ALU.mult))
                ch.done(V.tensor_tensor(v3(BS), v3(St), bj(BT[:, st, :]), ALU.mult))
                ch.reach(m)
                m = ch.mark(V.tensor_reduce(RET[:, 0, :], v3(PRD), AX, ALU.add))
                beside(1)
                if st == 0:
                    dve.wait_ge(sig["vq_copied"], u + 1)
                ch.reach(m)
                m = ch.mark(V.tensor_tensor(RET[:, 1, :], VV[:, st, :], RET[:, 0, :], ALU.subtract))
                beside(2)
                ch.reach(m)
                m = ch.mark(V.tensor_tensor(v3(ZB), bj(RET[:, 1, :]), bi(KN[:, st, :]), ALU.mult))
                beside(3)
                ch.reach(m)
                V.tensor_tensor(ZB, ZB, BS, ALU.add).then_inc(sig["z_ready"], 1)
                if st >= 1:
                    products(u, st - 1)
                beside(4)
                dve.wait_ge(sig["w_ready"], u * STEPS + st + 1)
                ch.updated = ch.mark(V.scalar_tensor_tensor(St, St, SM16[:, 6, st:st + 1], TH, ALU.mult, ALU.add))

            def maxima(u, c, j):
                dve.wait_ge(sig["f_s"], u * 24 + 3 * c + j + 1)
                n = 4 if j == 0 else 2
                V.tensor_reduce(NM[:, j, 0:n], PB[j][:, :].rearrange("p (h k) -> p h k", h=n), AX, ALU.max,
                                negate=True).then_inc(sig["f_m"], 1)

            def row_sums(u, ch, b):
                dve.wait_ge(sig["f_pv"], 1 + u * 8 + 4 * (b + 1))
                return ch.mark(V.reciprocal(RI[:, :, :], RS[:, b, :, :]))

            def attention_out(u, ch, m):
                ch.reach(m)
                V.tensor_tensor(Y[:, :, :].rearrange("p q (h d) -> p (q h) d", d=HD),
                                PB[5][:, 0:2 * P].rearrange("p (q d) -> p q d", d=HD),
                                RI[:, :, :].rearrange("p q h -> p (q h)").unsqueeze(2).to_broadcast([P, 2 * NH, HD]),
                                ALU.mult).then_inc(sig["f_y"], 1)

            def residual(u, b):
                dve.wait_ge(sig["f_pj"], u * UB + b + 1)
                x = XN[:, bass.ds(u * TILES + 2 * b, 2), :]
                V.tensor_tensor(x, x, PB[6][:, 2 * P:4 * P].rearrange("p (n d) -> p n d", d=D), ALU.add).then_inc(sig["f_x2"], 1)

            def add_expert(u, e, tiles):
                dve.wait_ge(sig["m_y"], u * E + e + 1)
                if e >= 1 and tiles[0] == 0:
                    dve.wait_ge(sig["m_acc"], 1 + u * E + e)
                for i in tiles:
                    x = tilef(XN, u, i)
                    last = V.scalar_tensor_tensor(x, PB[4 + e % 2][:, i * P:(i + 1) * P], GATE[:, i, e:e + 1], x,
                                                  ALU.mult, ALU.add)
                if tiles[-1] == TILES - 1:
                    last.then_inc(sig["m_acc"], 1)

            def beside_step(u, ch, st):
                lg = PB[6][:, 0:TILES * E].rearrange("p (n e) -> p n e", e=E)
                other = LG[:, :, :].unsqueeze(2).to_broadcast([P, TILES, E, E])
                own = LG[:, :, :].unsqueeze(3).to_broadcast([P, TILES, E, E])
                larger, equal = (CMP[:, k, :].rearrange("p (n e f) -> p n e f", n=TILES, e=E) for k in range(2))

                def work(slot):
                    if 1 <= st <= 8 and slot <= 2:
                        maxima(u, st - 1, slot)
                    if st >= 3 and st % 2 == 1 and slot == 3:
                        reduce_pair(u, st - 2).then_inc(sig["sq_reduced"], 1)
                    if (st, slot) == (5, 4):
                        attention_out(u, ch, row_sums(u, ch, 0))
                    if (st, slot) == (7, 4):
                        residual(u, 0)
                    if (st, slot) == (9, 0):
                        ch.row_sums = row_sums(u, ch, 1)
                    if (st, slot) == (9, 1):
                        attention_out(u, ch, ch.row_sums)
                    if (st, slot) == (9, 4):
                        residual(u, 1)
                        dve.wait_ge(sig["f_x2"], 1 + u * UB + 2)
                        norm_stats(dve, ch, lambda i: tilef(XN, u, i), sig["h_var"])
                    if st == 10 and slot <= 3:
                        if slot == 0:
                            dve.wait_ge(sig["h_rstd"], u + 1)
                        last = V.tensor_scalar(XNT[:, slot, :], tilef(XN, u, slot), MV[:, slot, 0:1],
                                               RSTD[:, slot:slot + 1], ALU.subtract, ALU.mult)
                        if slot == 3:
                            last.then_inc(sig["h_xn"], 1)
                    if (st, slot) == (10, 4):
                        dve.wait_ge(sig["h_lg"], u + 1)
                        ch.then(V.tensor_copy(LG[:, :, :], lg))
                        ch.then(V.tensor_reduce(MX[:, :], LG[:, :, :], AX, ALU.max))
                        V.tensor_tensor(LC[:, :, :], LG[:, :, :], MX[:, :].unsqueeze(2).to_broadcast([P, TILES, E]),
                                        ALU.subtract).then_inc(sig["h_c"], 1)
                    if (st, slot) == (11, 0):
                        ch.equal = ch.mark(V.tensor_tensor(equal, other, own, ALU.is_equal))
                        ch.done(V.tensor_tensor(larger, other, own, ALU.is_gt))
                    if (st, slot) == (11, 1):
                        ch.reach(ch.equal)
                        eqf = CMP[:, 1, :].rearrange("p (n e) -> p n e", n=TILES)
                        low = CST[:, C_LT8:C_LT8 + E * E].unsqueeze(1).to_broadcast([P, TILES, E * E])
                        ch.equal = ch.mark(V.tensor_tensor(eqf, eqf, low, ALU.mult))
                    if (st, slot) == (11, 2):
                        ch.reach(ch.equal)
                        ch.equal = ch.mark(V.tensor_tensor(CMP[:, 0, :], CMP[:, 0, :], CMP[:, 1, :], ALU.add))
                    if (st, slot) == (11, 3):
                        ch.reach(ch.equal)
                        ch.done(V.tensor_reduce(RK[:, :, :], larger, AX, ALU.add))
                    if (st, slot) == (11, 4):
                        ch.settle()
                        top_two(dve, ch, sig["h_ex"], u + 1, sig["h_gate"])
                    if st >= 12:
                        if (st, slot) == (12, 0):
                            dve.wait_ge(sig["h_gate"], u + 1)
                        e = 2 * (st - 12)
                        if slot < 4:
                            add_expert(u, e, (slot,))
                        else:
                            add_expert(u, e + 1, range(TILES))
                return work

            with dve.Fori(0, UNITS) as u:
                ch = Chain(dve, dve_chain, start + u * PER_CELL)
                prep(u, ch)
                for st in range(STEPS):
                    scan_step(u, ch, st, beside_step(u, ch, st))
                ch.reach(ch.updated)
                products(u, STEPS - 1)
                dve.wait_ge(sig["m_acc"], 1 + u * E + E)
                xs = X[:, bass.ds(u * TILES, TILES), :]
                ch.done(V.tensor_tensor(xs, xs, XN[:, bass.ds(u * TILES, TILES), :], ALU.add))
                reduce_pair(u, STEPS - 1).then_inc(sig["sq_ready"], 1)
                dve.wait_ge(sig["sq_ready"], u + 1)
                sqf = SQ[:, :, :].rearrange("p s i -> p (s i)")
                dve.wait_ge(sig["sq_t"], u + 1)
                ch.then(V.scalar_tensor_tensor(TB[:, :], TB[:, :], 1.0, sqf, ALU.add, ALU.mult))
                ch.then(V.tensor_tensor(TB[:, :], TB[:, :], sqf, ALU.mult))
                tb = TB[:, :].rearrange("p (s j) -> p s j", j=NS)
                V.tensor_tensor(tb, tb, SM16[:, 7, :].unsqueeze(2).to_broadcast([P, STEPS, NS]), ALU.mult)\
                    .then_inc(sig["bo_ready"], 1)
                dve.wait_ge(sig["bo_ready"], u + 1)
                assert ch.n == PER_CELL, ch.n
            with dve.Fori(0, UNITS) as u:
                dve.wait_ge(sig["o_y"], 1 + u + 1)
                xs = X[:, bass.ds(u * TILES, TILES), :]
                V.tensor_tensor(xs, xs, PB[0][:, :].rearrange("p (n d) -> p n d", d=D), ALU.add).then_inc(sig["o_x"], 1)


        @block.sync
        def _(sp):
            sp.dma_start(WA[:, :, :], A["WA"]).then_inc(loaded, 16)
            sp.dma_start(VEC[:, :], A["VEC"]).then_inc(loaded, 16)
            sp.dma_start(CST[:, :], A["CST"]).then_inc(loaded, 16)
            sp.dma_start(WR0[:, :], A["WR0"]).then_inc(loaded, 16)
            xs = A["x"].rearrange("(n p) d -> p n d", p=P)
            sp.dma_start(X[:, :, :], xs).then_inc(loaded, 16)
            for dst, name in ((W2[:, :, :], "W2"), (B2[:, :], "B2"), (NEG[:, :], "NEG"), (WIN[:, :], "WIN"),
                              (WC[:, :, :], "WC"), (WOUT[:, :], "WOUT"), (WQKV[:, :], "WQKV"), (WPR[:, :], "WPR"),
                              (WR1[:, :], "WR1")):
                sp.dma_start(dst, A[name]).then_inc(late_loaded, 16)
            sp.wait_ge(sig["g_rstd"], 1)
            sp.wait_ge(sig["weights_used"], 1)
            sp.dma_start(W1[:, :], A["W1"]).then_inc(late_loaded, 16)
            sp.wait_ge(sig["b_acc"], 1 + UNITS * E)
            sp.dma_start(W1[:, 0:E * H1C * P], A["W1b"]).then_inc(late_loaded, 16)
            sp.dma_start(W2[:, 0:E * H1C, :], A["W2b"]).then_inc(late_loaded, 16)
            cell_sync(sp)

        @block.gpsimd
        def _(pool):
            pool.wait_ge(loaded, 16 * n_early)
            with pool.Fori(0, UNITS) as u:
                pool.wait_ge(sig["a_var"], u + 1)
                rstd_pow(RSTD[:, :], VE[:, :], TILES, sig["a_rstd"])
            pool.wait_ge(sig["g_ve"], 1)
            nc.gpsimd.tensor_tensor(GMS[:, 4, :], GMS[:, 3, :], NSC[:, 1, :], ALU.pow).then_inc(sig["g_rstd"], 1)
            with pool.Fori(0, UNITS) as u:
                pool.wait_ge(sig["c_var"], u + 1)
                rstd_pow(RSTD[:, :], VE[:, :], TILES, sig["c_rstd"])
            cell_pool(pool)

        @block.scalar
        def _(act):
            prime(act, (sig["a_xt"], sig["a_er"], sig["b_h"], sig["f_pc"], sig["c_xt"], sig["c_xp"], sig["co_copied"]))
            act.wait_ge(loaded, 16 * n_early)
            nc.scalar.activation(DW[:, 0:1], vec(DECAY), ACT.Exp).then_inc(sig["decay_exp"], 1)
            with act.Fori(0, UNITS) as u:
                act.wait_ge(sig["a_tr"], 1 + u + 1)
                apart(act)
                nc.scalar.activation(XT[:, bass.ds(u * UB, UB), 1:T + 1],
                                     two(PB[0][:, :]), ACT.Copy).then_inc(sig["a_xt"], 1)
                act.wait_ge(sig["a_r"], u + 1)
                act.wait_ge(sig["a_done"], 1 + u)
                nc.scalar.activation(ER, PB[1][:, :], ACT.Exp, scale=-1.0).then_inc(sig["a_er"], 1)
                act.wait_ge(sig["a_d"], u + 1)
                nc.scalar.activation(SC[:, 1024:2048], SC[:, 0:1024], ACT.Exp).then_inc(sig["a_e"], 1)
                act.wait_ge(sig["a_s"], u + 1)
                nc.scalar.activation(L1, Sx, ACT.Ln, bias=CST[:, C_EPS:C_EPS + 1]).then_inc(sig["a_l"], 1)
                act.wait_ge(sig["a_f"], u + 1)
                nc.scalar.activation(HT[:, 1, :], HT[:, 0, :], ACT.Exp).then_inc(sig["a_g"], 1)
            with act.Fori(0, UNITS) as u:
                act.wait_ge(sig["b_y"], 1 + u * E)
                apart(act)
                nc.scalar.activation(two(XU), XT[:, bass.ds(u * UB, UB), 1:T + 1], ACT.Copy).then_inc(sig["b_xu"], 1)
                act.wait_ge(sig["b_c"], u + 1)
                nc.scalar.activation(EX[:, :, :], LC[:, :, :], ACT.Exp).then_inc(sig["b_ex"], 1)
                act.wait_ge(sig["b_gt"], u + 1)
                nc.scalar.activation(GT[:, :], PB[6][0:E, :], ACT.Copy).then_inc(sig["b_gtc"], 1)
                for e in range(E):
                    if e >= 2:
                        act.wait_ge(sig["b_y"], 1 + u * E + e - 1)
                    for c in range(H0C):
                        k = e * H0C + c
                        act.wait_ge(sig["b_hp"], u * (E * H0C) + k + 1)
                        nc.scalar.activation(HT[:, e % 2, c * TOK:(c + 1) * TOK], PB[c][:, :], ACT.Relu,
                                             bias=CST[:, C_B1 + k:C_B1 + k + 1]).then_inc(sig["b_h"], 1)
            with act.Fori(0, UNITS) as u:
                act.wait_ge(sig["c_tr"], 1 + u + 1)
                act.wait_ge(sig["c_in"], 1 + u)
                nc.scalar.activation(HT[:, 0, 0:TOK], PB[0][:, :], ACT.Copy).then_inc(sig["c_xt"], 1)
                act.wait_ge(sig["c_in"], 1 + u + 1)
                apart(act)
                nc.scalar.activation(XP[:, bass.ds(u * UB, UB), :], two(PB[1][:, :]), ACT.Silu).then_inc(sig["c_xp"], 1)
            cell_act(act)

        @block.tensor
        def _(pe):
            prime(pe, (sig["a_tr"], sig["b_at"], sig["b_y"], sig["c_in"], sig["c_tr"], sig["f_pv"], sig["sq_summed"], sig["o_y"]))
            pe.wait_ge(loaded, 16 * n_early)
            pe.wait_ge(prepared, 1)
            with pe.Fori(0, UNITS) as u:
                pe.wait_ge(sig["a_xn"], u + 1)
                pe.wait_ge(sig["a_xt"], 1 + u)
                for i in range(TILES):
                    last = nc.tensor.transpose(PB[0][:, i * P:(i + 1) * P], XNa[:, i, :], ident)
                last.then_inc(sig["a_tr"], 1)
                pe.wait_ge(sig["a_xt"], 1 + u + 1)
                pe.wait_ge(sig["a_done"], 1 + u)
                pe.wait_ge(sig["a_er"], 1 + u)
                for m, (bank, signal) in enumerate(((1, sig["a_r"]), (2, None), (3, sig["a_kv"]))):
                    nc.tensor.matmul(two(PB[bank][:, :]), WM[:, 0, m, :], XT[:, bass.ds(u * UB, UB), 1:T + 1],
                                     start=True, stop=False)
                    last = nc.tensor.matmul(two(PB[bank][:, :]), WM[:, 1, m, :], XT[:, bass.ds(u * UB, UB), 0:T],
                                            start=False, stop=True)
                    if signal is not None:
                        last.then_inc(signal, 1)
            pe.wait_ge(sig["a_done"], 1 + UNITS)
            nc.tensor.matmul(PB[0][:, 0:B], CST[:, C_GROUP:C_GROUP + P], MVR[:, :, 0], start=True,
                             stop=True).then_inc(sig["g_mean"], 1)
            pe.wait_ge(sig["g_dev"], 1)
            nc.tensor.matmul(PB[1][:, 0:B], CST[:, C_GROUP:C_GROUP + P], GMS[:, 2, :], start=True,
                             stop=True).then_inc(sig["g_var"], 1)
            pe.wait_ge(late_loaded, 16 * 10)
            with pe.Fori(0, UNITS) as u:
                pe.wait_ge(sig["b_xu"], u + 1)
                for i in range(TILES):
                    last = nc.tensor.matmul(PB[7][:, i * E:(i + 1) * E], XU[:, i * P:(i + 1) * P], WR0[:, :],
                                            start=True, stop=True)
                last.then_inc(sig["b_lg"], 1)

                def hidden(e):
                    for c in range(H0C):
                        k = e * H0C + c
                        if e >= 1:
                            pe.wait_ge(sig["b_h"], 1 + u * (E * H0C) + k - H0C + 1)
                        else:
                            pe.wait_ge(sig["b_h"], 1 + u * (E * H0C))
                        nc.tensor.matmul(PB[c][:, :], W1[:, k * P:(k + 1) * P], XU, start=True,
                                         stop=True).then_inc(sig["b_hp"], 1)

                pe.wait_ge(sig["b_gate"], u + 1)
                pe.wait_ge(sig["b_acc"], 1 + u * E)
                for i in range(TILES):
                    last = nc.tensor.transpose(PB[6][0:E, i * P:(i + 1) * P], GATE[:, i, :], ident)
                last.then_inc(sig["b_gt"], 1)
                hidden(0)
                pe.wait_ge(sig["b_n"], u + 1)
                pe.wait_ge(sig["b_gtc"], u + 1)
                pe.wait_ge(sig["b_x"], 1 + u)
                for i in range(TILES):
                    o = PB[5][:, i * P:(i + 1) * P]
                    nc.tensor.matmul(o, RN[:, i * P:(i + 1) * P],
                                     WA[:, 3, :], start=True, stop=False)
                    last = nc.tensor.matmul(o, GT[:, i * P:(i + 1) * P], B2[:, :], start=False, stop=True)
                last.then_inc(sig["b_at"], 1)
                for e in range(E):
                    if e + 1 < E:
                        hidden(e + 1)
                    pe.wait_ge(sig["b_h"], 1 + u * (E * H0C) + (e + 1) * H0C)
                    if e >= 2:
                        pe.wait_ge(sig["b_acc"], 1 + u * E + e - 1)
                    yb = PB[4 if e % 2 == 0 else 6]
                    for i in range(TILES):
                        for c in range(H0C):
                            last = nc.tensor.matmul(yb[:, i * P:(i + 1) * P],
                                                    HT[:, e % 2, c * TOK + i * P:c * TOK + (i + 1) * P],
                                                    W2[:, e * H0C + c, :], start=(c == 0), stop=(c == H0C - 1))
                    last.then_inc(sig["b_y"], 1)
            with pe.Fori(0, UNITS) as u:
                pe.wait_ge(sig["c_xn"], u + 1)
                pe.wait_ge(sig["c_xt"], 1 + u)
                for i in range(TILES):
                    last = nc.tensor.transpose(PB[0][:, i * P:(i + 1) * P], XNT[:, i, :], ident)
                last.then_inc(sig["c_tr"], 1)
                pe.wait_ge(sig["c_xt"], 1 + u + 1)
                pe.wait_ge(sig["c_xp"], 1 + u)
                nc.tensor.matmul(PB[1][:, :], WIN[:, :], HT[:, 0, 0:TOK], start=True, stop=True).then_inc(sig["c_in"], 1)
            cell_pe(pe)

        @block.vector
        def _(dve):
            prime(dve, (sig["a_done"], sig["b_acc"], sig["b_x"], sig["f_y"], sig["m_acc"], sig["o_x"], sig["f_x2"]))
            V = nc.vector
            dve.wait_ge(loaded, 16 * n_early)
            ch = Chain(dve, dve_chain)
            ch.done(V.memset(XT[:, :, 0:1], 0.0))
            ch.done(V.memset(Dx[:, 0, :, 0:1], LOW))
            ch.done(V.memset(Bx[:, :, 0:1], LOW))
            ch.done(V.memset(Ax[:, 0:1], 0.0))
            for m in range(3):
                ch.done(V.tensor_scalar(WM[:, 0, m, :], WA[:, m, :], vec(MIX_R + m), None, ALU.mult))
            ch.then(V.tensor_scalar(NSC[:, 0, 0:3], VEC[:, 0:3], -1.0, 1.0, ALU.mult, ALU.add))
            for m in range(3):
                ch.done(V.tensor_scalar(WM[:, 1, m, :], WA[:, m, :], NSC[:, 0, m:m + 1], None, ALU.mult))
            dve.wait_ge(sig["decay_exp"], 1)
            ch.then(V.tensor_scalar(DW[:, 1:2], DW[:, 0:1], -1.0, None, ALU.mult))
            ch.then(V.tensor_scalar(WD, CST[:, C_ID:C_ID + 1].to_broadcast([P, TOK]), 0.0, DW[:, 1:2],
                                    ALU.mult, ALU.add))
            V.memset(two(WD)[:, :, 0:1], LOW).then_inc(prepared, 1)
            dve.wait_ge(prepared, 1)
            start = ch.n
            PER_A = 29
            with dve.Fori(0, UNITS) as u:
                ch = Chain(dve, dve_chain, start + u * PER_A)
                tile = lambda i: X[:, bass.ds(u * TILES + i, 1), :].rearrange("p n d -> p (n d)")
                norm_stats(dve, ch, tile, sig["a_var"])
                dve.wait_ge(sig["a_rstd"], u + 1)
                dve.wait_ge(sig["a_tr"], 1 + u)
                norm_apply(lambda i: XNa[:, i, :], tile, sig["a_xn"])
                K, Vv = PB[2][:, :], PB[3][:, :]
                w, first = DW[:, 1:2], vec(FIRST)
                dve.wait_ge(sig["a_kv"], u + 1)
                ch.then(V.tensor_tensor_scan(Mx, WD, K, LOW, ALU.add, ALU.max))
                ch.done(V.scalar_tensor_tensor(Dx[:, 0, :, 1:T], two(Mx)[:, :, 0:T - 1], w, two(Mx)[:, :, 1:T],
                                               ALU.add, ALU.subtract))
                V.tensor_tensor(Dx[:, 1, :, :], two(K), two(Mx), ALU.subtract).then_inc(sig["a_d"], 1)
                dve.wait_ge(sig["a_e"], u + 1)
                V.tensor_tensor_scan(Sx, SC[:, 1024:1536], SC[:, 1536:2048], 0.0, ALU.mult, ALU.add).then_inc(sig["a_s"], 1)
                dve.wait_ge(sig["a_l"], u + 1)
                ch.then(V.tensor_tensor(Bx[:, :, 1:T + 1], two(Mx), two(L1), ALU.add))
                Bp = Bx[:, :, 0:T]
                ch.done(V.scalar_tensor_tensor(two(P2), Bp, w, two(K), ALU.add, ALU.max))
                ch.then(V.scalar_tensor_tensor(two(P1), two(K), first, Bp, ALU.add, ALU.max))
                ch.done(V.scalar_tensor_tensor(Fx[:, 0, :, :], Bp, w, two(P2), ALU.add, ALU.subtract))
                ch.done(V.tensor_tensor(Fx[:, 1, :, :], two(K), two(P2), ALU.subtract))
                ch.done(V.tensor_tensor(Fx[:, 2, :, :], Bp, two(P1), ALU.subtract))
                V.scalar_tensor_tensor(Fx[:, 3, :, :], two(K), first, two(P1), ALU.add, ALU.subtract)\
                    .then_inc(sig["a_f"], 1)
                dve.wait_ge(sig["a_g"], u + 1)
                g = [HT[:, 1, k * TOK:(k + 1) * TOK] for k in range(4)]
                ch.then(V.tensor_tensor(N1, g[1], Vv, ALU.mult))
                ch.then(V.tensor_tensor_scan(Ax[:, 1:TOK + 1], g[0], N1, 0.0, ALU.mult, ALU.add))
                ch.done(V.tensor_tensor(N1, g[2], Ax[:, 0:TOK], ALU.mult))
                ch.then(V.tensor_tensor(N2, g[3], Vv, ALU.mult))
                ch.done(V.tensor_tensor(N1, N1, N2, ALU.add))
                ch.then(V.scalar_tensor_tensor(P1, g[2], WKV_EPS, g[3], ALU.add, ALU.add))
                dve.wait_ge(sig["a_er"], 1 + u + 1)
                ch.then(V.scalar_tensor_tensor(P1, ER, 1.0, P1, ALU.add, ALU.mult))
                ch.then(V.reciprocal(P1, P1))
                rw = RW[:, bass.ds(u * UB, UB), :]
                ch.then(V.tensor_tensor(rw, two(N1), two(P1), ALU.mult))
                apart(dve)
                for b in range(UB):
                    ch.done(V.bn_stats(BNR[:, b, :], RW[:, bass.ds(u * UB + b, 1), :].rearrange("p b t -> p (b t)")))
                ch.settle()
                apart(dve)
                ch.done(V.bn_aggr(MVU[:, 0, :], BNR[:, 0, :]))
                ch.then(V.bn_aggr(MVU[:, 1, :], BNR[:, 1, :]))
                V.tensor_copy(MVR[:, bass.ds(u * UB, UB), :], MVU).then_inc(sig["a_done"], 1)
                assert ch.n == PER_A
            start += UNITS * PER_A
            ch = Chain(dve, dve_chain, start)
            dve.wait_ge(sig["g_mean"], 1)
            dve.wait_ge(sig["a_done"], 1 + UNITS)
            ch.done(V.tensor_copy(GMS[:, 0, :], PB[0][:, 0:B]))
            ch.then(V.tensor_tensor(GMS[:, 1, :], MVR[:, :, 0], PB[0][:, 0:B], ALU.subtract))
            ch.then(V.tensor_tensor(GMS[:, 1, :], GMS[:, 1, :], GMS[:, 1, :], ALU.mult))
            V.tensor_tensor(GMS[:, 2, :], GMS[:, 1, :], MVR[:, :, 1], ALU.add).then_inc(sig["g_dev"], 1)
            dve.wait_ge(sig["g_var"], 1)
            ch.then(V.memset(NSC[:, 1, :], -0.5))
            V.tensor_scalar(GMS[:, 3, :], PB[1][:, 0:B], LN_EPS, None, ALU.add).then_inc(sig["g_ve"], 1)
            dve.wait_ge(sig["g_rstd"], 1)
            ch.then(V.tensor_scalar(NSC[:, 0, :], GMS[:, 4, :], vec(GAMMA), None, ALU.mult))
            ch.then(V.tensor_tensor(GMS[:, 5, :], GMS[:, 0, :], NSC[:, 0, :], ALU.mult))
            V.tensor_scalar(NSC[:, 1, :], GMS[:, 5, :], -1.0, vec(BETA), ALU.mult, ALU.add).then_inc(sig["weights_used"], 1)
            dve.wait_ge(sig["weights_used"], 1)
            start += ch.n
            PER_B = 10
            with dve.Fori(0, UNITS) as u:
                ch = Chain(dve, dve_chain, start + u * PER_B)
                dve.wait_ge(sig["b_at"], 1 + u)
                for b in range(UB):
                    row = RW[:, bass.ds(u * UB + b, 1), :].rearrange("p b t -> p (b t)")
                    last = V.tensor_scalar(RN[:, b * T:(b + 1) * T], row, NSC[:, 0, bass.ds(u * UB + b, 1)],
                                           NSC[:, 1, bass.ds(u * UB + b, 1)], ALU.mult, ALU.add)
                last.then_inc(sig["b_n"], 1)
                dve.wait_ge(sig["b_lg"], u + 1)
                gate_logits(dve, ch, True, sig["b_c"])
                gate_weights(dve, ch, sig["b_ex"], u + 1, sig["b_gate"])
                dve.wait_ge(sig["b_gate"], u + 1)
                dve.wait_ge(sig["b_at"], 1 + u + 1)
                xs = X[:, bass.ds(u * TILES, TILES), :]
                V.tensor_tensor(xs, xs, PB[5][:, :].rearrange("p (n d) -> p n d", d=D), ALU.add).then_inc(sig["b_x"], 1)
                dve.wait_ge(sig["b_x"], 1 + u + 1)
                for e in range(E):
                    dve.wait_ge(sig["b_y"], 1 + u * E + e + 1)
                    if e >= 1:
                        dve.wait_ge(sig["b_acc"], 1 + u * E + e)
                    yb = PB[4 if e % 2 == 0 else 6]
                    for i in range(TILES):
                        x = X[:, bass.ds(u * TILES + i, 1), :].rearrange("p n d -> p (n d)")
                        last = V.scalar_tensor_tensor(x, yb[:, i * P:(i + 1) * P], GATE[:, i, e:e + 1], x,
                                                      ALU.mult, ALU.add)
                    last.then_inc(sig["b_acc"], 1)
                assert ch.n == PER_B
            start += UNITS * PER_B
            dve.wait_ge(sig["b_acc"], 1 + UNITS * E)
            with dve.Fori(0, UNITS) as u:
                ch = Chain(dve, dve_chain, start + u * 9)
                tile = lambda i: X[:, bass.ds(u * TILES + i, 1), :].rearrange("p n d -> p (n d)")
                norm_stats(dve, ch, tile, sig["c_var"])
                dve.wait_ge(sig["c_rstd"], u + 1)
                dve.wait_ge(sig["c_tr"], 1 + u)
                norm_apply(lambda i: XNT[:, i, :], tile, sig["c_xn"])
                dve.wait_ge(sig["c_xn"], u + 1)
                ch.done(V.tensor_copy(XN[:, bass.ds(u * TILES, TILES), :], XNT[:, :, :]))
            start += UNITS * 9
            cell_dve(dve, start)


def kernel(**inputs):
    import numpy as np
    import ml_dtypes
    import concourse.bacc as bacc
    from concourse.bass_utils import run_bass_kernel_spmd

    def arr(n):
        return np.asarray(inputs[n])

    q = np.arange(P)
    cst = np.zeros((P, C_END), np.float32)
    cst[:, C_ID:C_ID + P] = np.eye(P)
    cst[:, C_GROUP:C_GROUP + P] = (q[:, None] // HD == q[None, :] // HD) / HD
    cst[:, C_SEL:C_SEL + NS] = q[:, None] % B == np.arange(B)[None, :]
    cst[:, C_MASK:C_MASK + 4] = (q[:, None] % 32 // HD == np.arange(4)[None, :]) / np.sqrt(HD)
    cst[:, C_HOT:C_HOT + NB] = q[:, None] // B == np.arange(NB)[None, :]
    cst[:, C_LT8:C_LT8 + E * E] = (np.arange(E)[None, :] < np.arange(E)[:, None]).reshape(1, -1)
    cst[:, C_LT4:C_LT4 + NB * NB] = (np.arange(NB)[None, :] < np.arange(NB)[:, None]).reshape(1, -1)
    cst[:, C_BR:C_BR + E] = arr("L0_ffn_br")[None, :]
    cst[:, C_BB:C_BB + NS] = np.repeat(arr("L1_attn_b_beta"), B, axis=0)
    cst[:, C_B1:C_B1 + E * H0C] = arr("L0_ffn_b1").reshape(E * H0C, P).T
    cst[:, C_NHALF:C_NHALF + TILES] = -0.5
    cst[:, C_HALF:C_HALF + STEPS] = 0.5
    cst[:, C_EPS] = WKV_EPS
    neg = np.zeros((P, 3 * P), ml_dtypes.bfloat16)
    neg[:, 0:P] = np.eye(P)
    neg[:, 2 * P:3 * P] = np.where(q[None, :] > q[:, None], -1e30, 0.0)
    wkv = arr("L1_attn_W_kv").reshape(NB, 2, NS, D)
    wb = arr("L1_attn_W_beta").reshape(NB, NS, D)
    wq, wr = arr("L1_attn_W_q"), arr("L1_attn_W_router")
    wc = np.stack([np.concatenate([wkv[n, 0], wkv[n, 1], wb[n], wq, wr]) for n in range(NB)])
    data = {
        "x": arr("L0_attn_x").reshape(B * T, D),
        "WA": np.stack([arr("L0_attn_W_" + c).T for c in "rkvo"], axis=1),
        "VEC": np.stack([arr(n).reshape(D) for n in (
            "L0_attn_time_mix_r", "L0_attn_time_mix_k", "L0_attn_time_mix_v", "L0_attn_time_decay",
            "L0_attn_time_first", "L0_attn_ln_gamma", "L0_attn_ln_beta", "L1_ffn_ln1_w", "L1_ffn_ln2_w")], axis=1),
        "CST": cst, "NEG": neg,
        "WR0": arr("L0_ffn_Wr"),
        "W1": arr("L0_ffn_W1").transpose(1, 0, 2).reshape(D, E * H0C * P),
        "W2": arr("L0_ffn_W2").reshape(E * H0C, P, D).transpose(1, 0, 2),
        "B2": arr("L0_ffn_b2"),
        "WIN": arr("L1_attn_W_in").T,
        "WC": wc.transpose(2, 0, 1),
        "WOUT": arr("L1_attn_W_out").T,
        "WQKV": arr("L1_ffn_c_attn_w"),
        "WPR": arr("L1_ffn_c_proj_w"),
        "WR1": arr("L1_ffn_router_w"),
        "W1b": arr("L1_ffn_w1"),
        "W2b": arr("L1_ffn_w2").reshape(E * H1C, P, D).transpose(1, 0, 2),
    }
    nc = bacc.Bacc("TRN2", target_bir_lowering=False, num_devices=1)
    arrays, aps = {}, {}
    for name, a in data.items():
        a = np.ascontiguousarray(a)
        arrays["in_" + name] = a
        aps[name] = nc.dram_tensor("in_" + name, a.shape, mybir.dt.from_np(a.dtype), kind="ExternalInput").ap()
    out = nc.dram_tensor("out", (B * T, D), F32, kind="ExternalOutput").ap()
    build(nc, aps, out)
    r = run_bass_kernel_spmd(nc, [arrays], core_ids=[0])
    return r.results[0]["out"].reshape(B, T, D)
```

```python
import concourse.bass as bass
from concourse import mybir
from contextlib import ExitStack

B, T, D = 32, 256, 128
P = 128
UB = 2
UNITS = B // UB
TILES = UB * T // P
TOK = UB * T
E = 8
H0C, H1C = 4, 2
NH, HD = 16, 8
NB, NS = 4, 32
STEPS = T // UNITS
CELL = 4 * NS + NB
LN_EPS, WKV_EPS = 1e-5, 1e-8
LOW = -1e38

F32 = mybir.dt.float32
BF16 = mybir.dt.bfloat16
ALU = mybir.AluOpType
ACT = mybir.ActivationFunctionType
AX = mybir.AxisListType.X

MIX_R, MIX_K, MIX_V, DECAY, FIRST, GAMMA, BETA, LN1_W, LN2_W = range(9)
C_ID = 0
C_GROUP = C_ID + P
C_SEL = C_GROUP + P
C_MASK = C_SEL + NS
C_HOT = C_MASK + 4
C_LT8 = C_HOT + NB
C_LT4 = C_LT8 + E * E
C_BR = C_LT4 + NB * NB
C_BB = C_BR + E
C_B1 = C_BB + NS
C_NHALF = C_B1 + E * H0C
C_HALF = C_NHALF + TILES
C_EPS = C_HALF + STEPS
C_END = C_EPS + 1


PER_CELL = 167
CELL_SEMS = (
    "scaled", "p_proj", "p_copied", "p_b", "p_bt", "p_ss", "p_norm", "p_lc", "p_le", "vq_copied", "p_beta",
    "z_ready", "th_done", "w_ready", "sq_product", "sq_summed", "sq_reduced", "sq_ready", "sq_t", "bo_ready", "co_ready", "co_copied",
    "f_var", "f_rstd", "f_xn", "f_tr", "f_xa", "f_q", "f_k", "f_v", "f_vt",
    "f_s", "f_m", "f_e", "f_t", "f_pc", "f_pv", "f_y", "f_yt", "f_yc", "f_pj", "f_x2",
    "h_var", "h_rstd", "h_xn", "h_tr", "h_xm", "h_lg", "h_c", "h_ex", "h_gate",
    "m_hp", "m_h", "m_y", "m_acc", "o_y", "o_x")


class Chain:

    def __init__(self, eng, sem, base=0):
        self.eng, self.sem, self.base, self.n = eng, sem, base, 0

    def done(self, ins):
        ins.then_inc(self.sem, 1)
        self.n += 1

    def mark(self, ins):
        self.done(ins)
        return self.n

    def reach(self, step):
        self.eng.wait_ge(self.sem, self.base + step)

    def settle(self):
        self.eng.wait_ge(self.sem, self.base + self.n)

    def then(self, ins):
        self.done(ins)
        self.settle()


def build(nc, A, out):
    ctx = ExitStack()
    with ctx:
        def sb(name, shape, dt=F32):
            return ctx.enter_context(nc.sbuf_tensor(name, shape, dt))

        def sem(name):
            return ctx.enter_context(nc.semaphore(name))

        X = sb("X", [P, B * T // P, D])
        FT = sb("FT", [P, B * (T + 1)])
        XT = FT[:, :].rearrange("p (b t) -> p b t", b=B)
        XP = FT[:, 0:B * T].rearrange("p (b t) -> p b t", b=B)
        RX = sb("RX", [P, B * T])
        RW = RX[:, :].rearrange("p (b t) -> p b t", b=B)
        XN = RX[:, :].rearrange("p (n d) -> p n d", d=D)
        W1 = sb("W1", [P, E * H0C * P])
        W2 = sb("W2", [P, E * H0C, D])
        WA = sb("WA", [P, 4, D])
        WM = sb("WM", [P, 2, 3, D])
        WR0 = sb("WR0", [P, E])
        B2 = sb("B2", [E, D])
        VEC = sb("VEC", [P, 9])
        CST = sb("CST", [P, C_END])
        NEG = sb("NEG", [P, 3 * P], BF16)
        WIN = sb("WIN", [P, D])
        WC = sb("WC", [P, NB, CELL])
        WOUT = sb("WOUT", [NS, D])
        WQKV = sb("WQKV", [P, 3 * D])
        WPR = sb("WPR", [P, D])
        WR1 = sb("WR1", [P, E])
        HT = sb("HT", [P, 2, H0C * TOK])
        SC = sb("SC", [P, 6 * NS * NS])
        BNS = sb("BNS", [P, TILES, 6])
        MV = sb("MV", [P, TILES, 2])
        VE = sb("VE", [P, TILES])
        RSTD = sb("RSTD", [P, TILES])
        XNT = sb("XNT", [P, TILES, D])
        LG = sb("LG", [P, TILES, E])
        MX = sb("MX", [P, TILES])
        LC = sb("LC", [P, TILES, E])
        EX = sb("EX", [P, TILES, E])
        CMP = sb("CMP", [P, 2, TILES * E * E])
        RK = sb("RK", [P, TILES, E])
        GATE = sb("GATE", [P, TILES, E])
        GS = sb("GS", [P, TILES])
        TB = sb("TB", [P, TOK])
        GT = TB[0:E, :]

        ident = CST[:, C_ID:C_ID + P]

        def vec(c):
            return VEC[:, c:c + 1]

        PB = [ctx.enter_context(nc.psum_tensor(f"PB{i}", [P, 512], F32)) for i in range(8)]

        loaded = sem("loaded")
        x_loaded = sem("x_loaded")
        late_loaded = sem("late_loaded")
        prepared = sem("prepared")
        dve_chain = sem("dve_chain")

        block = ctx.enter_context(nc.Block())

        WD = W1[:, 0:TOK]
        MVR = W1[:, 2048:2048 + 2 * B].rearrange("p (b k) -> p b k", k=2)
        BNR = W1[:, 2112:2112 + 6 * UB].rearrange("p (b k) -> p b k", k=6)
        MVU = W1[:, 2130:2130 + 2 * UB].rearrange("p (b k) -> p b k", k=2)
        GMS = W1[:, 2200:2200 + 6 * B].rearrange("p (k b) -> p k b", k=6)
        MV2 = W1[:, 2400:2416].rearrange("p (k i m) -> p k i m", k=2, m=2)
        VE2, RSTD2 = (W1[:, c:c + 8].rearrange("p (k i) -> p k i", k=2) for c in (2416, 2424))
        DW = sb("DW", [P, 2])
        NSC = sb("NSC", [P, 2, B])
        QM = sb("QM", [P, 4, TOK])
        RAW = sb("RAW", [P, STEPS, CELL])
        QMf = QM[:, :, :].rearrange("p h t -> p (h t)")
        RAWf = RAW[:, :, :].rearrange("p s c -> p (s c)")

        def cols(buf, first, n=TOK):
            return buf[:, first:first + n]

        WKV = (dict(D=cols(SC, 0, 2 * TOK), M=cols(SC, 1024), S=cols(SC, 1536), B=cols(SC, 2048, UB * (T + 1)),
                    A=cols(SC, 2564, TOK + 1), P1=cols(SC, 3080), P2=cols(SC, 3592), N1=cols(SC, 4104),
                    ER=cols(SC, 4616), N2=cols(SC, 5128), F=HT[:, 0, :], XN=XNT[:, :, :]),
               dict(D=cols(QMf, 0, 2 * TOK), M=cols(RAWf, 0), S=cols(RAWf, 512), B=cols(RAWf, 1024, UB * (T + 1)),
                    A=cols(W1, 2560, TOK + 1), P1=cols(QMf, 1024), P2=cols(QMf, 1536), N1=cols(RAWf, 1540),
                    ER=cols(W1, 1024), N2=cols(W1, 512), F=HT[:, 1, :],
                    XN=cols(W1, 1536).rearrange("p (n d) -> p n d", d=D)))

        def pair(w, name, k=2):
            return w[name].rearrange("p (k b t) -> p k b t", k=k, b=UB)

        XU = SC[:, 0:TOK]
        CX = QMf[:, 0:TOK]
        RN = SC[:, TOK:2 * TOK]

        def two(ap):
            return ap.rearrange("p (b t) -> p b t", b=UB)

        sig = {n: sem(n) for n in (
            "a_var", "a_rstd", "a_xn", "a_tr", "a_xt", "a_r", "a_k", "a_er", "a_d", "a_e", "a_s", "a_l",
            "a_f", "a_g", "a_done", "g_mean", "g_dev", "g_var", "g_ve", "g_rstd", "weights_used",
            "b_n", "b_xu", "f_cu", "o_st", "b_lg", "b_c", "b_ex", "b_gate", "b_gt", "b_gtc", "b_at", "b_x", "b_hp", "b_h", "b_y", "b_acc",
            "c_var", "c_rstd", "c_xn", "c_tr", "c_xt", "c_in", "c_xp",
            "decay_exp", "stored") + CELL_SEMS}

        n_early = 5

        def prime(eng, signals):
            for signal in signals:
                eng.sem_inc(signal, 1)

        def apart(eng):
            eng.nop(nofuse=True)

        def norm_stats(dve, ch, src, signal):
            row_moments(dve, ch, row_stats(dve, ch, src), signal)

        def row_stats(dve, ch, src):
            apart(dve)
            for i in range(TILES):
                ch.done(nc.vector.bn_stats(BNS[:, i, :], src(i)))
            return ch.n

        def row_moments(dve, ch, stats, signal):
            ch.reach(stats)
            apart(dve)
            for i in range(TILES):
                ch.done(nc.vector.bn_aggr(MV[:, i, :], BNS[:, i, :]))
            ch.settle()
            nc.vector.tensor_scalar(VE[:, :], MV[:, :, 1], LN_EPS, None, ALU.add).then_inc(signal, 1)

        def norm_apply(dst, src, signal):
            for i in range(TILES):
                last = nc.vector.tensor_scalar(dst(i), src(i), MV[:, i, 0:1], RSTD[:, i:i + 1],
                                               ALU.subtract, ALU.mult)
            last.then_inc(signal, 1)

        def rstd_pow(out_ap, in_ap, n, signal):
            nc.gpsimd.tensor_tensor(out_ap, in_ap, CST[:, C_NHALF:C_NHALF + n], ALU.pow).then_inc(signal, 1)

        def gate_logits(dve, ch, signal):
            ch.then(nc.vector.tensor_tensor(
                LG[:, :, :], PB[7][:, 0:TILES * E].rearrange("p (n e) -> p n e", e=E),
                CST[:, C_BR:C_BR + E].unsqueeze(1).to_broadcast([P, TILES, E]), ALU.add))
            ch.then(nc.vector.tensor_reduce(MX[:, :], LG[:, :, :], AX, ALU.max))
            nc.vector.tensor_tensor(LC[:, :, :], LG[:, :, :], MX[:, :].unsqueeze(2).to_broadcast([P, TILES, E]),
                                    ALU.subtract).then_inc(signal, 1)

        def top_two_rank(ch, lg, rank, n, e, lt):
            other = lg.unsqueeze(2).to_broadcast([P, n, e, e])
            own = lg.unsqueeze(3).to_broadcast([P, n, e, e])
            gt = CMP[:, 0, 0:n * e * e].rearrange("p (n e f) -> p n e f", n=n, e=e)
            eq = CMP[:, 1, 0:n * e * e].rearrange("p (n e f) -> p n e f", n=n, e=e)
            ch.done(nc.vector.tensor_tensor(gt, other, own, ALU.is_gt))
            ch.then(nc.vector.tensor_tensor(eq, other, own, ALU.is_equal))
            low = CST[:, lt:lt + e * e].unsqueeze(1).to_broadcast([P, n, e * e])
            eqf = CMP[:, 1, 0:n * e * e].rearrange("p (n e) -> p n e", n=n)
            ch.then(nc.vector.tensor_tensor(eqf, eqf, low, ALU.mult))
            ch.then(nc.vector.tensor_tensor(CMP[:, 0, 0:n * e * e], CMP[:, 0, 0:n * e * e],
                                            CMP[:, 1, 0:n * e * e], ALU.add))
            ch.then(nc.vector.tensor_reduce(rank, gt, AX, ALU.add))

        def gate_weights(dve, ch, exp_ready, value, signal):
            top_two_rank(ch, LG[:, :, :], RK[:, :, :], TILES, E, C_LT8)
            top_two(dve, ch, exp_ready, value, signal)

        def top_two(dve, ch, exp_ready, value, signal):
            dve.wait_ge(exp_ready, value)
            ch.then(nc.vector.scalar_tensor_tensor(GATE[:, :, :], RK[:, :, :], 2.0, EX[:, :, :],
                                                   ALU.is_lt, ALU.mult))
            ch.then(nc.vector.tensor_reduce(GS[:, :], GATE[:, :, :], AX, ALU.add))
            ch.then(nc.vector.reciprocal(GS[:, :], GS[:, :]))
            nc.vector.tensor_tensor(GATE[:, :, :], GATE[:, :, :], GS[:, :].unsqueeze(2).to_broadcast([P, TILES, E]),
                                    ALU.mult).then_inc(signal, 1)


        St = SC[:, 0:1024]
        PRD, ZB, BS, TH, PQ = (SC[:, k * 1024:(k + 1) * 1024] for k in range(1, 6))
        CU = QM[:, 0, :].rearrange("p (s b) -> p s b", b=B)
        KN, VV = (HT[:, 0, 1024 + k * 512:1536 + k * 512].rearrange("p (s j) -> p s j", j=NS) for k in range(2))
        QQ, BT = (HT[:, 1, 1024 + k * 512:1536 + k * 512].rearrange("p (s j) -> p s j", j=NS) for k in range(2))
        PEX = W1[:, 2048:3584].rearrange("p (j k) -> p j k", j=3)
        XA = W1[:, 3584:4096]
        W2f = W2[:, :, :].rearrange("p n d -> p (n d)")
        PTS = W2f[:, 2048:3584].rearrange("p (j k) -> p j k", j=3)
        KT = W2f[:, 3584:4096]
        VT = sb("VT", [P, TILES, D])
        WMf = WM[:, :, :, :].rearrange("p a m d -> p (a m d)")
        SQ = WMf[:, 0:STEPS * NS].rearrange("p (s i) -> p s i", i=NS)
        Y = WMf[:, STEPS * NS:STEPS * NS + 2 * D].rearrange("p (q d) -> p q d", d=D)
        YT = WA[:, 0:2, :].rearrange("p a d -> p (a d)")
        RS = sb("RS", [P, UB, 2, NH])
        RI = sb("RI", [P, 2, NH])
        NM = sb("NM", [P, 3, 4])
        SM16 = sb("SM16", [P, 8, STEPS])
        SM64 = WA[:, 2:4, :].rearrange("p a (k s n) -> p (a k) s n", k=2, n=NB)
        RET = NSC

        def t3(ap):
            return ap.rearrange("p (s j) -> p s j", j=NS)

        def rows(buf, h):
            return buf[:, h * 512:(h + 1) * 512]

        def v3(ap):
            return ap.rearrange("p (i j) -> p i j", j=NS)

        def bi(ap):
            return ap.unsqueeze(1).to_broadcast([P, NS, NS])

        def bj(ap):
            return ap.unsqueeze(2).to_broadcast([P, NS, NS])

        def tilef(buf, u, i):
            return buf[:, bass.ds(u * TILES + i, 1), :].rearrange("p n d -> p (n d)")

        def cell_sync(sp):
            outs = out.rearrange("(n p) d -> p n d", p=P)
            with sp.Fori(0, UNITS) as u:
                sp.wait_ge(sig["o_x"], 1 + u + 1)
                sp.dma_start(outs[:, bass.ds(u * TILES, TILES), :], X[:, bass.ds(u * TILES, TILES), :]).then_inc(sig["stored"], 16)
            sp.wait_ge(sig["stored"], 16 * UNITS)

        def cell_pool(pool):
            with pool.Fori(0, UNITS) as u:
                pool.wait_ge(sig["p_ss"], u + 1)
                nc.gpsimd.tensor_tensor(SM16[:, 1, :], SM16[:, 0, :], CST[:, C_HALF:C_HALF + STEPS],
                                        ALU.pow).then_inc(sig["p_norm"], 1)
                pool.wait_ge(sig["f_var"], u + 1)
                rstd_pow(RSTD[:, :], VE[:, :], TILES, sig["f_rstd"])
                pool.wait_ge(sig["h_var"], u + 1)
                rstd_pow(RSTD[:, :], VE[:, :], TILES, sig["h_rstd"])

        def cell_act(act):
            def copy_inputs(u, first=0):
                apart(act)
                rows = FT[:, first:first + B * T].rearrange("p (b t) -> p b t", b=B)
                nc.scalar.activation(CU, rows[:, :, bass.ds(u * STEPS, STEPS)].rearrange("p b t -> p t b"),
                                     ACT.Copy).then_inc(sig["f_cu"], 1)

            def copy_projections(u, pairs):
                for g in pairs:
                    act.wait_ge(sig["p_proj"], u * (STEPS // 2) + g + 1)
                    nc.scalar.activation(RAW[:, 2 * g:2 * g + 2, :],
                                         pair_bank(g), ACT.Copy).then_inc(sig["p_copied"], 1)

            def exponentials(u, c, parts):
                b, g = c // 4, c % 4
                for j in parts:
                    act.wait_ge(sig["f_m"], u * 24 + 3 * c + j + 1)
                    heads = range(4) if j == 0 else (2 * j - 2, 2 * j - 1)
                    w = 512 // len(heads)
                    for n, h in enumerate(heads):
                        last = nc.scalar.activation(PEX[:, j, n * w:(n + 1) * w], PB[j][:, n * w:(n + 1) * w],
                                                    ACT.Exp, bias=NM[:, j, n:n + 1],
                                                    accum_out=RS[:, b, min(j, 1), 4 * g + h:4 * g + h + 1])
                    last.then_inc(sig["f_e"], 1)

            def copy_transposes(u, c, parts):
                if parts[0] == 0:
                    act.wait_ge(sig["f_pv"], 1 + u * 8 + c)
                for j in parts:
                    act.wait_ge(sig["f_t"], u * 24 + 3 * c + j + 1)
                    nc.scalar.activation(PTS[:, j, :], PB[3 + j % 2][:, :], ACT.Copy).then_inc(sig["f_pc"], 1)

            def copy_attention(u, b):
                act.wait_ge(sig["f_yt"], u * UB + b + 1)
                nc.scalar.activation(YT[:, :], PB[6][:, 0:2 * P], ACT.Copy).then_inc(sig["f_yc"], 1)

            def gelu(u, e):
                if e >= 2:
                    act.wait_ge(sig["m_y"], u * E + e - 1)
                for c in range(H1C):
                    act.wait_ge(sig["m_hp"], u * (E * H1C) + e * H1C + c + 1)
                    nc.scalar.activation(HT[:, e % 2, c * TOK:(c + 1) * TOK], PB[2 * (e % 2) + c][:, :],
                                         ACT.Gelu).then_inc(sig["m_h"], 1)

            def before_tanh(u, st):
                if st == 0:
                    act.wait_ge(sig["f_tr"], u + 1)
                    nc.scalar.activation(XA, PB[6][:, :], ACT.Copy).then_inc(sig["f_xa"], 1)
                    act.wait_ge(sig["f_q"], u + 1)
                    for h in range(4):
                        nc.scalar.activation(QM[:, h, :], PB[0][:, :], ACT.Copy,
                                             scale=CST[:, C_MASK + h:C_MASK + h + 1])
                    act.wait_ge(sig["f_k"], u + 1)
                    nc.scalar.activation(KT, PB[1][:, :], ACT.Copy)
                    act.wait_ge(sig["f_v"], u + 1)
                    nc.scalar.activation(VT[:, :, :], PB[2][:, :].rearrange("p (n d) -> p n d", d=D),
                                         ACT.Copy).then_inc(sig["f_vt"], 1)
                if st == 7:
                    copy_attention(u, 0)
                if 1 <= st <= 8:
                    exponentials(u, st - 1, (1, 2))
                if st == 10:
                    copy_projections(u + 1, (4, 5))
                if 12 <= st <= 14:
                    gelu(u, 2 * (st - 11))

            def after_tanh(u, st):
                if 1 <= st <= 8:
                    copy_transposes(u, st - 1, (0,))
                if st <= 7:
                    exponentials(u, st, (0,))
                if 1 <= st <= 8:
                    copy_transposes(u, st - 1, (1, 2))
                if st == 8:
                    act.wait_ge(sig["f_s"], (u + 1) * 24)
                    act.wait_ge(sig["co_copied"], 1 + u)
                    copy_inputs(u, STEPS)
                if st == 9:
                    copy_projections(u + 1, (0, 1))
                    copy_attention(u, 1)
                    copy_projections(u + 1, (2, 3))
                if st == 10:
                    copy_projections(u + 1, (6, 7))
                    act.wait_ge(sig["h_tr"], u + 1)
                    nc.scalar.activation(XA, PB[6][:, :], ACT.Copy).then_inc(sig["h_xm"], 1)
                if st == 11:
                    act.wait_ge(sig["h_c"], u + 1)
                    nc.scalar.activation(EX[:, :, :], LC[:, :, :], ACT.Exp).then_inc(sig["h_ex"], 1)
                    gelu(u, 0)
                if 11 <= st <= 14:
                    gelu(u, 2 * (st - 11) + 1)

            act.wait_ge(sig["c_xp"], 1 + UNITS)
            copy_inputs(0)
            copy_projections(0, range(STEPS // 2))
            act.wait_ge(sig["scaled"], 1)
            with act.Fori(0, UNITS) as u:
                act.wait_ge(sig["p_b"], u + 1)
                nc.scalar.activation(BS[:, 512:1024], BS[:, 0:512], ACT.Tanh, scale=0.5).then_inc(sig["p_bt"], 1)
                act.wait_ge(sig["p_bt"], u + 1)
                nc.scalar.activation(BT, t3(BS[:, 512:1024]), ACT.Identity, bias=CST[:, C_HALF:C_HALF + 1],
                                     scale=0.5).then_inc(sig["p_beta"], 1)
                act.wait_ge(sig["p_lc"], u + 1)
                nc.scalar.activation(SM64[:, 1, :, :], SM64[:, 0, :, :], ACT.Exp).then_inc(sig["p_le"], 1)
                act.wait_ge(sig["p_copied"], (u + 1) * (STEPS // 2))
                nc.scalar.activation(VV, RAW[:, :, NS:2 * NS], ACT.Copy)
                nc.scalar.activation(QQ, RAW[:, :, 3 * NS:4 * NS], ACT.Copy).then_inc(sig["vq_copied"], 1)
                for st in range(STEPS):
                    before_tanh(u, st)
                    for h in range(2):
                        act.wait_ge(sig["z_ready"], 2 * (u * STEPS + st) + h + 1)
                        nc.scalar.activation(rows(TH, h), rows(ZB, h), ACT.Tanh).then_inc(sig["th_done"], 1)
                    for h in range(2):
                        act.wait_ge(sig["th_done"], 2 * (u * STEPS + st) + h + 1)
                        nc.scalar.activation(rows(TH, h), rows(TH, h), ACT.Copy,
                                             scale=SM16[:, 4, st:st + 1]).then_inc(sig["w_ready"], 1)
                    after_tanh(u, st)
                act.wait_ge(sig["sq_ready"], u + 1)
                nc.scalar.activation(TB[:, :], SQ[:, :, :].rearrange("p s i -> p (s i)"), ACT.Tanh,
                                     scale=0.5).then_inc(sig["sq_t"], 1)
                act.wait_ge(sig["co_ready"], u + 1)
                apart(act)
                nc.scalar.activation(XP[0:NS, :, bass.ds(u * STEPS, STEPS)],
                                     PB[7][0:NS, :].rearrange("i (t b) -> i b t", b=B), ACT.Copy).then_inc(sig["co_copied"], 1)
            act.wait_ge(sig["co_copied"], 1 + UNITS)
            with act.Fori(0, UNITS) as u:
                act.wait_ge(sig["o_y"], 1 + u)
                apart(act)
                nc.scalar.activation(two(SC[0:NS, 0:TOK]), XP[0:NS, bass.ds(u * UB, UB), :], ACT.Copy).then_inc(sig["o_st"], 1)

        def pair_bank(g):
            return PB[3 + g % 2][:, 0:2 * CELL].rearrange("p (s c) -> p s c", c=CELL)

        def cell_pe(pe):
            def scores(u, c, j):
                b, g = c // 4, c % 4
                q0, q1 = 32 * g, 32 * g + 32
                if c >= 1:
                    pe.wait_ge(sig["f_e"], u * 24 + 3 * (c - 1) + j + 1)
                if j == 0:
                    nc.tensor.matmul(PB[0][:, :].rearrange("p (h k) -> p h k", h=4), NEG[:, 0:P],
                                     NEG[:, 2 * P:3 * P].unsqueeze(1).to_broadcast([P, 4, P]), start=True, stop=False)
                    for h in range(4):
                        last = nc.tensor.matmul(PB[0][:, h * P:(h + 1) * P], QM[q0:q1, h, b * T:b * T + P],
                                                KT[q0:q1, b * T:b * T + P], start=False, stop=(h == 3), tile_position=(q0, 0))
                else:
                    nc.tensor.matmul(PB[j][:, :].rearrange("p (h k) -> p h k", h=2), NEG[:, 0:P],
                                     NEG[:, P:3 * P].unsqueeze(1).to_broadcast([P, 2, 2 * P]), start=True, stop=False)
                    for n in range(2):
                        h = 2 * j - 2 + n
                        last = nc.tensor.matmul(PB[j][:, n * T:(n + 1) * T], QM[q0:q1, h, b * T + P:b * T + 2 * P],
                                                KT[q0:q1, b * T:b * T + T], start=False, stop=(n == 1), tile_position=(q0, 0))
                last.then_inc(sig["f_s"], 1)

            def transposes(u, c, j):
                pe.wait_ge(sig["f_e"], u * 24 + 3 * c + j + 1)
                if j == 2:
                    pe.wait_ge(sig["f_pc"], 1 + u * 24 + 3 * c + 1)
                elif c >= 1:
                    pe.wait_ge(sig["f_pc"], 1 + u * 24 + 3 * c)
                for k in range(4):
                    last = nc.tensor.transpose(PB[3 + j % 2][:, k * P:(k + 1) * P], PEX[:, j, k * P:(k + 1) * P], ident)
                last.then_inc(sig["f_t"], 1)

            def values(u, c, heads):
                b, g = c // 4, c % 4
                if heads[0] == 0:
                    if c % 4 == 0:
                        pe.wait_ge(sig["f_y"], 1 + u * UB + b)
                    pe.wait_ge(sig["f_pc"], 1 + u * 24 + 3 * c + 3)
                for h in heads:
                    o = (4 * g + h) * HD
                    nc.tensor.matmul(PB[5][:, o:o + HD], PTS[:, 0, h * P:(h + 1) * P], VT[:, 2 * b, o:o + HD],
                                     start=True, stop=True)
                    for kt in range(2):
                        col = (h % 2) * T + kt * P
                        last = nc.tensor.matmul(PB[5][:, P + o:P + o + HD], PTS[:, 1 + h // 2, col:col + P],
                                                VT[:, 2 * b + kt, o:o + HD], start=(kt == 0), stop=(kt == 1))
                if heads[-1] == 3:
                    last.then_inc(sig["f_pv"], 1)

            def transpose_attention(u, b):
                pe.wait_ge(sig["f_y"], 1 + u * UB + b + 1)
                if b == 1:
                    pe.wait_ge(sig["f_x2"], 1 + u * UB + 1)
                for qt in range(2):
                    last = nc.tensor.transpose(PB[6][:, qt * P:(qt + 1) * P], Y[:, qt, :], ident)
                last.then_inc(sig["f_yt"], 1)

            def project_attention(u, b):
                pe.wait_ge(sig["f_yc"], u * UB + b + 1)
                for qt in range(2):
                    last = nc.tensor.matmul(PB[6][:, (2 + qt) * P:(3 + qt) * P], YT[:, qt * P:(qt + 1) * P], WPR[:, :],
                                            start=True, stop=True)
                last.then_inc(sig["f_pj"], 1)

            def project_cell(u, pairs):
                for g in pairs:
                    if g >= 2:
                        pe.wait_ge(sig["p_copied"], u * (STEPS // 2) + g - 1)
                    for k in range(2):
                        for n in range(NB):
                            last = nc.tensor.matmul(pair_bank(g)[32 * n:32 * n + 32, k, :],
                                                    CU[:, 2 * g + k, :],
                                                    WC[:, n, :], start=True, stop=True, tile_position=(0, 32 * n))
                    last.then_inc(sig["p_proj"], 1)

            def sum_products(u, k):
                pe.wait_ge(sig["sq_product"], u * STEPS + k + 1)
                if k % 2 == 0 and k > 0:
                    pe.wait_ge(sig["sq_reduced"], u * (STEPS // 2 - 1) + k // 2)
                if k == 0:
                    pe.wait_ge(sig["co_copied"], 1 + u)
                pq = v3(PQ)
                for m in range(NS // 4):
                    last = nc.tensor.matmul(PB[7][:, (k % 2) * P:(k % 2 + 1) * P].rearrange("p (i l) -> p i l", l=4),
                                            ident, pq[:, :, 4 * m:4 * m + 4], start=(m == 0), stop=(m == NS // 4 - 1))
                last.then_inc(sig["sq_summed"], 1)

            def hidden(u, e):
                for c in range(H1C):
                    k = e * H1C + c
                    if e >= 2:
                        pe.wait_ge(sig["m_h"], u * (E * H1C) + k - 2 * H1C + 1)
                    nc.tensor.matmul(PB[2 * (e % 2) + c][:, :], W1[:, k * P:(k + 1) * P], XA, start=True,
                                     stop=True).then_inc(sig["m_hp"], 1)

            def expert_out(u, e):
                pe.wait_ge(sig["m_h"], u * (E * H1C) + (e + 1) * H1C)
                if e >= 2:
                    pe.wait_ge(sig["m_acc"], 1 + u * E + e - 1)
                yb = PB[4 + e % 2]
                for i in range(TILES):
                    for c in range(H1C):
                        last = nc.tensor.matmul(yb[:, i * P:(i + 1) * P],
                                                HT[:, e % 2, c * TOK + i * P:c * TOK + (i + 1) * P],
                                                W2[:, e * H1C + c, :], start=(c == 0), stop=(c == H1C - 1))
                last.then_inc(sig["m_y"], 1)

            pe.wait_ge(sig["c_xp"], 1 + UNITS)
            pe.wait_ge(sig["f_cu"], 1)
            project_cell(0, range(STEPS // 2))
            pe.wait_ge(late_loaded, 16 * 12)
            pe.wait_ge(sig["scaled"], 1)
            with pe.Fori(0, UNITS) as u:
                pe.wait_ge(sig["f_xn"], u + 1)
                for i in range(TILES):
                    last = nc.tensor.transpose(PB[6][:, i * P:(i + 1) * P], XNT[:, i, :], ident)
                last.then_inc(sig["f_tr"], 1)
                pe.wait_ge(sig["f_xa"], u + 1)
                nc.tensor.matmul(PB[0][:, :], WQKV[:, 0:D], XA, start=True, stop=True).then_inc(sig["f_q"], 1)
                nc.tensor.matmul(PB[1][:, :], WQKV[:, D:2 * D], XA, start=True, stop=True).then_inc(sig["f_k"], 1)
                for i in range(TILES):
                    last = nc.tensor.matmul(PB[2][:, i * P:(i + 1) * P], XA[:, i * P:(i + 1) * P], WQKV[:, 2 * D:3 * D],
                                            start=True, stop=True)
                last.then_inc(sig["f_v"], 1)
                pe.wait_ge(sig["f_vt"], u + 1)
                for j in range(3):
                    scores(u, 0, j)
                for c in range(8):
                    if c == 6:
                        transpose_attention(u, 0)
                    for j in range(3):
                        if (c, j) == (7, 0):
                            project_attention(u, 0)
                        if j == 2:
                            sum_products(u, c)
                        transposes(u, c, j)
                        if c >= 1 and j == 1:
                            values(u, c - 1, (0, 1))
                        if c < 7:
                            scores(u, c + 1, j)
                        if c >= 1 and j == 1:
                            values(u, c - 1, (2, 3))
                values(u, 7, range(4))
                pe.wait_ge(sig["f_cu"], u + 2)
                pe.wait_ge(sig["f_pc"], 1 + (u + 1) * 24)
                project_cell(u + 1, (0, 1))
                transpose_attention(u, 1)
                project_attention(u, 1)
                sum_products(u, 8)
                project_cell(u + 1, (2, 3))
                project_cell(u + 1, (4, 5, 6, 7))
                sum_products(u, 9)
                pe.wait_ge(sig["h_xn"], u + 1)
                for i in range(TILES):
                    last = nc.tensor.transpose(PB[6][:, i * P:(i + 1) * P], XNT[:, i, :], ident)
                last.then_inc(sig["h_tr"], 1)
                pe.wait_ge(sig["h_xm"], u + 1)
                for i in range(TILES):
                    last = nc.tensor.matmul(PB[6][:, i * E:(i + 1) * E], XA[:, i * P:(i + 1) * P], WR1[:, :],
                                            start=True, stop=True)
                last.then_inc(sig["h_lg"], 1)
                hidden(u, 0)
                pe.wait_ge(sig["p_copied"], (u + 2) * (STEPS // 2))
                hidden(u, 1)
                for st in range(11, 15):
                    e = 2 * (st - 11)
                    sum_products(u, st - 1)
                    expert_out(u, e)
                    if e + 2 < E:
                        hidden(u, e + 2)
                    expert_out(u, e + 1)
                    if e + 3 < E:
                        hidden(u, e + 3)
                sum_products(u, 14)
                sum_products(u, 15)
                pe.wait_ge(sig["bo_ready"], u + 1)
                for t in range(STEPS):
                    last = nc.tensor.matmul(PB[7][0:NS, t * B:(t + 1) * B], TB[:, t * NS:(t + 1) * NS],
                                            CST[:, C_SEL:C_SEL + NS], start=True, stop=True)
                last.then_inc(sig["co_ready"], 1)
            pe.wait_ge(sig["co_copied"], 1 + UNITS)
            with pe.Fori(0, UNITS) as u:
                pe.wait_ge(sig["o_st"], u + 1)
                pe.wait_ge(sig["o_x"], 1 + u)
                for i in range(TILES):
                    last = nc.tensor.matmul(PB[0][:, i * P:(i + 1) * P], SC[0:NS, i * P:(i + 1) * P],
                                            WOUT[:, :], start=True, stop=True)
                last.then_inc(sig["o_y"], 1)

        def cell_dve(dve, start):
            V = nc.vector
            ch = Chain(dve, dve_chain, start)
            dve.wait_ge(late_loaded, 16 * 12)
            for w, c in ((WQKV[:, :], LN1_W), (WR1[:, :], LN2_W), (W1[:, 0:E * H1C * P], LN2_W)):
                ch.done(V.tensor_scalar(w, w, vec(c), None, ALU.mult))
            dve.wait_ge(sig["g_rstd"], 1)
            V.memset(St, 0.0).then_inc(sig["scaled"], 1)
            dve.wait_ge(sig["scaled"], 1)
            start += ch.n

            def prep(u, ch):
                kq = lambda c: RAW[:, :, c * NS:(c + 1) * NS]
                b16 = lambda ap: ap.unsqueeze(2).to_broadcast([P, STEPS, NS])
                b4 = lambda ap: ap.unsqueeze(2).to_broadcast([P, STEPS, NB])
                logits = RAW[:, :, 4 * NS:CELL]
                tile = lambda i: tilef(XN, u, i)
                probs, rank = SM64[:, 1, :, :], SM64[:, 3, :, :]
                dve.wait_ge(sig["p_copied"], (u + 1) * (STEPS // 2))
                m = ch.mark(V.tensor_tensor(KN, kq(0), kq(0), ALU.mult))
                V.tensor_tensor(t3(BS[:, 0:512]), kq(2), CST[:, C_BB:C_BB + NS].unsqueeze(1).to_broadcast([P, STEPS, NS]),
                                ALU.add).then_inc(sig["p_b"], 1)
                n = ch.mark(V.tensor_reduce(SM16[:, 2, :], logits, AX, ALU.max))
                ch.reach(m)
                V.tensor_reduce(SM16[:, 0, :], KN, AX, ALU.add).then_inc(sig["p_ss"], 1)
                ch.reach(n)
                V.tensor_tensor(SM64[:, 0, :, :], logits, b4(SM16[:, 2, :]), ALU.subtract).then_inc(sig["p_lc"], 1)
                apart(dve)
                for i in range(TILES):
                    m = ch.mark(V.bn_stats(BNS[:, i, :], tile(i)))
                other = logits.unsqueeze(2).to_broadcast([P, STEPS, NB, NB])
                own = logits.unsqueeze(3).to_broadcast([P, STEPS, NB, NB])
                larger, equal = (CMP[:, k, :].rearrange("p (n e f) -> p n e f", n=STEPS, e=NB) for k in range(2))
                low = CST[:, C_LT4:C_LT4 + NB * NB].unsqueeze(1).to_broadcast([P, STEPS, NB * NB])
                eqf = CMP[:, 1, :].rearrange("p (n e) -> p n e", n=STEPS)
                n = ch.mark(V.tensor_tensor(equal, other, own, ALU.is_equal))
                ch.reach(m)
                apart(dve)
                for i in range(TILES):
                    m = ch.mark(V.bn_aggr(MV[:, i, :], BNS[:, i, :]))
                ch.done(V.tensor_tensor(larger, other, own, ALU.is_gt))
                ch.reach(m)
                V.tensor_scalar(VE[:, :], MV[:, :, 1], LN_EPS, None, ALU.add).then_inc(sig["f_var"], 1)
                ch.reach(n)
                n = ch.mark(V.tensor_tensor(eqf, eqf, low, ALU.mult))
                dve.wait_ge(sig["p_le"], u + 1)
                m = ch.mark(V.tensor_reduce(SM16[:, 2, :], probs, AX, ALU.add))
                ch.reach(n)
                n = ch.mark(V.tensor_tensor(CMP[:, 0, :], CMP[:, 0, :], CMP[:, 1, :], ALU.add))
                ch.reach(m)
                m = ch.mark(V.reciprocal(SM16[:, 2, :], SM16[:, 2, :]))
                ch.reach(n)
                ch.done(V.tensor_reduce(rank, larger, AX, ALU.add))
                ch.reach(m)
                m = ch.mark(V.tensor_tensor(probs, probs, b4(SM16[:, 2, :]), ALU.mult))
                dve.wait_ge(sig["f_rstd"], u + 1)

                def apply(i):
                    return V.tensor_scalar(XNT[:, i, :], tile(i), MV[:, i, 0:1], RSTD[:, i:i + 1],
                                           ALU.subtract, ALU.mult)
                apply(0)
                ch.reach(m)
                m = ch.mark(V.scalar_tensor_tensor(rank, rank, 2.0, probs, ALU.is_lt, ALU.mult))
                apply(1)
                ch.reach(m)
                m = ch.mark(V.tensor_reduce(SM16[:, 3, :], rank, AX, ALU.add))
                apply(2)
                apply(3).then_inc(sig["f_xn"], 1)
                ch.reach(m)
                m = ch.mark(V.tensor_scalar(SM16[:, 3, :], SM16[:, 3, :], 1e-8, None, ALU.add))
                dve.wait_ge(sig["p_norm"], u + 1)
                n = ch.mark(V.tensor_scalar(SM16[:, 1, :], SM16[:, 1, :], 1e-6, None, ALU.add))
                ch.reach(m)
                m = ch.mark(V.reciprocal(SM16[:, 3, :], SM16[:, 3, :]))
                ch.reach(n)
                n = ch.mark(V.reciprocal(SM16[:, 1, :], SM16[:, 1, :]))
                ch.reach(m)
                m = ch.mark(V.tensor_tensor(rank, rank, b4(SM16[:, 3, :]), ALU.mult))
                ch.reach(n)
                ch.done(V.tensor_tensor(KN, kq(0), b16(SM16[:, 1, :]), ALU.mult))
                hot = CST[:, C_HOT:C_HOT + NB].unsqueeze(1).to_broadcast([P, STEPS, NB])
                ch.reach(m)
                m = ch.mark(V.tensor_tensor(rank, rank, hot, ALU.mult))
                n = ch.mark(V.tensor_tensor(probs, probs, hot, ALU.mult))
                ch.reach(m)
                m = ch.mark(V.tensor_reduce(SM16[:, 4, :], rank, AX, ALU.add))
                ch.reach(n)
                n = ch.mark(V.tensor_reduce(SM16[:, 5, :], probs, AX, ALU.add))
                ch.reach(m)
                ch.done(V.tensor_scalar(SM16[:, 6, :], SM16[:, 4, :], -1.0, 1.0, ALU.mult, ALU.add))
                ch.reach(n)
                ch.done(V.tensor_scalar(SM16[:, 7, :], SM16[:, 5, :], 0.5, None, ALU.mult))

            def products(u, k):
                dve.wait_ge(sig["sq_summed"], 1 + u * STEPS + k)
                V.tensor_tensor(v3(PQ), v3(St), bi(QQ[:, k, :]), ALU.mult).then_inc(sig["sq_product"], 1)

            def reduce_pair(u, k):
                dve.wait_ge(sig["sq_summed"], 1 + u * STEPS + k + 1)
                return V.tensor_reduce(SQ[:, k - 1:k + 1, :].rearrange("p s i -> p (s i)"),
                                       PB[7][:, 0:2 * P].rearrange("p (n l) -> p n l", l=4), AX, ALU.add)

            def scan_step(u, ch, st, beside):
                beside(0)
                if st >= 1:
                    ch.reach(ch.updated)
                else:
                    ch.settle()
                    dve.wait_ge(sig["p_beta"], u + 1)
                m = ch.mark(V.tensor_tensor(v3(PRD), v3(St), bi(KN[:, st, :]), ALU.mult))
                ch.done(V.tensor_tensor(v3(BS), v3(St), bj(BT[:, st, :]), ALU.mult))
                ch.reach(m)
                m = ch.mark(V.tensor_reduce(RET[:, 0, :], v3(PRD), AX, ALU.add))
                beside(1)
                if st == 0:
                    dve.wait_ge(sig["vq_copied"], u + 1)
                ch.reach(m)
                m = ch.mark(V.tensor_tensor(RET[:, 1, :], VV[:, st, :], RET[:, 0, :], ALU.subtract))
                beside(2)
                ch.reach(m)
                m = ch.mark(V.tensor_tensor(v3(ZB), bj(RET[:, 1, :]), bi(KN[:, st, :]), ALU.mult))
                beside(3)
                ch.reach(m)
                for h in range(2):
                    V.tensor_tensor(rows(ZB, h), rows(ZB, h), rows(BS, h), ALU.add).then_inc(sig["z_ready"], 1)
                if st >= 1:
                    products(u, st - 1)
                beside(4)
                if st >= 1:
                    dve.wait_ge(sig["sq_product"], u * STEPS + st)
                for h in range(2):
                    dve.wait_ge(sig["w_ready"], 2 * (u * STEPS + st) + h + 1)
                    ch.updated = ch.mark(V.scalar_tensor_tensor(rows(St, h), rows(St, h), SM16[:, 6, st:st + 1],
                                                                rows(TH, h), ALU.mult, ALU.add))

            def maxima(u, c, j):
                dve.wait_ge(sig["f_s"], u * 24 + 3 * c + j + 1)
                n = 4 if j == 0 else 2
                V.tensor_reduce(NM[:, j, 0:n], PB[j][:, :].rearrange("p (h k) -> p h k", h=n), AX, ALU.max,
                                negate=True).then_inc(sig["f_m"], 1)

            def row_sums(u, ch, b):
                dve.wait_ge(sig["f_pv"], 1 + u * 8 + 4 * (b + 1))
                return ch.mark(V.reciprocal(RI[:, :, :], RS[:, b, :, :]))

            def attention_out(u, ch, m):
                ch.reach(m)
                V.tensor_tensor(Y[:, :, :].rearrange("p q (h d) -> p (q h) d", d=HD),
                                PB[5][:, 0:2 * P].rearrange("p (q d) -> p q d", d=HD),
                                RI[:, :, :].rearrange("p q h -> p (q h)").unsqueeze(2).to_broadcast([P, 2 * NH, HD]),
                                ALU.mult).then_inc(sig["f_y"], 1)

            def residual(u, b):
                dve.wait_ge(sig["f_pj"], u * UB + b + 1)
                x = XN[:, bass.ds(u * TILES + 2 * b, 2), :]
                V.tensor_tensor(x, x, PB[6][:, 2 * P:4 * P].rearrange("p (n d) -> p n d", d=D), ALU.add).then_inc(sig["f_x2"], 1)

            def add_expert(u, e, tiles):
                dve.wait_ge(sig["m_y"], u * E + e + 1)
                if e >= 1 and tiles[0] == 0:
                    dve.wait_ge(sig["m_acc"], 1 + u * E + e)
                for i in tiles:
                    x = tilef(XN, u, i)
                    last = V.scalar_tensor_tensor(x, PB[4 + e % 2][:, i * P:(i + 1) * P], GATE[:, i, e:e + 1], x,
                                                  ALU.mult, ALU.add)
                if tiles[-1] == TILES - 1:
                    last.then_inc(sig["m_acc"], 1)

            def beside_step(u, ch, st):
                lg = PB[6][:, 0:TILES * E].rearrange("p (n e) -> p n e", e=E)
                other = LG[:, :, :].unsqueeze(2).to_broadcast([P, TILES, E, E])
                own = LG[:, :, :].unsqueeze(3).to_broadcast([P, TILES, E, E])
                larger, equal = (CMP[:, k, :].rearrange("p (n e f) -> p n e f", n=TILES, e=E) for k in range(2))

                def work(slot):
                    if st <= 7 and slot == 4:
                        maxima(u, st, 0)
                    if 1 <= st <= 8 and slot in (1, 3):
                        maxima(u, st - 1, (slot + 1) // 2)
                    if st >= 3 and st % 2 == 1 and slot == (2 if st <= 8 else 3):
                        reduce_pair(u, st - 2).then_inc(sig["sq_reduced"], 1)
                    if (st, slot) == (6, 1):
                        ch.row_sums = row_sums(u, ch, 0)
                    if (st, slot) == (6, 2):
                        attention_out(u, ch, ch.row_sums)
                    if (st, slot) == (8, 4):
                        residual(u, 0)
                    if (st, slot) == (9, 4):
                        attention_out(u, ch, row_sums(u, ch, 1))
                    if (st, slot) == (10, 2):
                        residual(u, 1)
                        dve.wait_ge(sig["f_x2"], 1 + u * UB + 2)
                        ch.stats = row_stats(dve, ch, lambda i: tilef(XN, u, i))
                    if (st, slot) == (10, 3):
                        row_moments(dve, ch, ch.stats, sig["h_var"])
                    if (st, slot) == (10, 4):
                        dve.wait_ge(sig["h_rstd"], u + 1)
                        norm_apply(lambda i: XNT[:, i, :], lambda i: tilef(XN, u, i), sig["h_xn"])
                    if (st, slot) == (11, 2):
                        dve.wait_ge(sig["h_lg"], u + 1)
                        ch.logits = ch.mark(V.tensor_copy(LG[:, :, :], lg))
                    if (st, slot) == (11, 3):
                        ch.reach(ch.logits)
                        ch.most = ch.mark(V.tensor_reduce(MX[:, :], LG[:, :, :], AX, ALU.max))
                        ch.equal = ch.mark(V.tensor_tensor(equal, other, own, ALU.is_equal))
                    if (st, slot) == (11, 4):
                        ch.reach(ch.most)
                        V.tensor_tensor(LC[:, :, :], LG[:, :, :], MX[:, :].unsqueeze(2).to_broadcast([P, TILES, E]),
                                        ALU.subtract).then_inc(sig["h_c"], 1)
                        ch.done(V.tensor_tensor(larger, other, own, ALU.is_gt))
                        ch.reach(ch.equal)
                        eqf = CMP[:, 1, :].rearrange("p (n e) -> p n e", n=TILES)
                        low = CST[:, C_LT8:C_LT8 + E * E].unsqueeze(1).to_broadcast([P, TILES, E * E])
                        ch.then(V.tensor_tensor(eqf, eqf, low, ALU.mult))
                        ch.then(V.tensor_tensor(CMP[:, 0, :], CMP[:, 0, :], CMP[:, 1, :], ALU.add))
                        ch.gates = ch.mark(V.tensor_reduce(RK[:, :, :], larger, AX, ALU.add))
                    if (st, slot) == (12, 0):
                        dve.wait_ge(sig["h_ex"], u + 1)
                        ch.reach(ch.gates)
                        ch.gates = ch.mark(V.scalar_tensor_tensor(GATE[:, :, :], RK[:, :, :], 2.0, EX[:, :, :],
                                                                  ALU.is_lt, ALU.mult))
                    if (st, slot) == (12, 1):
                        ch.reach(ch.gates)
                        ch.gates = ch.mark(V.tensor_reduce(GS[:, :], GATE[:, :, :], AX, ALU.add))
                    if (st, slot) == (12, 2):
                        ch.reach(ch.gates)
                        ch.gates = ch.mark(V.reciprocal(GS[:, :], GS[:, :]))
                    if (st, slot) == (12, 3):
                        ch.reach(ch.gates)
                        V.tensor_tensor(GATE[:, :, :], GATE[:, :, :], GS[:, :].unsqueeze(2).to_broadcast([P, TILES, E]),
                                        ALU.mult).then_inc(sig["h_gate"], 1)
                    if (st, slot) == (12, 4):
                        dve.wait_ge(sig["h_gate"], u + 1)
                    if st >= 12 and slot == 4:
                        add_expert(u, 2 * (st - 12), range(TILES))
                    elif st >= 13:
                        add_expert(u, 2 * (st - 13) + 1, (slot,))
                return work

            with dve.Fori(0, UNITS) as u:
                ch = Chain(dve, dve_chain, start + u * PER_CELL)
                prep(u, ch)
                for st in range(STEPS):
                    scan_step(u, ch, st, beside_step(u, ch, st))
                add_expert(u, E - 1, (0, 1))
                ch.reach(ch.updated)
                products(u, STEPS - 1)
                add_expert(u, E - 1, (2, 3))
                dve.wait_ge(sig["m_acc"], 1 + u * E + E)
                xs = X[:, bass.ds(u * TILES, TILES), :]
                ch.done(V.tensor_tensor(xs, xs, XN[:, bass.ds(u * TILES, TILES), :], ALU.add))
                reduce_pair(u, STEPS - 1).then_inc(sig["sq_ready"], 1)
                dve.wait_ge(sig["sq_ready"], u + 1)
                sqf = SQ[:, :, :].rearrange("p s i -> p (s i)")
                dve.wait_ge(sig["sq_t"], u + 1)
                ch.then(V.scalar_tensor_tensor(TB[:, :], TB[:, :], 1.0, sqf, ALU.add, ALU.mult))
                ch.then(V.tensor_tensor(TB[:, :], TB[:, :], sqf, ALU.mult))
                tb = TB[:, :].rearrange("p (s j) -> p s j", j=NS)
                V.tensor_tensor(tb, tb, SM16[:, 7, :].unsqueeze(2).to_broadcast([P, STEPS, NS]), ALU.mult)\
                    .then_inc(sig["bo_ready"], 1)
                dve.wait_ge(sig["bo_ready"], u + 1)
                assert ch.n == PER_CELL, ch.n
            with dve.Fori(0, UNITS) as u:
                dve.wait_ge(sig["o_y"], 1 + u + 1)
                xs = X[:, bass.ds(u * TILES, TILES), :]
                V.tensor_tensor(xs, xs, PB[0][:, :].rearrange("p (n d) -> p n d", d=D), ALU.add).then_inc(sig["o_x"], 1)


        @block.sync
        def _(sp):
            sp.dma_start(WA[:, :, :], A["WA"]).then_inc(loaded, 16)
            sp.dma_start(VEC[:, :], A["VEC"]).then_inc(loaded, 16)
            sp.dma_start(CST[:, :], A["CST"]).then_inc(loaded, 16)
            sp.dma_start(WR0[:, :], A["WR0"]).then_inc(loaded, 16)
            xs = A["x"].rearrange("(n p) d -> p n d", p=P)
            sp.dma_start(X[:, 0:2 * TILES, :], xs[:, 0:2 * TILES, :]).then_inc(loaded, 16)
            sp.dma_start(X[:, 2 * TILES:, :], xs[:, 2 * TILES:, :]).then_inc(x_loaded, 16)
            for dst, name in ((W2[:, :, :], "W2"), (B2[:, :], "B2"), (NEG[:, :], "NEG"), (WIN[:, :], "WIN"),
                              (WC[:, :, :], "WC"), (WOUT[:, :], "WOUT"), (WQKV[:, :], "WQKV"), (WPR[:, :], "WPR"),
                              (WR1[:, :], "WR1")):
                sp.dma_start(dst, A[name]).then_inc(late_loaded, 16)
            sp.wait_ge(sig["g_rstd"], 1)
            sp.wait_ge(sig["weights_used"], 1)
            sp.dma_start(W1[:, :], A["W1"]).then_inc(late_loaded, 16)
            sp.wait_ge(sig["b_acc"], 1 + UNITS * E)
            sp.dma_start(W1[:, 0:E * H1C * P], A["W1b"]).then_inc(late_loaded, 16)
            sp.dma_start(W2[:, 0:E * H1C, :], A["W2b"]).then_inc(late_loaded, 16)
            cell_sync(sp)

        @block.gpsimd
        def _(pool):
            pool.wait_ge(loaded, 16 * n_early)
            with pool.Fori(0, UNITS // 2) as v:
                for k in range(2):
                    pool.wait_ge(sig["a_var"], 2 * v + k + 1)
                    rstd_pow(RSTD2[:, k, :], VE2[:, k, :], TILES, sig["a_rstd"])
            pool.wait_ge(sig["g_ve"], 1)
            nc.gpsimd.tensor_tensor(GMS[:, 4, :], GMS[:, 3, :], NSC[:, 1, :], ALU.pow).then_inc(sig["g_rstd"], 1)
            with pool.Fori(0, UNITS) as u:
                pool.wait_ge(sig["c_var"], u + 1)
                rstd_pow(RSTD[:, :], VE[:, :], TILES, sig["c_rstd"])
            cell_pool(pool)

        @block.scalar
        def _(act):
            prime(act, (sig["a_xt"], sig["a_er"], sig["b_h"], sig["f_pc"], sig["c_xt"], sig["c_xp"], sig["co_copied"]))
            act.wait_ge(loaded, 16 * n_early)
            nc.scalar.activation(DW[:, 0:1], vec(DECAY), ACT.Exp).then_inc(sig["decay_exp"], 1)
            nc.scalar.preload_act_table_set("natural_log_exp_and_others")
            with act.Fori(0, UNITS // 2) as v:
                for k in range(2):
                    act.wait_ge(sig["a_tr"], 1 + 2 * v + k + 1)
                    apart(act)
                    nc.scalar.activation(XT[:, bass.ds(v * 2 * UB + k * UB, UB), 1:T + 1],
                                         two(PB[4 * k][:, :]), ACT.Copy).then_inc(sig["a_xt"], 1)
                for k in range(2):
                    d = pair(WKV[k], "D")
                    act.wait_ge(sig["a_d"], 2 * v + k + 1)
                    nc.scalar.activation(d[:, 0, :, 1:T], d[:, 0, :, 1:T], ACT.Exp)
                    nc.scalar.activation(d[:, 1, :, :], d[:, 1, :, :], ACT.Exp).then_inc(sig["a_e"], 1)
                for k in range(2):
                    act.wait_ge(sig["a_r"], 2 * v + k + 1)
                    act.wait_ge(sig["a_done"], 1 + 2 * v + k)
                    nc.scalar.activation(WKV[k]["ER"], PB[4 * k + 1][:, :], ACT.Exp, scale=-1.0).then_inc(sig["a_er"], 1)
                for k in range(2):
                    act.wait_ge(sig["a_s"], 2 * v + k + 1)
                    nc.scalar.activation(WKV[k]["S"], WKV[k]["S"], ACT.Ln, bias=CST[:, C_EPS:C_EPS + 1]).then_inc(sig["a_l"], 1)
                for k in range(2):
                    act.wait_ge(sig["a_f"], 2 * v + k + 1)
                    nc.scalar.activation(WKV[k]["F"], WKV[k]["F"], ACT.Exp).then_inc(sig["a_g"], 1)
            def expert_unit(u, done):
                act.wait_ge(sig["b_hp"], 1 + u * (E * H0C))
                apart(act)
                nc.scalar.activation(two(XU), XT[:, bass.ds(u * UB, UB), 1:T + 1], ACT.Copy).then_inc(sig["b_xu"], 1)
                for e in range(E):
                    act.wait_ge(sig["b_y"], 1 + u * E + e)
                    for c in range(H0C):
                        k = e * H0C + c
                        act.wait_ge(sig["b_hp"], 1 + u * (E * H0C) + k + 1)
                        nc.scalar.activation(HT[:, e % 2, c * TOK:(c + 1) * TOK], PB[c][:, :], ACT.Relu,
                                             bias=CST[:, C_B1 + k:C_B1 + k + 1]).then_inc(sig["b_h"], 1)
                    if e == 0:
                        act.wait_ge(sig["b_c"], u + 1)
                        nc.scalar.activation(EX[:, :, :], LC[:, :, :], ACT.Exp).then_inc(sig["b_ex"], 1)
                    if e == 1:
                        act.wait_ge(sig["b_gt"], u + 1)
                        nc.scalar.activation(GT[:, :], PB[6][0:E, :], ACT.Copy).then_inc(sig["b_gtc"], 1)
                    if e == 3 and done is not None:
                        copy_normed(done)
                    if e == 5 and done is not None:
                        cell_input(done)

            def copy_normed(u):
                act.wait_ge(sig["c_tr"], 1 + u + 1)
                act.wait_ge(sig["c_in"], 1 + u)
                nc.scalar.activation(CX, PB[7][:, :], ACT.Copy).then_inc(sig["c_xt"], 1)

            def cell_input(u):
                act.wait_ge(sig["c_in"], 1 + u + 1)
                act.wait_ge(sig["b_xu"], u + 1)
                apart(act)
                nc.scalar.activation(XP[:, bass.ds(u * UB, UB), :], two(PB[5][:, :]), ACT.Silu).then_inc(sig["c_xp"], 1)

            expert_unit(0, None)
            with act.Fori(0, UNITS - 1) as u:
                expert_unit(u + 1, u)
            copy_normed(UNITS - 1)
            cell_input(UNITS - 1)
            cell_act(act)

        @block.tensor
        def _(pe):
            pe.sem_inc(sig["b_y"], 2)
            prime(pe, (sig["b_hp"], sig["a_tr"], sig["b_at"], sig["c_in"], sig["c_tr"], sig["f_pv"], sig["sq_summed"], sig["o_y"]))
            pe.wait_ge(loaded, 16 * n_early)
            pe.wait_ge(prepared, 1)
            with pe.Fori(0, UNITS // 2) as v:
                for k in range(2):
                    pe.wait_ge(sig["a_xn"], 2 * v + k + 1)
                    pe.wait_ge(sig["a_xt"], 1 + 2 * v)
                    for i in range(TILES):
                        last = nc.tensor.transpose(PB[4 * k][:, i * P:(i + 1) * P], WKV[k]["XN"][:, i, :], ident)
                    last.then_inc(sig["a_tr"], 1)
                for k in range(2):
                    pe.wait_ge(sig["a_done"], 1 + 2 * v + k)
                    pe.wait_ge(sig["a_er"], 1 + 2 * v)
                    pe.wait_ge(sig["a_xt"], 1 + 2 * v + k + 1)
                    for m, signal in ((1, sig["a_k"]), (2, None), (0, sig["a_r"])):
                        bank = two(PB[4 * k + 1 + m][:, :])
                        nc.tensor.matmul(bank, WM[:, 0, m, :], XT[:, bass.ds(v * 2 * UB + k * UB, UB), 1:T + 1],
                                         start=True, stop=False)
                        last = nc.tensor.matmul(bank, WM[:, 1, m, :], XT[:, bass.ds(v * 2 * UB + k * UB, UB), 0:T],
                                                start=False, stop=True)
                        if signal is not None:
                            last.then_inc(signal, 1)
            pe.wait_ge(sig["a_done"], 2 + UNITS)
            nc.tensor.matmul(PB[0][:, 0:B], CST[:, C_GROUP:C_GROUP + P], MVR[:, :, 0], start=True,
                             stop=True).then_inc(sig["g_mean"], 1)
            pe.wait_ge(sig["g_dev"], 1)
            nc.tensor.matmul(PB[1][:, 0:B], CST[:, C_GROUP:C_GROUP + P], GMS[:, 2, :], start=True,
                             stop=True).then_inc(sig["g_var"], 1)
            pe.wait_ge(late_loaded, 16 * 10)
            def expert_unit(u, done):
                def hidden(e):
                    for c in range(H0C):
                        k = e * H0C + c
                        pe.wait_ge(sig["b_h"], 1 + u * (E * H0C) + max(k - H0C + 1, 0))
                        nc.tensor.matmul(PB[c][:, :], W1[:, k * P:(k + 1) * P], XU, start=True,
                                         stop=True).then_inc(sig["b_hp"], 1)

                pe.wait_ge(sig["b_xu"], u + 1)
                for i in range(TILES):
                    last = nc.tensor.matmul(PB[7][:, i * E:(i + 1) * E], XU[:, i * P:(i + 1) * P], WR0[:, :],
                                            start=True, stop=True)
                last.then_inc(sig["b_lg"], 1)
                hidden(0)
                hidden(1)
                pe.wait_ge(sig["b_gate"], u + 1)
                pe.wait_ge(sig["b_acc"], 1 + u * E)
                for i in range(TILES):
                    last = nc.tensor.transpose(PB[6][0:E, i * P:(i + 1) * P], GATE[:, i, :], ident)
                last.then_inc(sig["b_gt"], 1)
                for e in range(E):
                    if 1 <= e < E - 1:
                        hidden(e + 1)
                    if e == 1:
                        pe.wait_ge(sig["b_n"], u + 1)
                        pe.wait_ge(sig["b_gtc"], u + 1)
                        if done is not None:
                            pe.wait_ge(sig["c_xp"], 1 + done)
                        for i in range(TILES):
                            o = PB[5][:, i * P:(i + 1) * P]
                            nc.tensor.matmul(o, RN[:, i * P:(i + 1) * P],
                                             WA[:, 3, :], start=True, stop=False)
                            last = nc.tensor.matmul(o, GT[:, i * P:(i + 1) * P], B2[:, :], start=False, stop=True)
                        last.then_inc(sig["b_at"], 1)
                    pe.wait_ge(sig["b_h"], 1 + u * (E * H0C) + (e + 1) * H0C)
                    if e >= 2:
                        pe.wait_ge(sig["b_acc"], 1 + u * E + e - 1)
                    yb = PB[4 if e % 2 == 0 else 6]
                    for i in range(TILES):
                        for c in range(H0C):
                            last = nc.tensor.matmul(yb[:, i * P:(i + 1) * P],
                                                    HT[:, e % 2, c * TOK + i * P:c * TOK + (i + 1) * P],
                                                    W2[:, e * H0C + c, :], start=(c == 0), stop=(c == H0C - 1))
                    last.then_inc(sig["b_y"], 1)
                    if e == 2 and done is not None:
                        transpose_normed(done)
                    if e == 4 and done is not None:
                        pe.wait_ge(sig["b_x"], 1 + u + 1)
                        project_input(done)

            def transpose_normed(u):
                pe.wait_ge(sig["c_xn"], u + 1)
                for i in range(TILES):
                    last = nc.tensor.transpose(PB[7][:, i * P:(i + 1) * P], XNT[:, i, :], ident)
                last.then_inc(sig["c_tr"], 1)

            def project_input(u):
                pe.wait_ge(sig["c_xt"], 1 + u + 1)
                nc.tensor.matmul(PB[5][:, :], WIN[:, :], CX, start=True, stop=True).then_inc(sig["c_in"], 1)

            expert_unit(0, None)
            with pe.Fori(0, UNITS - 1) as u:
                expert_unit(u + 1, u)
            transpose_normed(UNITS - 1)
            project_input(UNITS - 1)
            cell_pe(pe)

        @block.vector
        def _(dve):
            dve.sem_inc(sig["a_done"], 2)
            prime(dve, (sig["b_acc"], sig["b_x"], sig["f_y"], sig["m_acc"], sig["o_x"], sig["f_x2"]))
            V = nc.vector
            dve.wait_ge(loaded, 16 * n_early)
            ch = Chain(dve, dve_chain)
            ch.done(V.memset(XT[:, :, 0:1], 0.0))
            for w in WKV:
                ch.done(V.memset(pair(w, "D")[:, 0, :, 0:1], 0.0))
                ch.done(V.memset(two(w["B"])[:, :, 0:1], LOW))
                ch.done(V.memset(w["A"][:, 0:1], 0.0))
            for m in range(3):
                ch.done(V.tensor_scalar(WM[:, 0, m, :], WA[:, m, :], vec(MIX_R + m), None, ALU.mult))
            ch.then(V.tensor_scalar(NSC[:, 0, 0:3], VEC[:, 0:3], -1.0, 1.0, ALU.mult, ALU.add))
            for m in range(3):
                ch.done(V.tensor_scalar(WM[:, 1, m, :], WA[:, m, :], NSC[:, 0, m:m + 1], None, ALU.mult))
            dve.wait_ge(sig["decay_exp"], 1)
            ch.then(V.tensor_scalar(DW[:, 1:2], DW[:, 0:1], -1.0, None, ALU.mult))
            ch.then(V.tensor_scalar(WD, CST[:, C_ID:C_ID + 1].to_broadcast([P, TOK]), 0.0, DW[:, 1:2],
                                    ALU.mult, ALU.add))
            V.memset(two(WD)[:, :, 0:1], LOW).then_inc(prepared, 1)
            dve.wait_ge(prepared, 1)
            start = ch.n
            PER_A = 58

            def stats(ch, v, k):
                apart(dve)
                for i in range(TILES):
                    ch.done(V.bn_stats(BNS[:, i, :], X[:, bass.ds(v * 2 * TILES + k * TILES + i, 1), :]
                                       .rearrange("p n d -> p (n d)")))
                ch.settle()
                apart(dve)
                for i in range(TILES):
                    ch.done(V.bn_aggr(MV2[:, k, i, :], BNS[:, i, :]))
                ch.settle()
                V.tensor_scalar(VE2[:, k, :], MV2[:, k, :, 1], LN_EPS, None, ALU.add).then_inc(sig["a_var"], 1)

            def normed(ch, v, k):
                dve.wait_ge(sig["a_rstd"], 2 * v + k + 1)
                dve.wait_ge(sig["a_tr"], 1 + 2 * v)
                for i in range(TILES):
                    tile = X[:, bass.ds(v * 2 * TILES + k * TILES + i, 1), :].rearrange("p n d -> p (n d)")
                    last = V.tensor_scalar(WKV[k]["XN"][:, i, :], tile, MV2[:, k, i, 0:1], RSTD2[:, k, i:i + 1],
                                           ALU.subtract, ALU.mult)
                last.then_inc(sig["a_xn"], 1)

            def running_maximum(ch, v, k):
                w, key, d = WKV[k], PB[4 * k + 2][:, :], pair(WKV[k], "D")
                dve.wait_ge(sig["a_k"], 2 * v + k + 1)
                ch.then(V.tensor_tensor_scan(w["M"], WD, key, LOW, ALU.add, ALU.max))
                ch.done(V.scalar_tensor_tensor(d[:, 0, :, 1:T], two(w["M"])[:, :, 0:T - 1], DW[:, 1:2],
                                               two(w["M"])[:, :, 1:T], ALU.add, ALU.subtract))
                V.tensor_tensor(d[:, 1, :, :], two(key), two(w["M"]), ALU.subtract).then_inc(sig["a_d"], 1)

            def running_sum(ch, v, k):
                w = WKV[k]
                dve.wait_ge(sig["a_e"], 2 * v + k + 1)
                V.tensor_tensor_scan(w["S"], w["D"][:, 0:TOK], w["D"][:, TOK:2 * TOK], 0.0, ALU.mult, ALU.add)\
                    .then_inc(sig["a_s"], 1)

            def exponents(ch, v, k):
                w, key, f = WKV[k], PB[4 * k + 2][:, :], pair(WKV[k], "F", 4)
                decay, first = DW[:, 1:2], vec(FIRST)
                dve.wait_ge(sig["a_l"], 2 * v + k + 1)
                ch.then(V.tensor_tensor(two(w["B"])[:, :, 1:T + 1], two(w["M"]), two(w["S"]), ALU.add))
                before = two(w["B"])[:, :, 0:T]
                p2 = ch.mark(V.scalar_tensor_tensor(two(w["P2"]), before, decay, two(key), ALU.add, ALU.max))
                p1 = ch.mark(V.scalar_tensor_tensor(two(w["P1"]), two(key), first, before, ALU.add, ALU.max))
                ch.reach(p2)
                ch.done(V.scalar_tensor_tensor(f[:, 0, :, :], before, decay, two(w["P2"]), ALU.add, ALU.subtract))
                ch.done(V.tensor_tensor(f[:, 1, :, :], two(key), two(w["P2"]), ALU.subtract))
                ch.reach(p1)
                ch.done(V.tensor_tensor(f[:, 2, :, :], before, two(w["P1"]), ALU.subtract))
                V.scalar_tensor_tensor(f[:, 3, :, :], two(key), first, two(w["P1"]), ALU.add, ALU.subtract)\
                    .then_inc(sig["a_f"], 1)

            def receptance(ch, v, k):
                w, value = WKV[k], PB[4 * k + 3][:, :]
                dve.wait_ge(sig["a_g"], 2 * v + k + 1)
                dve.wait_ge(sig["a_er"], 1 + 2 * v + k + 1)
                g = [w["F"][:, j * TOK:(j + 1) * TOK] for j in range(4)]
                n1 = ch.mark(V.tensor_tensor(w["N1"], g[1], value, ALU.mult))
                p1 = ch.mark(V.scalar_tensor_tensor(w["P1"], g[2], WKV_EPS, g[3], ALU.add, ALU.add))
                ch.reach(n1)
                a = ch.mark(V.tensor_tensor_scan(w["A"][:, 1:TOK + 1], g[0], w["N1"], 0.0, ALU.mult, ALU.add))
                ch.done(V.tensor_tensor(w["N2"], g[3], value, ALU.mult))
                ch.reach(a)
                n1 = ch.mark(V.tensor_tensor(w["N1"], g[2], w["A"][:, 0:TOK], ALU.mult))
                ch.reach(p1)
                p1 = ch.mark(V.scalar_tensor_tensor(w["P1"], w["ER"], 1.0, w["P1"], ALU.add, ALU.mult))
                ch.reach(n1)
                ch.done(V.tensor_tensor(w["N1"], w["N1"], w["N2"], ALU.add))
                ch.reach(p1)
                ch.then(V.reciprocal(w["P1"], w["P1"]))
                rw = RW[:, bass.ds(v * 2 * UB + k * UB, UB), :]
                ch.then(V.tensor_tensor(rw, two(w["N1"]), two(w["P1"]), ALU.mult))
                apart(dve)
                for b in range(UB):
                    ch.done(V.bn_stats(BNR[:, b, :], RW[:, bass.ds(v * 2 * UB + k * UB + b, 1), :]
                                       .rearrange("p b t -> p (b t)")))
                ch.settle()
                apart(dve)
                ch.done(V.bn_aggr(MVU[:, 0, :], BNR[:, 0, :]))
                ch.then(V.bn_aggr(MVU[:, 1, :], BNR[:, 1, :]))
                V.tensor_copy(MVR[:, bass.ds(v * 2 * UB + k * UB, UB), :], MVU).then_inc(sig["a_done"], 1)

            def both(ch, v, stages):
                for stage in stages:
                    for k in range(2):
                        if stage is receptance and k == 1:
                            dve.wait_ge(sig["a_done"], 2 + 2 * v + 1)
                        stage(ch, v, k)

            first, rest = (stats, normed), (running_maximum, running_sum, exponents)
            ch = Chain(dve, dve_chain, start)
            both(ch, 0, first + rest)
            start += ch.n
            dve.wait_ge(x_loaded, 16)
            with dve.Fori(0, UNITS // 2 - 1) as v:
                ch = Chain(dve, dve_chain, start + v * PER_A)
                both(ch, v + 1, first)
                both(ch, v, (receptance,))
                both(ch, v + 1, rest)
                assert ch.n == PER_A, ch.n
            start += (UNITS // 2 - 1) * PER_A
            ch = Chain(dve, dve_chain, start)
            both(ch, UNITS // 2 - 1, (receptance,))
            start += ch.n
            ch = Chain(dve, dve_chain, start)
            dve.wait_ge(sig["g_mean"], 1)
            dve.wait_ge(sig["a_done"], 2 + UNITS)
            ch.done(V.tensor_copy(GMS[:, 0, :], PB[0][:, 0:B]))
            ch.then(V.tensor_tensor(GMS[:, 1, :], MVR[:, :, 0], PB[0][:, 0:B], ALU.subtract))
            ch.then(V.tensor_tensor(GMS[:, 1, :], GMS[:, 1, :], GMS[:, 1, :], ALU.mult))
            V.tensor_tensor(GMS[:, 2, :], GMS[:, 1, :], MVR[:, :, 1], ALU.add).then_inc(sig["g_dev"], 1)
            dve.wait_ge(sig["g_var"], 1)
            ch.then(V.memset(NSC[:, 1, :], -0.5))
            V.tensor_scalar(GMS[:, 3, :], PB[1][:, 0:B], LN_EPS, None, ALU.add).then_inc(sig["g_ve"], 1)
            dve.wait_ge(sig["g_rstd"], 1)
            ch.then(V.tensor_scalar(NSC[:, 0, :], GMS[:, 4, :], vec(GAMMA), None, ALU.mult))
            ch.then(V.tensor_tensor(GMS[:, 5, :], GMS[:, 0, :], NSC[:, 0, :], ALU.mult))
            V.tensor_scalar(NSC[:, 1, :], GMS[:, 5, :], -1.0, vec(BETA), ALU.mult, ALU.add).then_inc(sig["weights_used"], 1)
            dve.wait_ge(sig["weights_used"], 1)
            start += ch.n
            def expert_unit(ch, u, done):
                dve.wait_ge(sig["b_at"], 1 + u)
                for b in range(UB):
                    row = RW[:, bass.ds(u * UB + b, 1), :].rearrange("p b t -> p (b t)")
                    last = V.tensor_scalar(RN[:, b * T:(b + 1) * T], row, NSC[:, 0, bass.ds(u * UB + b, 1)],
                                           NSC[:, 1, bass.ds(u * UB + b, 1)], ALU.mult, ALU.add)
                last.then_inc(sig["b_n"], 1)
                dve.wait_ge(sig["b_lg"], u + 1)
                gate_logits(dve, ch, sig["b_c"])
                gate_weights(dve, ch, sig["b_ex"], u + 1, sig["b_gate"])
                if done is not None:
                    norm_stats(dve, ch, lambda i: tilef(X, done, i), sig["c_var"])
                dve.wait_ge(sig["b_gate"], u + 1)
                for e in range(E):
                    if e == 1:
                        dve.wait_ge(sig["b_at"], 1 + u + 1)
                        dve.wait_ge(sig["b_acc"], 1 + u * E + 1)
                        xs = X[:, bass.ds(u * TILES, TILES), :]
                        V.tensor_tensor(xs, xs, PB[5][:, :].rearrange("p (n d) -> p n d", d=D), ALU.add).then_inc(sig["b_x"], 1)
                        dve.wait_ge(sig["b_x"], 1 + u + 1)
                        if done is not None:
                            second_norm(ch, done)
                    dve.wait_ge(sig["b_y"], 2 + u * E + e + 1)
                    if e >= 1:
                        dve.wait_ge(sig["b_acc"], 1 + u * E + e)
                    yb = PB[4 if e % 2 == 0 else 6]
                    for i in range(TILES):
                        x = tilef(X, u, i)
                        last = V.scalar_tensor_tensor(x, yb[:, i * P:(i + 1) * P], GATE[:, i, e:e + 1], x,
                                                      ALU.mult, ALU.add)
                    last.then_inc(sig["b_acc"], 1)

            def second_norm(ch, u):
                dve.wait_ge(sig["c_rstd"], u + 1)
                norm_apply(lambda i: XNT[:, i, :], lambda i: tilef(X, u, i), sig["c_xn"])
                dve.wait_ge(sig["c_xn"], u + 1)
                ch.done(V.tensor_copy(XN[:, bass.ds(u * TILES, TILES), :], XNT[:, :, :]))

            ch = Chain(dve, dve_chain, start)
            expert_unit(ch, 0, None)
            start += ch.n
            PER_B = 19
            with dve.Fori(0, UNITS - 1) as u:
                ch = Chain(dve, dve_chain, start + u * PER_B)
                expert_unit(ch, u + 1, u)
                assert ch.n == PER_B, ch.n
            start += (UNITS - 1) * PER_B
            ch = Chain(dve, dve_chain, start)
            dve.wait_ge(sig["b_acc"], 1 + UNITS * E)
            norm_stats(dve, ch, lambda i: tilef(X, UNITS - 1, i), sig["c_var"])
            second_norm(ch, UNITS - 1)
            start += ch.n
            cell_dve(dve, start)


def kernel(**inputs):
    import numpy as np
    import ml_dtypes
    import concourse.bacc as bacc
    from concourse.bass_utils import run_bass_kernel_spmd

    def arr(n):
        return np.asarray(inputs[n])

    q = np.arange(P)
    cst = np.zeros((P, C_END), np.float32)
    cst[:, C_ID:C_ID + P] = np.eye(P)
    cst[:, C_GROUP:C_GROUP + P] = (q[:, None] // HD == q[None, :] // HD) / HD
    cst[:, C_SEL:C_SEL + NS] = q[:, None] % B == np.arange(B)[None, :]
    cst[:, C_MASK:C_MASK + 4] = (q[:, None] % 32 // HD == np.arange(4)[None, :]) / np.sqrt(HD)
    cst[:, C_HOT:C_HOT + NB] = q[:, None] // B == np.arange(NB)[None, :]
    cst[:, C_LT8:C_LT8 + E * E] = (np.arange(E)[None, :] < np.arange(E)[:, None]).reshape(1, -1)
    cst[:, C_LT4:C_LT4 + NB * NB] = (np.arange(NB)[None, :] < np.arange(NB)[:, None]).reshape(1, -1)
    cst[:, C_BR:C_BR + E] = arr("L0_ffn_br")[None, :]
    cst[:, C_BB:C_BB + NS] = np.repeat(arr("L1_attn_b_beta"), B, axis=0)
    cst[:, C_B1:C_B1 + E * H0C] = arr("L0_ffn_b1").reshape(E * H0C, P).T
    cst[:, C_NHALF:C_NHALF + TILES] = -0.5
    cst[:, C_HALF:C_HALF + STEPS] = 0.5
    cst[:, C_EPS] = WKV_EPS
    neg = np.zeros((P, 3 * P), ml_dtypes.bfloat16)
    neg[:, 0:P] = np.eye(P)
    neg[:, 2 * P:3 * P] = np.where(q[None, :] > q[:, None], -1e30, 0.0)
    wkv = arr("L1_attn_W_kv").reshape(NB, 2, NS, D)
    wb = arr("L1_attn_W_beta").reshape(NB, NS, D)
    wq, wr = arr("L1_attn_W_q"), arr("L1_attn_W_router")
    wc = np.stack([np.concatenate([wkv[n, 0], wkv[n, 1], wb[n], wq, wr]) for n in range(NB)])
    data = {
        "x": arr("L0_attn_x").reshape(B * T, D),
        "WA": np.stack([arr("L0_attn_W_" + c).T for c in "rkvo"], axis=1),
        "VEC": np.stack([arr(n).reshape(D) for n in (
            "L0_attn_time_mix_r", "L0_attn_time_mix_k", "L0_attn_time_mix_v", "L0_attn_time_decay",
            "L0_attn_time_first", "L0_attn_ln_gamma", "L0_attn_ln_beta", "L1_ffn_ln1_w", "L1_ffn_ln2_w")], axis=1),
        "CST": cst, "NEG": neg,
        "WR0": arr("L0_ffn_Wr"),
        "W1": arr("L0_ffn_W1").transpose(1, 0, 2).reshape(D, E * H0C * P),
        "W2": arr("L0_ffn_W2").reshape(E * H0C, P, D).transpose(1, 0, 2),
        "B2": arr("L0_ffn_b2"),
        "WIN": arr("L1_attn_W_in").T,
        "WC": wc.transpose(2, 0, 1),
        "WOUT": arr("L1_attn_W_out").T,
        "WQKV": arr("L1_ffn_c_attn_w"),
        "WPR": arr("L1_ffn_c_proj_w"),
        "WR1": arr("L1_ffn_router_w"),
        "W1b": arr("L1_ffn_w1"),
        "W2b": arr("L1_ffn_w2").reshape(E * H1C, P, D).transpose(1, 0, 2),
    }
    nc = bacc.Bacc("TRN2", target_bir_lowering=False, num_devices=1)
    arrays, aps = {}, {}
    for name, a in data.items():
        a = np.ascontiguousarray(a)
        arrays["in_" + name] = a
        aps[name] = nc.dram_tensor("in_" + name, a.shape, mybir.dt.from_np(a.dtype), kind="ExternalInput").ap()
    out = nc.dram_tensor("out", (B * T, D), F32, kind="ExternalOutput").ap()
    build(nc, aps, out)
    r = run_bass_kernel_spmd(nc, [arrays], core_ids=[0])
    return r.results[0]["out"].reshape(B, T, D)
```
